# Optimizing a Trainium2 kernel written in Bass

```python
import numpy as np
import jax
import jax.numpy as jnp

def _softmax(x, axis=-1):
    return jax.nn.softmax(x, axis=axis)

def _gelu(x):
    return jax.nn.gelu(x, approximate=True)

def _silu(x):
    return jax.nn.silu(x)

def _sigmoid(x):
    return jax.nn.sigmoid(x)

def _layernorm(x, axis=-1, eps=1e-05):
    m = jnp.mean(x, axis=axis, keepdims=True)
    v = jnp.var(x, axis=axis, keepdims=True)
    return (x - m) / jnp.sqrt(v + eps)

def _scatter_add(tgt, idx, src, axis=0):
    return tgt.at[idx].add(src)

def _segment_sum(src, seg, n):
    return jax.ops.segment_sum(src, seg, n)
kernel_name = 'mk_flamingo_gated_d2_seqx_r4_b3b821'

def setup_inputs(seed: int=0):
    np.random.seed(seed)
    _w = jnp.asarray

    def _rec_inputs():
        import jax
        import jax.numpy as jnp
        _rk = jax.random.key(seed)
        x = 0.002226 + 0.9996 * jax.random.normal(jax.random.fold_in(_rk, 1), (32, 112, 256), jnp.float32)
        _lenS = 112 - jax.random.randint(jax.random.fold_in(_rk, 7), (32,), 0, max(1, 112 // 4) + 1, jnp.int32)
        _lenS2 = 375 - jax.random.randint(jax.random.fold_in(_rk, 8), (32,), 0, max(1, 375 // 4) + 1, jnp.int32)
        _ctx_1024P = jax.random.normal(jax.random.fold_in(_rk, 11), (32, 16, 256), jnp.float32)
        _ctx_1024c = jax.random.dirichlet(jax.random.fold_in(_rk, 511), 0.3 * jnp.ones((16,), jnp.float32), (32, 375))
        _ctx_1024t = jnp.einsum('bsk,bkd->bsd', _ctx_1024c, _ctx_1024P)
        _ctx_1024t = _ctx_1024t * jax.lax.rsqrt(jnp.mean(jnp.square(_ctx_1024t)) + 1e-12) * 0.953939
        ctx_1024 = -0.000125008 + 0.999885 * (_ctx_1024t + 0.3 * jax.random.normal(jax.random.fold_in(_rk, 611), (32, 375, 256), jnp.float32))
        _g = jax.random.normal(jax.random.fold_in(_rk, 9001), (2, 2), jnp.float32)
        _g = jnp.sign(_g) * jnp.maximum(jnp.abs(_g), 1.0) + (_g == 0) * 1.0
        g_xattn = _g[0]
        g_ffn = _g[1]
        return (x, ctx_1024, g_xattn, g_ffn)
    x, ctx_1024, g_xattn, g_ffn = _rec_inputs()

    def _L0_xattn_setup():
        import jax, jax.numpy as jnp
        import numpy as np
        B, M, N, DIM, DH, H = (8, 1024, 64, 256, 128, 8)
        INNER = DH * H
        EPS = 1e-05

        def _layernorm(x, g, b):
            mu = jnp.mean(x, axis=-1, keepdims=True)
            var = jnp.var(x, axis=-1, keepdims=True)
            return (x - mu) * jax.lax.rsqrt(var + EPS) * g + b
        key = jax.random.key(seed)
        ks = jax.random.split(key, 8)
        sd = 0.02
        return {'x': jax.random.normal(ks[0], (B, M, DIM), jnp.float32), 'latents': jax.random.normal(ks[1], (B, N, DIM), jnp.float32), 'gamma_media': jnp.ones((DIM,), jnp.float32), 'beta_media': jnp.zeros((DIM,), jnp.float32), 'gamma_lat': jnp.ones((DIM,), jnp.float32), 'beta_lat': jnp.zeros((DIM,), jnp.float32), 'Wq': jax.random.normal(ks[2], (DIM, INNER), jnp.float32) * sd, 'bq': jnp.zeros((INNER,), jnp.float32), 'Wkv': jax.random.normal(ks[3], (DIM, 2 * INNER), jnp.float32) * sd, 'bkv': jnp.zeros((2 * INNER,), jnp.float32), 'Wo': jax.random.normal(ks[4], (INNER, DIM), jnp.float32) * sd, 'bo': jnp.zeros((DIM,), jnp.float32)}
    _L0_xattn_all = _L0_xattn_setup()
    _L0_xattn_in = {k: v for k, v in _L0_xattn_all.items() if k in ('gamma_media', 'beta_media', 'gamma_lat', 'beta_lat', 'Wq', 'bq', 'Wkv', 'bkv', 'Wo', 'bo')}
    del _L0_xattn_all

    def _L0_ffn_setup():
        import jax, jax.numpy as jnp
        import numpy as np
        B, T, C = (1, 1024, 256)
        E, K = (64, 8)
        G, TG = (8, 4)
        H, HS = (128, 512)
        STD = 0.02

        def _route(xf, router_w, e_bias):
            S = xf.shape[0]
            scores = jax.nn.sigmoid(xf @ router_w.T)
            sb = scores + e_bias
            epg = E // G
            grp = jax.lax.top_k(sb.reshape(S, G, epg), K // TG)[0].sum(-1)
            gidx = jax.lax.top_k(grp, TG)[1]
            gmask = jnp.zeros((S, G), bool).at[jnp.arange(S)[:, None], gidx].set(True)
            emask = jnp.repeat(gmask, epg, axis=1)
            masked = jnp.where(emask, sb, -jnp.inf)
            topk_idx = jax.lax.top_k(masked, K)[1]
            w = jnp.take_along_axis(scores, topk_idx, axis=1)
            w = w / (w.sum(-1, keepdims=True) + 1e-20)
            return (topk_idx, w)
        key = jax.random.key(seed)
        ks = jax.random.split(key, 9)
        return {'x': jax.random.normal(ks[0], (B, T, C), jnp.float32), 'router_w': jax.random.normal(ks[1], (E, C), jnp.float32) * C ** (-0.5), 'e_bias': jnp.zeros((E,), jnp.float32), 'gate_w': jax.random.normal(ks[2], (E, C, H), jnp.float32) * STD, 'up_w': jax.random.normal(ks[3], (E, C, H), jnp.float32) * STD, 'down_w': jax.random.normal(ks[4], (E, H, C), jnp.float32) * STD, 'sh_gate_w': jax.random.normal(ks[5], (C, HS), jnp.float32) * STD, 'sh_up_w': jax.random.normal(ks[6], (C, HS), jnp.float32) * STD, 'sh_down_w': jax.random.normal(ks[7], (HS, C), jnp.float32) * STD}
    _L0_ffn_all = _L0_ffn_setup()
    _L0_ffn_in = {k: v for k, v in _L0_ffn_all.items() if k in ('router_w', 'e_bias', 'gate_w', 'up_w', 'down_w', 'sh_gate_w', 'sh_up_w', 'sh_down_w')}
    del _L0_ffn_all

    def _L1_xattn_setup():
        import jax, jax.numpy as jnp
        import numpy as np
        E = 256
        H = 16
        D = E // H
        key = jax.random.key(seed)
        ks = jax.random.split(key, 12)
        B, Tq, Tk = (2, 256, 2048)
        s = 0.02
        return {'hidden_states': jax.random.normal(ks[0], (B, Tq, E), jnp.float32), 'key_value_states': jax.random.normal(ks[1], (B, Tk, E), jnp.float32), 'Wq': jax.random.normal(ks[2], (E, E), jnp.float32) * s, 'bq': jnp.zeros((E,), jnp.float32), 'Wk': jax.random.normal(ks[3], (E, E), jnp.float32) * s, 'bk': jnp.zeros((E,), jnp.float32), 'Wv': jax.random.normal(ks[4], (E, E), jnp.float32) * s, 'bv': jnp.zeros((E,), jnp.float32), 'Wo': jax.random.normal(ks[5], (E, E), jnp.float32) * s, 'bo': jnp.zeros((E,), jnp.float32), 'stride': 16}
    _L1_xattn_all = _L1_xattn_setup()
    _L1_xattn_in = {k: v for k, v in _L1_xattn_all.items() if k in ('Wq', 'bq', 'Wk', 'bk', 'Wv', 'bv', 'Wo', 'bo')}
    del _L1_xattn_all

    def _L1_ffn_setup():
        import jax, jax.numpy as jnp
        import numpy as np
        TOP_K = 2
        NUM_EXPERTS = 8
        key = jax.random.key(seed)
        ks = jax.random.split(key, 8)
        h, d, ds, E = (256, 128, 256, NUM_EXPERTS)
        s = 1.0 / np.sqrt(h)
        return {'x': jax.random.normal(ks[0], (2, 512, h), jnp.float32), 'router': jax.random.normal(ks[1], (h, E), jnp.float32) * s, 'experts_gate': jax.random.normal(ks[2], (E, h, d), jnp.float32) * s, 'experts_up': jax.random.normal(ks[3], (E, h, d), jnp.float32) * s, 'experts_down': jax.random.normal(ks[4], (E, d, h), jnp.float32) * (1.0 / np.sqrt(d)), 'shared_gate': jax.random.normal(ks[5], (h, ds), jnp.float32) * s, 'shared_up': jax.random.normal(ks[6], (h, ds), jnp.float32) * s, 'shared_down': jax.random.normal(ks[7], (ds, h), jnp.float32) * (1.0 / np.sqrt(ds))}
    _L1_ffn_all = _L1_ffn_setup()
    _L1_ffn_in = {k: v for k, v in _L1_ffn_all.items() if k in ('router', 'experts_gate', 'experts_up', 'experts_down', 'shared_gate', 'shared_up', 'shared_down')}
    del _L1_ffn_all
    return {'x': x, 'ctx_1024': ctx_1024, 'g_xattn': g_xattn, 'g_ffn': g_ffn, 'L0_xattn_gamma_media': _L0_xattn_in['gamma_media'], 'L0_xattn_beta_media': _L0_xattn_in['beta_media'], 'L0_xattn_gamma_lat': _L0_xattn_in['gamma_lat'], 'L0_xattn_beta_lat': _L0_xattn_in['beta_lat'], 'L0_xattn_Wq': _L0_xattn_in['Wq'], 'L0_xattn_bq': _L0_xattn_in['bq'], 'L0_xattn_Wkv': _L0_xattn_in['Wkv'], 'L0_xattn_bkv': _L0_xattn_in['bkv'], 'L0_xattn_Wo': _L0_xattn_in['Wo'], 'L0_xattn_bo': _L0_xattn_in['bo'], 'L0_ffn_router_w': _L0_ffn_in['router_w'], 'L0_ffn_e_bias': _L0_ffn_in['e_bias'], 'L0_ffn_gate_w': _L0_ffn_in['gate_w'], 'L0_ffn_up_w': _L0_ffn_in['up_w'], 'L0_ffn_down_w': _L0_ffn_in['down_w'], 'L0_ffn_sh_gate_w': _L0_ffn_in['sh_gate_w'], 'L0_ffn_sh_up_w': _L0_ffn_in['sh_up_w'], 'L0_ffn_sh_down_w': _L0_ffn_in['sh_down_w'], 'L1_xattn_Wq': _L1_xattn_in['Wq'], 'L1_xattn_bq': _L1_xattn_in['bq'], 'L1_xattn_Wk': _L1_xattn_in['Wk'], 'L1_xattn_bk': _L1_xattn_in['bk'], 'L1_xattn_Wv': _L1_xattn_in['Wv'], 'L1_xattn_bv': _L1_xattn_in['bv'], 'L1_xattn_Wo': _L1_xattn_in['Wo'], 'L1_xattn_bo': _L1_xattn_in['bo'], 'L1_ffn_router': _L1_ffn_in['router'], 'L1_ffn_experts_gate': _L1_ffn_in['experts_gate'], 'L1_ffn_experts_up': _L1_ffn_in['experts_up'], 'L1_ffn_experts_down': _L1_ffn_in['experts_down'], 'L1_ffn_shared_gate': _L1_ffn_in['shared_gate'], 'L1_ffn_shared_up': _L1_ffn_in['shared_up'], 'L1_ffn_shared_down': _L1_ffn_in['shared_down']}

def reference(x, ctx_1024, g_xattn, g_ffn, L0_xattn_gamma_media, L0_xattn_beta_media, L0_xattn_gamma_lat, L0_xattn_beta_lat, L0_xattn_Wq, L0_xattn_bq, L0_xattn_Wkv, L0_xattn_bkv, L0_xattn_Wo, L0_xattn_bo, L0_ffn_router_w, L0_ffn_e_bias, L0_ffn_gate_w, L0_ffn_up_w, L0_ffn_down_w, L0_ffn_sh_gate_w, L0_ffn_sh_up_w, L0_ffn_sh_down_w, L1_xattn_Wq, L1_xattn_bq, L1_xattn_Wk, L1_xattn_bk, L1_xattn_Wv, L1_xattn_bv, L1_xattn_Wo, L1_xattn_bo, L1_ffn_router, L1_ffn_experts_gate, L1_ffn_experts_up, L1_ffn_experts_down, L1_ffn_shared_gate, L1_ffn_shared_up, L1_ffn_shared_down):
    import jax
    import jax.numpy as jnp

    def _L0_xattn_ref(x, latents, gamma_media, beta_media, gamma_lat, beta_lat, Wq, bq, Wkv, bkv, Wo, bo):
        import jax, jax.numpy as jnp
        import numpy as np
        B, M, N, DIM, DH, H = (8, 1024, 64, 256, 128, 8)
        INNER = DH * H
        EPS = 1e-05

        def _layernorm(x, g, b):
            mu = jnp.mean(x, axis=-1, keepdims=True)
            var = jnp.var(x, axis=-1, keepdims=True)
            return (x - mu) * jax.lax.rsqrt(var + EPS) * g + b
        b = x.shape[0]
        xn = _layernorm(x, gamma_media, beta_media)
        ln = _layernorm(latents, gamma_lat, beta_lat)
        q = ln @ Wq + bq
        kv_input = jnp.concatenate([xn, ln], axis=1)
        kv = kv_input @ Wkv + bkv
        k, v = jnp.split(kv, 2, axis=-1)

        def to_heads(t):
            return t.reshape(b, t.shape[1], H, DH).transpose(0, 2, 1, 3)
        q, k, v = (to_heads(q), to_heads(k), to_heads(v))
        q = q * DH ** (-0.5)
        sim = jnp.einsum('bhid,bhjd->bhij', q, k)
        attn = jax.nn.softmax(sim, axis=-1)
        out = jnp.einsum('bhij,bhjd->bhid', attn, v)
        out = out.transpose(0, 2, 1, 3).reshape(b, -1, INNER)
        return out @ Wo + bo

    def _L0_ffn_ref(x, router_w, e_bias, gate_w, up_w, down_w, sh_gate_w, sh_up_w, sh_down_w):
        import jax, jax.numpy as jnp
        import numpy as np
        B, T, C = (1, 1024, 256)
        E, K = (64, 8)
        G, TG = (8, 4)
        H, HS = (128, 512)
        STD = 0.02

        def _route(xf, router_w, e_bias):
            S = xf.shape[0]
            scores = jax.nn.sigmoid(xf @ router_w.T)
            sb = scores + e_bias
            epg = E // G
            grp = jax.lax.top_k(sb.reshape(S, G, epg), K // TG)[0].sum(-1)
            gidx = jax.lax.top_k(grp, TG)[1]
            gmask = jnp.zeros((S, G), bool).at[jnp.arange(S)[:, None], gidx].set(True)
            emask = jnp.repeat(gmask, epg, axis=1)
            masked = jnp.where(emask, sb, -jnp.inf)
            topk_idx = jax.lax.top_k(masked, K)[1]
            w = jnp.take_along_axis(scores, topk_idx, axis=1)
            w = w / (w.sum(-1, keepdims=True) + 1e-20)
            return (topk_idx, w)
        Bq, Tq, Cq = x.shape
        xf = x.reshape(Bq * Tq, Cq)
        shared = jax.nn.silu(xf @ sh_gate_w) * (xf @ sh_up_w) @ sh_down_w
        topk_idx, w = _route(xf, router_w, e_bias)
        fe = topk_idx.reshape(-1)
        order = jnp.argsort(fe, stable=True)
        tok = order // K
        sorted_x = xf[tok]
        group_sizes = jnp.bincount(fe, length=E).astype(jnp.int32)
        g = jax.lax.ragged_dot(sorted_x, gate_w, group_sizes)
        u = jax.lax.ragged_dot(sorted_x, up_w, group_sizes)
        h = jax.nn.silu(g) * u
        o = jax.lax.ragged_dot(h, down_w, group_sizes)
        o = o * w.reshape(-1)[order][:, None]
        routed = jnp.zeros_like(xf).at[tok].add(o)
        return (shared + routed).reshape(Bq, Tq, Cq)

    def _L1_xattn_ref(hidden_states, key_value_states, Wq, bq, Wk, bk, Wv, bv, Wo, bo, stride):
        import jax, jax.numpy as jnp
        import numpy as np
        E = 256
        H = 16
        D = E // H
        B, Tq, _ = hidden_states.shape
        Tk = key_value_states.shape[1]
        scaling = D ** (-0.5)
        Q = (hidden_states @ Wq.T + bq).reshape(B, Tq, H, D).transpose(0, 2, 1, 3)
        K = (key_value_states @ Wk.T + bk).reshape(B, Tk, H, D).transpose(0, 2, 1, 3)
        V = (key_value_states @ Wv.T + bv).reshape(B, Tk, H, D).transpose(0, 2, 1, 3)
        m = Tk // stride
        idx = jnp.arange(H)[:, None] + stride * jnp.arange(m)[None, :]
        gather = idx[None, :, :, None]
        Kg = jnp.take_along_axis(K, gather, axis=2)
        Vg = jnp.take_along_axis(V, gather, axis=2)
        scores = jnp.einsum('bhqd,bhkd->bhqk', Q, Kg) * scaling
        attn = jax.nn.softmax(scores, axis=-1)
        out = jnp.einsum('bhqk,bhkd->bhqd', attn, Vg)
        out = out.transpose(0, 2, 1, 3).reshape(B, Tq, E)
        return out @ Wo.T + bo

    def _L1_ffn_ref(x, router, experts_gate, experts_up, experts_down, shared_gate, shared_up, shared_down):
        import jax, jax.numpy as jnp
        import numpy as np
        TOP_K = 2
        NUM_EXPERTS = 8
        b, s, h = x.shape
        E = router.shape[1]
        shared_act = jax.nn.silu(jnp.einsum('bsh,hd->bsd', x, shared_gate))
        shared_up_out = jnp.einsum('bsh,hd->bsd', x, shared_up)
        shared_out = jnp.einsum('bsd,dh->bsh', shared_act * shared_up_out, shared_down)
        router_probs = jax.nn.softmax(jnp.einsum('bsh,he->bse', x, router), axis=-1)
        topk_probs, topk_idx = jax.lax.top_k(router_probs, TOP_K)
        coef = jnp.sum(jax.nn.one_hot(topk_idx, E, dtype=x.dtype) * topk_probs[..., None], axis=2)
        coef = coef.reshape(b * s, E)
        x_flat = x.reshape(b * s, h)
        gate = jnp.einsum('th,ehd->etd', x_flat, experts_gate)
        up = jnp.einsum('th,ehd->etd', x_flat, experts_up)
        expert_out = jnp.einsum('etd,edh->eth', jax.nn.silu(gate) * up, experts_down)
        routed = jnp.einsum('eth,te->th', expert_out, coef)
        return routed.reshape(b, s, h) + shared_out
    x = x + jnp.tanh(g_xattn[0]) * _L0_xattn_ref(ctx_1024, _layernorm(x, axis=-1), L0_xattn_gamma_media, L0_xattn_beta_media, L0_xattn_gamma_lat, L0_xattn_beta_lat, L0_xattn_Wq, L0_xattn_bq, L0_xattn_Wkv, L0_xattn_bkv, L0_xattn_Wo, L0_xattn_bo)
    x = x + jnp.tanh(g_ffn[0]) * _L0_ffn_ref(_layernorm(x, axis=-1), L0_ffn_router_w, L0_ffn_e_bias, L0_ffn_gate_w, L0_ffn_up_w, L0_ffn_down_w, L0_ffn_sh_gate_w, L0_ffn_sh_up_w, L0_ffn_sh_down_w)
    x = x + jnp.tanh(g_xattn[1]) * _L1_xattn_ref(_layernorm(x, axis=-1), ctx_1024, L1_xattn_Wq, L1_xattn_bq, L1_xattn_Wk, L1_xattn_bk, L1_xattn_Wv, L1_xattn_bv, L1_xattn_Wo, L1_xattn_bo, 16)
    x = x + jnp.tanh(g_ffn[1]) * _L1_ffn_ref(_layernorm(x, axis=-1), L1_ffn_router, L1_ffn_experts_gate, L1_ffn_experts_up, L1_ffn_experts_down, L1_ffn_shared_gate, L1_ffn_shared_up, L1_ffn_shared_down)
    return x

_drawn_inputs = setup_inputs


def setup_inputs(seed=0):
    import zlib

    import numpy as np

    out = dict(_drawn_inputs(seed))
    spreads = {'g_ffn': (-1.0, 0.6),
     'L0_xattn_gamma_media': (1.0, 0.6),
     'L0_xattn_beta_media': (0.0, 0.505),
     'L0_xattn_gamma_lat': (1.0, 0.6),
     'L0_xattn_beta_lat': (0.0, 0.8),
     'L0_xattn_bq': (0.0, 0.8),
     'L0_xattn_bkv': (0.0, 0.1),
     'L0_xattn_bo': (0.0, 0.1),
     'L0_ffn_e_bias': (0.0, 0.8),
     'L1_xattn_bq': (0.0, 2.0),
     'L1_xattn_bk': (0.0, 2.0),
     'L1_xattn_bv': (0.0, 2.0),
     'L1_xattn_bo': (0.0, 0.692)}
    factors = {'L0_xattn_Wq': 8.0,
     'L0_ffn_router_w': 8.0,
     'L0_ffn_gate_w': 8.0,
     'L0_ffn_up_w': 8.0,
     'L0_ffn_down_w': 8.0,
     'L1_xattn_Wq': 51.07,
     'L1_xattn_Wk': 45.746,
     'L0_ffn_sh_gate_w': 7.128,
     'L0_ffn_sh_up_w': 6.74,
     'L0_ffn_sh_down_w': 7.035,
     'L1_xattn_Wv': 4.758}
    for name, (base, spread) in spreads.items():
        noise = np.random.default_rng([zlib.crc32(name.encode()), seed]).standard_normal(out[name].shape)
        drawn = base * np.exp(spread * noise) if base else spread * noise
        out[name] = jnp.asarray(drawn.astype(out[name].dtype))
    for name, factor in factors.items():
        out[name] = (out[name] * factor).astype(out[name].dtype)
    return out
```

```python
import concourse.bass as bass
from concourse import mybir
from contextlib import ExitStack

F32 = mybir.dt.float32
F32R = mybir.dt.float32r
I32 = mybir.dt.int32
U32 = mybir.dt.uint32
ALU = mybir.AluOpType
ACT = mybir.ActivationFunctionType
AX = mybir.AxisListType
LN_EPS = 1e-5
SUB, MUL, ADD = ALU.subtract, ALU.mult, ALU.add


class Batch:

    def __init__(self, i, off):
        self.i, self.off = i, off

    def count(self, per, k=0):
        return self.i * (2 * per) + (self.off * per + k)

    @property
    def parity(self):
        return self.off % 2

    def uses(self, k=0):
        return self.i * 16 + (16 * (self.off // 2 + k))

    def __add__(self, d):
        return Batch(self.i, self.off + d)

    def first(self, n):
        return isinstance(self.i, int) and self.off < n

    def last(self, nb):
        return isinstance(self.i, int) and self.off >= nb


def pipeline(eng, nb, step):
    step(None, None, Batch(0, 0))
    step(Batch(0, 0), None, Batch(0, 1))
    with eng.Fori(0, (nb - 2) // 2) as i:
        for off in (1, 2):
            step(Batch(i, off), Batch(i, off - 1), Batch(i, off + 1))
    step(Batch(0, nb - 1), Batch(0, nb - 2), None)
    step(None, Batch(0, nb - 1), None)


def wait_apart(eng, sem, value, passed):
    eng.wait_ge(sem, value)
    eng.sem_inc(passed, 1)


def mm3(nc, out, left, right, start, stop):
    (lh, ll), (rh, rl) = left, right
    nc.tensor.matmul(out, lh, rh, start=start, stop=False)
    nc.tensor.matmul(out, lh, rl, start=False, stop=False)
    return nc.tensor.matmul(out, ll, rh, start=False, stop=stop)


def make_identity(nc, pool, ident, sem):
    nc.gpsimd.memset(ident[:, :], 0.0).then_inc(sem, 1)
    pool.wait_ge(sem, 1)
    nc.gpsimd.affine_select(out=ident[:, :], in_=ident[:, :], compare_op=ALU.not_equal, fill=1.0,
                            base=0, pattern=[[-1, 128]], channel_multiplier=1).then_inc(sem, 1)


def row(ap, parts):
    return ap.partition_broadcast(parts)


def perceiver_attention(nc, x, ctx, g_xattn, gamma_media, beta_media, gamma_lat, beta_lat,
                        Wq, bq, Wkv, bkv, Wo, bo, x1):
    NB, Q, D = x.shape
    M = ctx.shape[1]
    DH = 128
    H = Wq.shape[1] // DH
    CC = D // 128
    MC = 3
    MP = M // MC
    KC = MC + 1
    KEYS = Q + M
    KPAD = KEYS + KEYS % 2
    ROWS = H * Q
    R = ROWS // 128
    HG = 2
    GH = H // HG
    GC = GH * Q
    SCALE = float(DH) ** -0.5
    kc_rows = [Q] + [MP] * MC
    kc_col = [0] + [Q + MP * c for c in range(MC)]

    with ExitStack() as outer:
        def sb(name, shape, dt=F32, stack=outer):
            return stack.enter_context(nc.sbuf_tensor(name, shape, dt))

        def split_sb(name, shape, stack=outer):
            return (sb(name + "_hi", shape, F32R, stack), sb(name + "_lo", shape, F32R, stack))

        wq = split_sb("wq", [128, CC, H * DH])
        wkT = split_sb("wkT", [DH, H, D])
        wv = split_sb("wv", [128, CC, H * DH])
        wo = split_sb("wo", [DH, H, D])
        ident = sb("ident_a", [128, 128])
        gm = sb("gm", [MP, D])
        bm = sb("bm", [MP, D])
        gl = sb("gl", [Q, D])
        bl = sb("bl", [Q, D])
        biasT = sb("biasT", [DH, 2 * H])
        bqT, bvT = biasT[:, 0:H], biasT[:, H:2 * H]
        gate = sb("gate_a", [Q, 1])
        gbo = sb("gbo", [Q, D])
        half = sb("half_a", [128, 4])
        xT = [split_sb(f"xT{p}", [128, CC, KPAD]) for p in range(2)]

        with ExitStack() as st:
            def sem(name):
                return nc.alloc_semaphore(name)
            wq_raw = sb("wq_raw", [128, CC, H * DH], stack=st)
            wkv_raw = sb("wkv_raw", [128, CC, 2 * H * DH], stack=st)
            wo_raw = sb("wo_raw", [DH, H, D], stack=st)
            wkT_ps = st.enter_context(nc.psum_tensor("wkT_ps", [128, H // 2, 2 * D], F32))
            bias_rows = sb("bias_rows", [2 * H, DH], stack=st)
            biasT_ps = st.enter_context(nc.psum_tensor("biasT_ps", [128, 512], F32))
            wq_in, wkv_in, wo_in, small_in = sem("wq_in"), sem("wkv_in"), sem("wo_in"), sem("small_in")
            ident_ok, turned, hi_ok, lo_ok = sem("ident_ok"), sem("turned"), sem("hi_ok"), sem("lo_ok")
            gate_ok, consts_ok = sem("gate_ok"), sem("consts_ok")
            block = st.enter_context(nc.Block())

            @block.sync
            def _(sp):
                sp.dma_start(wkv_raw[:, :, :], Wkv.rearrange("(c p) n -> p c n", p=128)).then_inc(wkv_in, 16)
                sp.dma_start(wq_raw[:, :, :], Wq.rearrange("(c p) n -> p c n", p=128)).then_inc(wq_in, 16)
                sp.dma_start(wo_raw[:, :, :], Wo.rearrange("(h p) n -> p h n", p=128)).then_inc(wo_in, 16)

            @block.gpsimd
            def _(pool):
                make_identity(nc, pool, ident, ident_ok)
                nc.gpsimd.memset(half[:, :], -0.5)
                for pair in xT:
                    for part in pair:
                        nc.gpsimd.memset(part[:, :, KEYS:KPAD].bitcast(F32), 0.0).then_inc(consts_ok, 1)
                pool.wait_ge(gate_ok, 1)
                nc.gpsimd.tensor_scalar(gbo[:, :], gbo[:, :], gate[:, 0:1], None, MUL).then_inc(consts_ok, 1)

            @block.scalar
            def _(act):
                small = [(gbo, row(bo, Q)), (gate, row(g_xattn[0:1], Q)), (gm, row(gamma_media, MP)),
                         (bm, row(beta_media, MP)), (gl, row(gamma_lat, Q)), (bl, row(beta_lat, Q)),
                         (bias_rows[0:H, :], bq.rearrange("(h p) -> h p", p=DH)),
                         (bias_rows[H:2 * H, :], bkv[H * DH:].rearrange("(h p) -> h p", p=DH))]
                for dst, src in small:
                    act.dma_start(dst[:, :], src).then_inc(small_in, 16)
                act.wait_ge(small_in, 16 * len(small))
                nc.scalar.activation(gate[:, :], gate[:, :], ACT.Tanh).then_inc(gate_ok, 1)
                for g in range(H // 2):
                    act.wait_ge(turned, g + 1)
                    nc.scalar.activation(wkT[0][:, 2 * g:2 * g + 2, :].rearrange("p h c -> p (h c)"),
                                         wkT_ps[:, g, :], ACT.Copy, scale=SCALE).then_inc(hi_ok, 1)
                for ready, dst, src in ((wkv_in, wv, wkv_raw[:, :, H * DH:]), (wq_in, wq, wq_raw), (wo_in, wo, wo_raw)):
                    act.wait_ge(ready, 16)
                    nc.scalar.activation(dst[0][:, :, :], src[:, :, :], ACT.Copy).then_inc(hi_ok, 1)

            @block.vector
            def _(dve):
                dve.wait_ge(turned, 1)
                nc.vector.tensor_copy(biasT[:, :], biasT_ps[:, 0:2 * H])
                for g in range(H // 2):
                    dve.wait_ge(hi_ok, g + 1)
                    hi, lo = (w[:, 2 * g:2 * g + 2, :].rearrange("p h c -> p (h c)") for w in wkT)
                    nc.vector.scalar_tensor_tensor(out=lo, in0=wkT_ps[:, g, :], scalar=SCALE, in1=hi.bitcast(F32),
                                                   op0=MUL, op1=SUB).then_inc(lo_ok, 1)
                for n, (dst, src) in enumerate(((wv, wkv_raw[:, :, H * DH:]), (wq, wq_raw), (wo, wo_raw))):
                    dve.wait_ge(hi_ok, H // 2 + n + 1)
                    nc.vector.tensor_tensor(dst[1][:, :, :], src[:, :, :], dst[0][:, :, :].bitcast(F32), SUB).then_inc(lo_ok, 1)

            @block.tensor
            def _(pe):
                pe.wait_ge(ident_ok, 2)
                pe.wait_ge(small_in, 16 * 8)
                nc.tensor.transpose(biasT_ps[:, 0:2 * H], bias_rows[:, :], ident[0:2 * H, 0:2 * H])
                pe.wait_ge(wkv_in, 16)
                for g in range(H // 2):
                    for k in range(2 * CC):
                        h, c = 2 * g + k // CC, k % CC
                        last = nc.tensor.transpose(wkT_ps[:, g, k * 128:(k + 1) * 128],
                                                   wkv_raw[:, c, h * DH:(h + 1) * DH], ident[:, :])
                    last.then_inc(turned, 1)

        with ExitStack() as st:
            def sem(name):
                return nc.alloc_semaphore(name)
            ctx_raw = [sb(f"ctx_raw{p}", [MP, MC, D], stack=st) for p in range(2)]
            x_lat = [sb(f"x_lat{p}", [Q, D], stack=st) for p in range(2)]
            x_res = [sb(f"x_res{p}", [Q, D], stack=st) for p in range(2)]
            raw_stats = sb("raw_stats", [128, KC + 1, 6], stack=st)
            mean_var = sb("mean_var", [128, KC + 1, 2], stack=st)
            var_eps = sb("var_eps", [128, KC + 1], stack=st)
            rstd = sb("rstd", [128, KC + 1], stack=st)
            xn32 = sb("xn32", [128, KC, D], stack=st)
            xn = [split_sb(f"xn{p}", [128, KC, D], st) for p in range(2)]
            head32 = sb("head32", [DH, ROWS], stack=st)
            q = split_sb("q", [DH, ROWS], st)
            qk = [split_sb(f"qk{p}", [128, CC, ROWS], st) for p in range(2)]
            probs = [sb(f"probs{n}", [128, KEYS], stack=st) for n in range(2)]
            nmax = sb("nmax", [128, 2], stack=st)
            rowsum = sb("rowsum", [128, 2], stack=st)
            rinv = sb("rinv", [128, 2], stack=st)
            pT = split_sb("pT", [MP, KC, ROWS], st)
            px = split_sb("px", [128, CC, ROWS], st)
            oT = split_sb("oT", [DH, ROWS], st)
            score_ps = st.enter_context(nc.psum_tensor("score_ps", [128, 2, 512], F32))
            turn_ps = st.enter_context(nc.psum_tensor("turn_ps", [128, 2, 512], F32))
            fill_ps = st.enter_context(nc.psum_tensor("fill_ps", [128, 4, 512], F32))

            ctx_in = [sem(f"ctx_in{p}") for p in range(2)]
            lat_in = [sem(f"lat_in{p}") for p in range(2)]
            res_in = [sem(f"res_in{p}") for p in range(2)]
            stored = [sem(f"stored{p}") for p in range(2)]
            bn_raw = sem("bn_raw")
            bn_done = sem("bn_done")
            ln_self = sem("ln_self")
            lat_z = sem("lat_z")
            xn_ready = sem("xn_ready")
            xn_hi_done = sem("xn_hi_done")
            xn_lo_done = sem("xn_lo_done")
            xT_mm, xT_hi_done, xT_done = sem("xT_mm"), sem("xT_hi_done"), sem("xT_done")
            q_mm, q32_done, q_hi_done, q_done = (sem(n) for n in ("q_mm", "q32_done", "q_hi_done", "q_done"))
            qk_mm, qk_hi_done, qk_done = sem("qk_mm"), sem("qk_hi_done"), sem("qk_done")
            score_mm, nmax_done, exp_done, rinv_done, probs_done = (
                sem(n) for n in ("score_mm", "nmax_done", "exp_done", "rinv_done", "probs_done"))
            turn_mm, pT_hi_done, pT_done = sem("turn_mm"), sem("pT_hi_done"), sem("pT_done")
            px_mm, px_hi_done, px_done = sem("px_mm"), sem("px_hi_done"), sem("px_done")
            oT_mm, o32_done, oT_hi_done, oT_done = (sem(n) for n in ("oT_mm", "o32_done", "oT_hi_done", "oT_done"))
            out_mm, xb_done, out_done = sem("out_mm"), sem("xb_done"), sem("out_done")
            pool_passed, dve_passed = sem("pool_passed"), sem("dve_passed")
            block = st.enter_context(nc.Block())

            G4 = HG * CC

            def tile_no(b, r):
                return (b.off * R + r) % 2

            @block.sync
            def _(sp):
                def load_rows(f):
                    p = f.parity
                    if not f.first(2):
                        sp.wait_ge(xn_ready, f.count(1, -1))
                    sp.dma_start(ctx_raw[p][:, :, :], ctx[f_index(f), :, :].rearrange("a (p c) d -> p (a c) d", c=MC)
                                 ).then_inc(ctx_in[p], 16)
                    sp.dma_start(x_lat[p][:, :], x[f_index(f), :, :].rearrange("a q d -> q (a d)")).then_inc(lat_in[p], 16)

                def f_index(b):
                    return bass.ds(b.count(1), 1)

                def step(s, t, f):
                    if f is not None:
                        load_rows(f)
                    if s is not None:
                        if not s.first(2):
                            sp.wait_ge(stored[s.parity], s.uses())
                        sp.dma_start(x_res[s.parity][:, :], x[f_index(s), :, :].rearrange("a q d -> q (a d)")
                                     ).then_inc(res_in[s.parity], 16)
                    if t is not None:
                        sp.wait_ge(out_done, t.count(1, 1))
                        sp.dma_start(x1[f_index(t), :, :].rearrange("a q d -> q (a d)"), x_res[t.parity][:, :]
                                     ).then_inc(stored[t.parity], 16)

                pipeline(sp, NB, step)
                for p in range(2):
                    sp.wait_ge(stored[p], 16 * (NB // 2))

            @block.gpsimd
            def _(pool):
                def norm(f):
                    p = f.parity
                    zlat, zmed = x_lat[p], ctx_raw[p]
                    wait_apart(pool, bn_done, f.count(2, 1), pool_passed)
                    nc.gpsimd.tensor_scalar(var_eps[:, 0:KC], mean_var[:, 0:KC, 1], LN_EPS, None, ADD).then_inc(ln_self, 1)
                    pool.wait_ge(ln_self, f.count(8, 1))
                    nc.gpsimd.tensor_tensor(rstd[:, 0:KC], var_eps[:, 0:KC], half[:, 0:KC], ALU.pow).then_inc(ln_self, 1)
                    wait_apart(pool, ln_self, f.count(8, 2), pool_passed)
                    nc.gpsimd.tensor_scalar(zlat[:, :], x_lat[p][:, :], mean_var[0:Q, 0, 0:1], rstd[0:Q, 0:1],
                                            SUB, MUL).then_inc(lat_z, 1)
                    for c in range(MC):
                        last = nc.gpsimd.tensor_scalar(zmed[:, c, :], ctx_raw[p][:, c, :], mean_var[0:MP, c + 1, 0:1],
                                                       rstd[0:MP, c + 1:c + 2], SUB, MUL)
                    last.then_inc(ln_self, 1)
                    pool.wait_ge(ln_self, f.count(8, 3))
                    nc.gpsimd.tensor_tensor(zmed[:, :, :], zmed[:, :, :], gm[:, :].unsqueeze(1).broadcast_to([MP, MC, D]),
                                            MUL).then_inc(ln_self, 1)
                    pool.wait_ge(ln_self, f.count(8, 4))
                    if not f.first(1):
                        pool.wait_ge(xT_mm, f.count(CC))
                        pool.wait_ge(xn_hi_done, f.count(1))
                    nc.gpsimd.tensor_tensor(xn32[0:MP, 1:KC, :], zmed[:, :, :], bm[:, :].unsqueeze(1).broadcast_to([MP, MC, D]),
                                            ADD)
                    wait_apart(pool, bn_done, f.count(2, 2), pool_passed)
                    nc.gpsimd.tensor_scalar(var_eps[0:Q, KC:KC + 1], mean_var[0:Q, KC, 1:2], LN_EPS, None, ADD).then_inc(ln_self, 1)
                    pool.wait_ge(ln_self, f.count(8, 5))
                    nc.gpsimd.tensor_tensor(rstd[0:Q, KC:KC + 1], var_eps[0:Q, KC:KC + 1], half[0:Q, 0:1], ALU.pow).then_inc(ln_self, 1)
                    wait_apart(pool, ln_self, f.count(8, 6), pool_passed)
                    nc.gpsimd.tensor_scalar(zlat[:, :], zlat[:, :], mean_var[0:Q, KC, 0:1], rstd[0:Q, KC:KC + 1],
                                            SUB, MUL).then_inc(ln_self, 1)
                    pool.wait_ge(ln_self, f.count(8, 7))
                    nc.gpsimd.tensor_tensor(zlat[:, :], zlat[:, :], gl[:, :], MUL).then_inc(ln_self, 1)
                    pool.wait_ge(ln_self, f.count(8, 8))
                    nc.gpsimd.tensor_tensor(xn32[0:Q, 0, :], zlat[:, :], bl[:, :], ADD).then_inc(xn_ready, 1)

                def step(s, t, f):
                    if t is not None:
                        pool.wait_ge(res_in[t.parity], t.uses(1))
                        nc.gpsimd.tensor_tensor(x_res[t.parity][:, :], x_res[t.parity][:, :], gbo[:, :], ADD).then_inc(xb_done, 1)
                    if f is not None:
                        norm(f)
                    if t is not None:
                        for g in range(HG):
                            cols = slice(g * GC, (g + 1) * GC)
                            pool.wait_ge(oT_hi_done, t.count(HG, g + 1))
                            nc.gpsimd.tensor_tensor(oT[1][:, cols], head32[:, cols], oT[0][:, cols].bitcast(F32), SUB
                                                    ).then_inc(oT_done, 1)
                    if f is not None:
                        for g in range(HG):
                            cols = slice(g * GC, (g + 1) * GC)
                            pool.wait_ge(q_hi_done, f.count(HG, g + 1))
                            nc.gpsimd.tensor_tensor(q[1][:, cols], head32[:, cols], q[0][:, cols].bitcast(F32), SUB
                                                    ).then_inc(q_done, 1)
                        p = f.parity
                        pool.wait_ge(xn_hi_done, f.count(1, 1))
                        pool.wait_ge(xn_ready, f.count(1, 1))
                        nc.gpsimd.tensor_tensor(xn[p][1][0:Q, 0, :], xn32[0:Q, 0, :], xn[p][0][0:Q, 0, :].bitcast(F32), SUB)
                        nc.gpsimd.tensor_tensor(xn[p][1][0:MP, 1:KC, :], xn32[0:MP, 1:KC, :],
                                                xn[p][0][0:MP, 1:KC, :].bitcast(F32), SUB).then_inc(xn_lo_done, 1)

                pipeline(pool, NB, step)

            @block.scalar
            def _(act):
                def copy(dst, src, done):
                    nc.scalar.activation(dst, src, ACT.Copy).then_inc(done, 1)

                def exps(s, r):
                    n = tile_no(s, r)
                    act.wait_ge(nmax_done, s.count(R, r + 1))
                    if not (s.first(1) and r < 2):
                        act.wait_ge(turn_mm, s.count(R, r - 1))
                    nc.scalar.activation(probs[n][:, :], score_ps[:, n, 0:KEYS], ACT.Exp, bias=nmax[:, n:n + 1],
                                         accum_out=rowsum[:, n:n + 1]).then_inc(exp_done, 1)

                def pT_hi(b, r):
                    n = tile_no(b, r)
                    act.wait_ge(turn_mm, b.count(R, r + 1))
                    if not b.first(1):
                        act.wait_ge(px_mm, b.count(G4, -2 if r < 3 else 0))
                    copy(pT[0][:, :, r * 128:(r + 1) * 128], turn_ps[0:MP, n, :].rearrange("p (k r) -> p k r", k=KC), pT_hi_done)

                def px_hi(t, k):
                    g, c = divmod(k, CC)
                    act.wait_ge(px_mm, t.count(G4, k + 1))
                    if not t.first(1) and k == 0:
                        act.wait_ge(oT_mm, t.count(HG))
                    copy(px[0][:, c, g * GC:(g + 1) * GC], fill_ps[:, k, 0:GC], px_hi_done)

                def step(s, t, f):
                    for r in range(R):
                        if s is not None:
                            exps(s, r)
                        if r < 2 and t is not None:
                            for k in (2 * r, 2 * r + 1):
                                px_hi(t, k)
                        if r == 2 and f is not None:
                            p = f.parity
                            act.wait_ge(xn_ready, f.count(1, 1))
                            if not f.first(2):
                                act.wait_ge(px_mm, f.count(G4, -G4))
                            nc.scalar.activation(xn[p][0][0:Q, 0, :], xn32[0:Q, 0, :], ACT.Copy)
                            copy(xn[p][0][0:MP, 1:KC, :], xn32[0:MP, 1:KC, :], xn_hi_done)
                        if r == 2 and t is not None:
                            for g in range(HG):
                                cols = slice(g * GC, (g + 1) * GC)
                                act.wait_ge(o32_done, t.count(HG, g + 1))
                                if not t.first(1) and g == 0:
                                    act.wait_ge(out_mm, t.count(1))
                                copy(oT[0][:, cols], head32[:, cols], oT_hi_done)
                        if r == 2 and f is not None:
                            for c in range(CC):
                                act.wait_ge(xT_mm, f.count(CC, c + 1))
                                if not f.first(2) and c == 0:
                                    act.wait_ge(score_mm, f.count(R, -R))
                                copy(xT[f.parity][0][:, c, 0:KEYS], fill_ps[:, 2 + c, 0:KEYS], xT_hi_done)
                        if r == 3 and f is not None:
                            for g in range(HG):
                                cols = slice(g * GC, (g + 1) * GC)
                                act.wait_ge(q32_done, f.count(HG, g + 1))
                                if not f.first(1) and g == 0:
                                    act.wait_ge(qk_mm, f.count(G4))
                                copy(q[0][:, cols], head32[:, cols], q_hi_done)
                        if r == 5 and f is not None:
                            for k in range(G4):
                                g, c = divmod(k, CC)
                                act.wait_ge(qk_mm, f.count(G4, k + 1))
                                copy(qk[f.parity][0][:, c, g * GC:(g + 1) * GC], fill_ps[:, (k + 3) % 4, 0:GC], qk_hi_done)
                        if r == 0 and t is not None:
                            pT_hi(t, R - 1)
                        if r >= 1 and s is not None:
                            pT_hi(s, r - 1)

                pipeline(act, NB, step)

            @block.vector
            def _(dve):
                def norm_stats(f, again):
                    p = f.parity
                    if not again:
                        dve.wait_ge(lat_in[p], f.uses(1))
                        nc.vector.bn_stats(raw_stats[0:Q, 0, :], x_lat[p][:, :])
                        dve.wait_ge(ctx_in[p], f.uses(1))
                        for c in range(MC):
                            last = nc.vector.bn_stats(raw_stats[0:MP, c + 1, :], ctx_raw[p][:, c, :])
                    else:
                        dve.wait_ge(lat_z, f.count(1, 1))
                        last = nc.vector.bn_stats(raw_stats[0:Q, KC, :], x_lat[p][:, :])
                    last.then_inc(bn_raw, 1)
                    wait_apart(dve, bn_raw, f.count(2, 1 + again), dve_passed)
                    if again:
                        nc.vector.bn_aggr(mean_var[0:Q, KC, :], raw_stats[0:Q, KC, :]).then_inc(bn_done, 1)
                        return
                    if not f.first(1):
                        wait_apart(dve, xn_ready, f.count(1), dve_passed)
                    nc.vector.bn_aggr(mean_var[0:Q, 0, :], raw_stats[0:Q, 0, :])
                    for c in range(MC):
                        last = nc.vector.bn_aggr(mean_var[0:MP, c + 1, :], raw_stats[0:MP, c + 1, :])
                    last.then_inc(bn_done, 1)

                def row_max(s, r):
                    n = tile_no(s, r)
                    dve.wait_ge(score_mm, s.count(R, r + 1))
                    nc.vector.tensor_reduce(nmax[:, n:n + 1], score_ps[:, n, 0:KEYS], AX.X, ALU.max, negate=True
                                            ).then_inc(nmax_done, 1)

                def norm_probs(b, r):
                    n = tile_no(b, r)
                    dve.wait_ge(exp_done, b.count(R, r + 1))
                    nc.vector.reciprocal(rinv[:, n:n + 1], rowsum[:, n:n + 1]).then_inc(rinv_done, 1)
                    dve.wait_ge(rinv_done, b.count(R, r + 1))
                    nc.vector.tensor_scalar(probs[n][:, :], probs[n][:, :], rinv[:, n:n + 1], None, MUL).then_inc(probs_done, 1)

                def low(dst, src, ready, value, done):
                    dve.wait_ge(ready, value)
                    nc.vector.tensor_tensor(dst[1], src, dst[0].bitcast(F32), SUB).then_inc(done, 1)

                def pT_lo(b, r):
                    n = tile_no(b, r)
                    low([w[:, :, r * 128:(r + 1) * 128] for w in pT], turn_ps[0:MP, n, :].rearrange("p (k r) -> p k r", k=KC),
                        pT_hi_done, b.count(R, r + 1), pT_done)

                def bias_add(dst, g, src, bias, ready, value, done):
                    dve.wait_ge(ready, value)
                    nc.vector.tensor_tensor(dst[:, g * GC:(g + 1) * GC].rearrange("p (h q) -> p h q", h=GH),
                                            src.rearrange("p (h q) -> p h q", h=GH),
                                            bias[:, g * GH:(g + 1) * GH].unsqueeze(2).broadcast_to([DH, GH, Q]),
                                            ADD).then_inc(done, 1)

                def step(s, t, f):
                    for r in range(R):
                        if r == 0 and t is not None:
                            norm_probs(t, R - 1)
                        if r >= 1 and s is not None:
                            norm_probs(s, r - 1)
                        if s is not None:
                            row_max(s, r)
                        if r < 2 and f is not None:
                            norm_stats(f, r)
                        if r < 2 and t is not None:
                            for k in (2 * r, 2 * r + 1):
                                g, c = divmod(k, CC)
                                low([w[:, c, g * GC:(g + 1) * GC] for w in px], fill_ps[:, k, 0:GC],
                                    px_hi_done, t.count(G4, k + 1), px_done)
                        if r == 2 and t is not None:
                            if s is not None:
                                dve.wait_ge(q_done, s.count(HG, HG))
                            for g in range(HG):
                                bias_add(head32, g, fill_ps[:, g, 0:GC], bvT, oT_mm, t.count(HG, g + 1), o32_done)
                        if r == 2 and f is not None:
                            for c in range(CC):
                                low([w[:, c, 0:KEYS] for w in xT[f.parity]], fill_ps[:, 2 + c, 0:KEYS],
                                    xT_hi_done, f.count(CC, c + 1), xT_done)
                        if r == 3 and f is not None:
                            if t is None and not f.first(1):
                                dve.wait_ge(q_done, f.count(HG))
                            for g in range(HG):
                                if t is not None:
                                    dve.wait_ge(oT_done, t.count(HG, g + 1))
                                bias_add(head32, g, fill_ps[:, g, 0:GC], bqT, q_mm, f.count(HG, g + 1), q32_done)
                        if r == 4 and t is not None:
                            p = t.parity
                            dve.wait_ge(out_mm, t.count(1, 1))
                            dve.wait_ge(xb_done, t.count(1, 1))
                            nc.vector.scalar_tensor_tensor(out=x_res[p][:, :], in0=fill_ps[0:Q, 2, 0:D], scalar=gate[:, 0:1],
                                                           in1=x_res[p][:, :], op0=MUL, op1=ADD).then_inc(out_done, 1)
                        if r == 5 and f is not None:
                            for k in range(G4):
                                g, c = divmod(k, CC)
                                low([w[:, c, g * GC:(g + 1) * GC] for w in qk[f.parity]], fill_ps[:, (k + 3) % 4, 0:GC],
                                    qk_hi_done, f.count(G4, k + 1), qk_done)
                        if r == 0 and t is not None:
                            pT_lo(t, R - 1)
                        if r >= 1 and s is not None:
                            pT_lo(s, r - 1)

                nc.vector.memset(mean_var[:, :, :], 1.0)
                pipeline(dve, NB, step)

            @block.tensor
            def _(pe):
                def scores(s, r):
                    n, p = tile_no(s, r), s.parity
                    if r == 0:
                        pe.wait_ge(qk_done, s.count(G4, G4))
                    if not (s.first(1) and r < 2):
                        pe.wait_ge(exp_done, s.count(R, r - 1))
                    for c in range(CC):
                        last = mm3(nc, score_ps[:, n, 0:KPAD], [w[:, c, r * 128:(r + 1) * 128] for w in qk[p]],
                                   [w[:, c, :] for w in xT[p]], c == 0, c == CC - 1)
                    last.then_inc(score_mm, 1)

                def turn(b, r):
                    n = tile_no(b, r)
                    pe.wait_ge(probs_done, b.count(R, r + 1))
                    if not (b.first(1) and r < 2):
                        pe.wait_ge(pT_done, b.count(R, r - 1))
                    for k in range(KC):
                        last = nc.tensor.transpose(turn_ps[0:MP, n, k * 128:(k + 1) * 128],
                                                   probs[n][:, kc_col[k]:kc_col[k] + MP], ident[:, :])
                    last.then_inc(turn_mm, 1)

                def weighted_rows(t, k):
                    g, c = divmod(k, CC)
                    pe.wait_ge(pT_done, t.count(R, 4 if g == 0 else R))
                    pe.wait_ge(xn_lo_done, t.count(1, 1))
                    for kc, n in enumerate(kc_rows):
                        last = mm3(nc, fill_ps[:, k, 0:GC], [w[0:n, kc, c * 128:(c + 1) * 128] for w in xn[t.parity]],
                                   [w[0:n, kc, g * GC:(g + 1) * GC] for w in pT], kc == 0, kc == KC - 1)
                    last.then_inc(px_mm, 1)

                def head_mm(dst, w, rhs, g, done):
                    for h in range(g * GH, (g + 1) * GH):
                        for c in range(CC):
                            last = mm3(nc, dst[:, (h - g * GH) * Q:(h - g * GH + 1) * Q],
                                       [u[:, c, h * DH:(h + 1) * DH] for u in w], rhs(h, c), c == 0, c == CC - 1)
                    last.then_inc(done, 1)

                def step(s, t, f):
                    for r in range(R):
                        if s is not None:
                            scores(s, r)
                        if r < 2 and t is not None:
                            for k in (2 * r, 2 * r + 1):
                                weighted_rows(t, k)
                        if r == 2 and t is not None:
                            for g in range(HG):
                                pe.wait_ge(px_done, t.count(G4, CC * (g + 1)))
                                head_mm(fill_ps[:, g, :], wv, lambda h, c: [w[:, c, h * Q:(h + 1) * Q] for w in px], g, oT_mm)
                        if r == 2 and f is not None:
                            pe.wait_ge(xn_ready, f.count(1, 1))
                            for c in range(CC):
                                for kc, n in enumerate(kc_rows):
                                    last = nc.tensor.transpose(fill_ps[:, 2 + c, kc_col[kc]:kc_col[kc] + n],
                                                               xn32[0:n, kc, c * 128:(c + 1) * 128], ident[0:n, 0:n])
                                last.then_inc(xT_mm, 1)
                        if r == 3 and f is not None:
                            pe.wait_ge(xT_done, f.count(CC, CC))
                            if t is not None:
                                pe.wait_ge(o32_done, t.count(HG, HG))
                            for g in range(HG):
                                head_mm(fill_ps[:, g, :], wq, lambda h, c: [w[:, c, 0:Q] for w in xT[f.parity]], g, q_mm)
                        if r == 4 and t is not None:
                            pe.wait_ge(oT_done, t.count(HG, HG))
                            for h in range(H):
                                last = mm3(nc, fill_ps[0:Q, 2, 0:D], [w[:, h * Q:(h + 1) * Q] for w in oT],
                                           [w[:, h, :] for w in wo], h == 0, h == H - 1)
                            last.then_inc(out_mm, 1)
                        if r == 5 and f is not None:
                            for k in range(G4):
                                g, c = divmod(k, CC)
                                pe.wait_ge(q_done, f.count(HG, g + 1))
                                if k == 3 and t is not None:
                                    pe.wait_ge(out_done, t.count(1, 1))
                                for h in range(g * GH, (g + 1) * GH):
                                    last = mm3(nc, fill_ps[:, (k + 3) % 4, (h - g * GH) * Q:(h - g * GH + 1) * Q],
                                               [w[:, h, c * 128:(c + 1) * 128] for w in wkT],
                                               [w[:, h * Q:(h + 1) * Q] for w in q], True, True)
                                last.then_inc(qk_mm, 1)
                        if r == 0 and t is not None:
                            turn(t, R - 1)
                        if r >= 1 and s is not None:
                            turn(s, r - 1)

                pipeline(pe, NB, step)


class Chain:

    def __init__(self, eng, sem):
        self.eng, self.sem, self.n = eng, sem, 0

    def link(self, instruction):
        self.n += 1
        instruction.then_inc(self.sem, 1)
        self.eng.wait_ge(self.sem, self.n)


def norm_and_turn(nc, tag, st, x_in, gate_in, X, gate, zT, ident, router, logits_ps, n_logits, per_bank):
    P, T, D = X.shape
    CC = D // 128
    B = 4
    NBLK = T // B

    def sem(name):
        return nc.alloc_semaphore(tag + name)

    def sb(name, shape, dt=F32):
        return st.enter_context(nc.sbuf_tensor(tag + name, shape, dt))
    raw_stats = sb("f_raw_stats", [P, B, 6])
    mean_var = sb("f_mean_var", [P, T, 2])
    var_eps = sb("f_var_eps", [P, T])
    rstd = sb("f_rstd", [P, T])
    half = sb("f_half", [P, B])
    z = [sb(f"f_z{i}", [P, B, D]) for i in range(2)]
    turn_ps = st.enter_context(nc.psum_tensor(tag + "f_turn_ps", [P, CC, B * P], F32))
    x_loaded = [sem(f"x_loaded{i}") for i in range(NBLK)]
    gate_loaded, ident_ok, gate_done = sem("gate_loaded"), sem("ident_ok_f"), sem("gate_done")
    stats_done, mv_done, eps_done, rstd_done = (sem(n) for n in ("stats_done", "mv_done", "eps_done", "rstd_done"))
    z_done, turned, hi_done, lo_done, logits_done = (sem(n) for n in ("z_done", "turned", "z_hi_done", "z_lo_done", "logits_done"))
    x_v = x_in.rearrange("(t p) d -> p t d", p=P)

    def sync(sp):
        for b in range(NBLK):
            sp.dma_start(X[:, B * b:B * (b + 1), :], x_v[:, B * b:B * (b + 1), :]).then_inc(x_loaded[b], 16)

    def gpsimd(pool):
        make_identity(nc, pool, ident, ident_ok)
        nc.gpsimd.memset(half[:, :], -0.5).then_inc(ident_ok, 1)
        pool.wait_ge(ident_ok, 3)
        for b in range(NBLK):
            tiles = slice(B * b, B * (b + 1))
            pool.wait_ge(mv_done, b + 1)
            nc.gpsimd.tensor_scalar(var_eps[:, tiles], mean_var[:, tiles, 1], LN_EPS, None, ADD).then_inc(eps_done, 1)
            pool.wait_ge(eps_done, b + 1)
            nc.gpsimd.tensor_tensor(rstd[:, tiles], var_eps[:, tiles], half[:, :], ALU.pow).then_inc(rstd_done, 1)

    def scalar(act):
        act.dma_start(gate[:, :], gate_in.partition_broadcast(P)).then_inc(gate_loaded, 16)
        act.wait_ge(gate_loaded, 16)
        nc.scalar.activation(gate[:, :], gate[:, :], ACT.Tanh).then_inc(gate_done, 1)
        for b in range(NBLK):
            for c in range(CC):
                act.wait_ge(turned, CC * b + c + 1)
                nc.scalar.activation(zT[0][:, c, b * B * P:(b + 1) * B * P], turn_ps[:, c, :], ACT.Copy).then_inc(hi_done, 1)

    def vector(dve):
        def stats(b):
            dve.wait_ge(x_loaded[b], 16)
            for k in range(B):
                last = nc.vector.bn_stats(raw_stats[:, k, :], X[:, B * b + k, :])
            last.then_inc(stats_done, 1)
            dve.wait_ge(stats_done, b + 1)
            for k in range(B):
                last = nc.vector.bn_aggr(mean_var[:, B * b + k, :], raw_stats[:, k, :])
            last.then_inc(mv_done, 1)

        def scaled(b):
            dve.wait_ge(rstd_done, b + 1)
            if b >= 2:
                dve.wait_ge(turned, CC * (b - 1))
            for k in range(B):
                t = B * b + k
                last = nc.vector.tensor_scalar(z[b % 2][:, k, :], X[:, t, :], mean_var[:, t, 0:1], rstd[:, t:t + 1], SUB, MUL)
            last.then_inc(z_done, 1)

        def low(b):
            for c in range(CC):
                dve.wait_ge(hi_done, CC * b + c + 1)
                cols = slice(b * B * P, (b + 1) * B * P)
                nc.vector.tensor_tensor(zT[1][:, c, cols], turn_ps[:, c, :], zT[0][:, c, cols].bitcast(F32), SUB).then_inc(lo_done, 1)

        stats(0)
        for b in range(NBLK):
            if b + 1 < NBLK:
                dve.wait_ge(mv_done, b + 1)
                stats(b + 1)
            scaled(b)
            if b >= 1:
                low(b - 1)
        low(NBLK - 1)

    def tensor(pe):
        pe.wait_ge(ident_ok, 2)

        def turn(b):
            pe.wait_ge(z_done, b + 1)
            for c in range(CC):
                if b >= 1:
                    pe.wait_ge(lo_done, CC * (b - 1) + c + 1)
                for k in range(B):
                    last = nc.tensor.transpose(turn_ps[:, c, k * P:(k + 1) * P], z[b % 2][:, k, c * 128:(c + 1) * 128], ident[:, :])
                last.then_inc(turned, 1)

        def logits(b):
            pe.wait_ge(lo_done, CC * (b + 1))
            for k in range(B):
                t = B * b + k
                bank, at = divmod(t, per_bank)
                for c in range(CC):
                    last = mm3(nc, logits_ps[:, bank, at * n_logits:(at + 1) * n_logits],
                               [w[:, c, t * P:(t + 1) * P] for w in zT], [w[:, c, :] for w in router], c == 0, c == CC - 1)
            last.then_inc(logits_done, 1)

        turn(0)
        for b in range(1, NBLK):
            turn(b)
            logits(b - 1)
        logits(NBLK - 1)

    return sync, gpsimd, scalar, vector, tensor, logits_done, gate_done, NBLK


def dense_experts(nc, tag, X, zT, coef, packed, x_out):
    P, T, D = X.shape
    CC = D // 128
    NE = packed.shape[0]
    B = 4
    NBLK = T // B
    WIDTH = packed.shape[2]
    UP, DOWN = CC * 128, 2 * CC * 128
    assert NE % 2 == 0 and NE >= 4

    with ExitStack() as st:
        def sem(name):
            return nc.alloc_semaphore(tag + name)

        def sb(name, shape, dt=F32):
            return st.enter_context(nc.sbuf_tensor(tag + name, shape, dt))
        w_raw = [sb(f"w_raw{p}", [P, WIDTH]) for p in range(2)]
        w = [(sb(f"w_hi{p}", [P, WIDTH], F32R), sb(f"w_lo{p}", [P, WIDTH], F32R)) for p in range(2)]
        weight = [sb(f"weight{p}", [P, T]) for p in range(2)]
        gated = [sb(f"gated{n}", [P, B * P]) for n in range(2)]
        h32 = [sb(f"h32_{n}", [P, B * P]) for n in range(2)]
        h = [(sb(f"h_hi{n}", [P, B * P], F32R), sb(f"h_lo{n}", [P, B * P], F32R)) for n in range(2)]
        gate_ps = st.enter_context(nc.psum_tensor(tag + "gate_ps", [P, 2, 512], F32))
        up_ps = st.enter_context(nc.psum_tensor(tag + "up_ps", [P, 2, 512], F32))
        down_ps = st.enter_context(nc.psum_tensor(tag + "down_ps", [P, 2, B * D], F32))
        w_in = [sem(f"w_in{p}") for p in range(2)]
        w_hi_done, w_lo_done, weight_done = sem("w_hi_done"), sem("w_lo_done"), sem("weight_done")
        gate_mm, up_mm, down_mm = sem("gate_mm"), sem("up_mm"), sem("down_mm")
        gated_done, h32_done, h_hi_done, h_done, added = (sem(n) for n in ("gated_done", "h32_done", "h_hi_done", "h_done", "added"))
        x_stored = sem("x_stored")
        block = st.enter_context(nc.Block())

        def experts(eng, one, after=None):
            for e in range(2):
                one(Batch(0, e))
            with eng.Fori(0, (NE - 2) // 2) as i:
                for off in (2, 3):
                    one(Batch(i, off))
            if after:
                after()

        def odd(e, j):
            return (e.off * NBLK + j) % 2

        def early(e, j, n):
            return isinstance(e.i, int) and e.off * NBLK + j < n

        @block.sync
        def _(sp):
            def one(e):
                p = e.parity
                if not e.first(2):
                    sp.wait_ge(w_lo_done, e.count(1, -1))
                sp.dma_start(w_raw[p][:, :], packed[bass.ds(e.count(1), 1), :, :].rearrange("a p n -> p (a n)")).then_inc(w_in[p], 16)
            experts(sp, one)
            sp.wait_ge(added, NE * NBLK)
            sp.dma_start(x_out.rearrange("(t p) d -> p t d", p=P), X[:, :, :]).then_inc(x_stored, 16)
            sp.wait_ge(x_stored, 16)

        @block.gpsimd
        def _(pool):
            def one(e):
                def split_low():
                    p = e.parity
                    pool.wait_ge(w_hi_done, e.count(1, 1))
                    nc.gpsimd.tensor_tensor(w[p][1][:, :], w_raw[p][:, :], w[p][0][:, :].bitcast(F32), SUB).then_inc(w_lo_done, 1)
                split_low()
                for j in range(NBLK):
                    n = odd(e, j)
                    pool.wait_ge(h_hi_done, e.count(NBLK, j + 1))
                    nc.gpsimd.tensor_tensor(h[n][1][:, :], h32[n][:, :], h[n][0][:, :].bitcast(F32), SUB).then_inc(h_done, 1)
            experts(pool, one)

        @block.scalar
        def _(act):
            def one(e):
                p = e.parity
                act.wait_ge(w_in[p], e.uses(1))
                if not e.first(2):
                    act.wait_ge(down_mm, e.count(NBLK, -NBLK))
                nc.scalar.activation(w[p][0][:, :], w_raw[p][:, :], ACT.Copy).then_inc(w_hi_done, 1)
                for j in range(NBLK):
                    n = odd(e, j)
                    act.wait_ge(gate_mm, e.count(NBLK, j + 1))
                    if not early(e, j, 2):
                        act.wait_ge(h32_done, e.count(NBLK, j - 1))
                    nc.scalar.activation(gated[n][:, :], gate_ps[:, n, :], ACT.Silu).then_inc(gated_done, 1)
                    act.wait_ge(h32_done, e.count(NBLK, j + 1))
                    if not early(e, j, 2):
                        act.wait_ge(down_mm, e.count(NBLK, j - 1))
                    nc.scalar.activation(h[n][0][:, :], h32[n][:, :], ACT.Copy).then_inc(h_hi_done, 1)
            experts(act, one)

        @block.vector
        def _(dve):
            def add(e, j):
                n = odd(e, j)
                dve.wait_ge(down_mm, e.count(NBLK, j + 1))
                if j == 0:
                    dve.wait_ge(weight_done, e.count(1, 1))
                if not early(e, j, NBLK):
                    dve.wait_ge(added, e.count(NBLK, j + 1 - NBLK))
                for k in range(B):
                    t = B * j + k
                    last = nc.vector.scalar_tensor_tensor(out=X[:, t, :], in0=down_ps[:, n, k * D:(k + 1) * D],
                                                          scalar=weight[e.parity][:, t:t + 1], in1=X[:, t, :],
                                                          op0=MUL, op1=ADD)
                last.then_inc(added, 1)

            def one(e):
                nc.vector.tensor_copy(weight[e.parity][:, :], coef[:, bass.ds(e.count(1), 1), :].rearrange("p a t -> p (a t)")).then_inc(weight_done, 1)
                for j in range(NBLK):
                    n = odd(e, j)
                    dve.wait_ge(gated_done, e.count(NBLK, j + 1))
                    dve.wait_ge(up_mm, e.count(NBLK, j + 1))
                    if not early(e, j, 2):
                        dve.wait_ge(h_done, e.count(NBLK, j - 1))
                    nc.vector.tensor_tensor(h32[n][:, :], gated[n][:, :], up_ps[:, n, :], MUL).then_inc(h32_done, 1)
                    if j:
                        add(e, j - 1)
                    elif not early(e, j, 1):
                        add(e + -1, NBLK - 1)
            experts(dve, one, lambda: add(Batch(0, NE - 1), NBLK - 1))

        @block.tensor
        def _(pe):
            def down(e, j):
                n, p = odd(e, j), e.parity
                pe.wait_ge(h_done, e.count(NBLK, j + 1))
                if not early(e, j, 2):
                    pe.wait_ge(added, e.count(NBLK, j - 1))
                for k in range(B):
                    last = mm3(nc, down_ps[:, n, k * D:(k + 1) * D], [u[:, k * P:(k + 1) * P] for u in h[n]],
                               [u[:, DOWN:DOWN + D] for u in w[p]], True, True)
                last.then_inc(down_mm, 1)

            def one(e):
                p = e.parity
                for j in range(NBLK):
                    n = odd(e, j)
                    if j == 0:
                        pe.wait_ge(w_lo_done, e.count(1, 1))
                    if not early(e, j, 2):
                        pe.wait_ge(h32_done, e.count(NBLK, j - 1))
                    for ps, at, done in ((gate_ps, 0, gate_mm), (up_ps, UP, up_mm)):
                        for c in range(CC):
                            last = mm3(nc, ps[:, n, :], [u[:, at + c * 128:at + (c + 1) * 128] for u in w[p]],
                                       [u[:, c, j * B * P:(j + 1) * B * P] for u in zT], c == 0, c == CC - 1)
                        last.then_inc(done, 1)
                    if j:
                        down(e, j - 1)
                    elif not early(e, j, 1):
                        down(e + -1, NBLK - 1)
            experts(pe, one, lambda: down(Batch(0, NE - 1), NBLK - 1))


def softmax_top2_ffn(nc, x_in, gate_in, routerT, packed, x_out):
    T = x_in.shape[0] // 128
    D = x_in.shape[1]
    CC = D // 128
    NR = routerT.shape[2]
    NE = packed.shape[0]
    TOP = 2
    with ExitStack() as outer:
        def sb(name, shape, dt=F32, stack=outer):
            return stack.enter_context(nc.sbuf_tensor(name, shape, dt))
        X = sb("X", [128, T, D])
        gate = sb("gate", [128, 1])
        zT = (sb("zT_hi", [128, CC, T * 128], F32R), sb("zT_lo", [128, CC, T * 128], F32R))
        coef = sb("coef", [128, NE, T])
        ident = sb("ident_f", [128, 128])
        with ExitStack() as st:
            def sem(name):
                return nc.alloc_semaphore(name)
            router_raw = sb("router_raw", [128, CC, NR], stack=st)
            router = (sb("router_hi", [128, CC, NR], F32R, st), sb("router_lo", [128, CC, NR], F32R, st))
            prob = sb("prob", [128, T, NR], stack=st)
            best = sb("best", [128, T, 8], stack=st)
            best_at = sb("best_at", [128, T, 8], U32, st)
            at_f = sb("at_f", [128, T, 8], stack=st)
            numbers = sb("numbers", [128, NR], stack=st)
            hit = sb("hit", [128, T, NR], stack=st)
            total = sb("total", [128, T], stack=st)
            peak = sb("peak", [128, T], stack=st)
            logits_ps = st.enter_context(nc.psum_tensor("logits_ps", [128, 1, 512], F32))
            router_in, router_ok, numbers_ok, shifted, exp_done, own = (
                sem(n) for n in ("router_in", "router_ok", "numbers_ok", "shifted", "exp_done_r", "own"))
            sync, gpsimd, scalar, vector, tensor, logits_done, gate_done, NBLK = norm_and_turn(
                nc, "L1_", st, x_in, gate_in, X, gate, zT, ident, router, logits_ps, NR, T)
            block = st.enter_context(nc.Block())

            @block.sync
            def _(sp):
                sp.dma_start(router_raw[:, :, :], routerT).then_inc(router_in, 16)
                sync(sp)

            @block.gpsimd
            def _(pool):
                nc.gpsimd.iota(numbers[:, :], pattern=[[1, NR]], base=0, channel_multiplier=0,
                               allow_small_or_imprecise_dtypes=True).then_inc(numbers_ok, 1)
                gpsimd(pool)

            @block.scalar
            def _(act):
                act.wait_ge(router_in, 16)
                nc.scalar.activation(router[0][:, :, :], router_raw[:, :, :], ACT.Copy).then_inc(router_ok, 1)
                scalar(act)
                act.wait_ge(shifted, 1)
                nc.scalar.activation(prob[:, :, :], prob[:, :, :], ACT.Exp).then_inc(exp_done, 1)

            @block.vector
            def _(dve):
                chain = Chain(dve, own)
                dve.wait_ge(router_ok, 1)
                nc.vector.tensor_tensor(router[1][:, :, :], router_raw[:, :, :], router[0][:, :, :].bitcast(F32), SUB).then_inc(router_ok, 1)
                vector(dve)
                dve.wait_ge(logits_done, NBLK)
                logits = logits_ps[:, 0, 0:T * NR].rearrange("p (t e) -> p t e", e=NR)
                chain.link(nc.vector.tensor_reduce(peak[:, :], logits, AX.X, ALU.max))
                nc.vector.tensor_tensor(prob[:, :, :], logits, peak[:, :].unsqueeze(2).broadcast_to([128, T, NR]), SUB).then_inc(shifted, 1)
                dve.wait_ge(exp_done, 1)
                chain.link(nc.vector.tensor_reduce(total[:, :], prob[:, :, :], AX.X, ADD))
                chain.link(nc.vector.reciprocal(total[:, :], total[:, :]))
                chain.link(nc.vector.tensor_tensor(prob[:, :, :], prob[:, :, :], total[:, :].unsqueeze(2).broadcast_to([128, T, NR]), MUL))
                for t in range(T):
                    last = nc.vector.max(best[:, t, :], prob[:, t, :])
                chain.link(last)
                for t in range(T):
                    last = nc.vector.max_index(best_at[:, t, :], best[:, t, :], prob[:, t, :])
                chain.link(last)
                chain.link(nc.vector.tensor_copy(at_f[:, :, :], best_at[:, :, :]))
                dve.wait_ge(numbers_ok, 1)
                dve.wait_ge(gate_done, 1)
                for k in range(TOP):
                    chain.link(nc.vector.tensor_tensor(hit[:, :, :], numbers[:, :].unsqueeze(1).broadcast_to([128, T, NR]),
                                                       at_f[:, :, k:k + 1].broadcast_to([128, T, NR]), ALU.is_equal))
                    dst = prob if k == 0 else hit
                    chain.link(nc.vector.tensor_tensor(dst[:, :, :], hit[:, :, :], best[:, :, k:k + 1].broadcast_to([128, T, NR]), MUL))
                chain.link(nc.vector.tensor_tensor(prob[:, :, :], prob[:, :, :], hit[:, :, :], ADD))
                nc.vector.tensor_scalar(coef[:, 0:NR, :], prob[:, :, :].rearrange("p t e -> p e t"), gate[:, 0:1], None, MUL)
                chain.link(nc.vector.memset(coef[:, NR:NE, :], 1.0))
                nc.vector.tensor_scalar(coef[:, NR:NE, :], coef[:, NR:NE, :], gate[:, 0:1], None, MUL)

            @block.tensor
            def _(pe):
                pe.wait_ge(router_ok, 2)
                tensor(pe)

        dense_experts(nc, "L1_", X, zT, coef, packed, x_out)


def strided_attention(nc, x, ctx, gate_in, WqT, WkT, WvT, WoT, biasT, bo, row_mask, col_mask, x_out):
    NB, Q, D = x.shape
    H = 16
    DH = D // H
    PER = ctx.shape[1] // H
    KEYS = PER * H
    CC = D // 128
    chunks = [(k, min(128, KEYS - k)) for k in range(0, KEYS, 128)]
    KC = len(chunks)
    SCALE = float(DH) ** -0.5
    C_T, Z_Q, K_0, S_B, P_OUT, O_B = 0, 2, 3, 5, 6, 7

    with ExitStack() as st:
        def sb(name, shape, dt=F32):
            return st.enter_context(nc.sbuf_tensor(name, shape, dt))

        def split_sb(name, shape):
            return (sb(name + "_hi", shape, F32R), sb(name + "_lo", shape, F32R))

        def sem(name):
            return nc.alloc_semaphore(name)

        raw = sb("c_w_raw", [128, 4, CC * D])
        w = split_sb("c_w", [128, 4, CC * D])
        wq, wk, wv, wo = ([part[:, n, :].rearrange("p (c o) -> p c o", c=CC) for part in w] for n in range(4))
        bias = sb("c_bias", [128, 3 * CC])
        bo_row = sb("c_bo", [Q, D])
        gate = sb("c_gate", [Q, 1])
        rmask = sb("c_row_mask", [128, D])
        cmask = sb("c_col_mask", [128, CC, KEYS])
        ident = sb("c_ident", [128, 128])
        half = sb("c_half", [Q, 1])
        rows = [sb(f"c_rows{p}", [128, KC, D]) for p in range(2)]
        x_in = [sb(f"c_x_in{p}", [Q, D]) for p in range(2)]
        x_res = [sb(f"c_x_res{p}", [Q, D]) for p in range(2)]
        stats = sb("c_stats", [Q, 6])
        mv = sb("c_mv", [Q, 2])
        var_eps = sb("c_var_eps", [Q, 1])
        rstd = sb("c_rstd", [Q, 1])
        z = sb("c_z", [Q, D])
        cT = split_sb("c_cT", [128, CC, KEYS])
        zT = split_sb("c_zT", [128, CC * Q])
        k32 = sb("c_k32", [128, CC, KEYS])
        kT = split_sb("c_kT", [128, CC, KEYS])
        q32 = sb("c_q32", [128, CC * Q])
        qT = split_sb("c_qT", [128, CC * Q])
        v32 = sb("c_v32", [128, KC, D])
        v = [split_sb(f"c_v{p}", [128, KC, D]) for p in range(2)]
        peak = sb("c_peak", [Q, H])
        e32 = sb("c_e32", [Q, KEYS])
        total = sb("c_total", [Q, H])
        inv = sb("c_inv", [Q, H])
        prob = sb("c_prob", [Q, KC * 128])
        pT = split_sb("c_pT", [128, KC * Q])
        o32 = sb("c_o32", [128, CC * Q])
        oT = split_sb("c_oT", [128, CC * Q])
        ps = st.enter_context(nc.psum_tensor("c_ps", [128, 8, 512], F32))

        w_in, small_in, ident_ok, gate_ok, w_hi_ok, w_lo_ok, bo_ok = (
            sem(n) for n in ("c_w_in", "c_small_in", "c_ident_ok", "c_gate_ok", "c_w_hi_ok", "c_w_lo_ok", "c_bo_ok"))
        rows_in, x_in_in, res_in, stored = ([sem(f"c_{n}{p}") for p in range(2)] for n in ("rows_in", "x_in_in", "res_in", "stored"))
        stats_done, mv_done, eps_done, rstd_done, z_done = (sem("c_" + n) for n in ("stats_done", "mv_done", "eps_done", "rstd_done", "z_done"))
        cT_mm, cT_hi_done, cT_done = (sem("c_" + n) for n in ("cT_mm", "cT_hi_done", "cT_done"))
        zT_mm, zT_hi_done, zT_done = (sem("c_" + n) for n in ("zT_mm", "zT_hi_done", "zT_done"))
        k_mm, k32_done, k_hi_done, k_done = (sem("c_" + n) for n in ("k_mm", "k32_done", "k_hi_done", "k_done"))
        q_mm, q32_done, q_hi_done, q_done = (sem("c_" + n) for n in ("q_mm", "q32_done", "q_hi_done", "q_done"))
        v_mm, v32_done, v_hi_done, v_done = (sem("c_" + n) for n in ("v_mm", "v32_done", "v_hi_done", "v_done"))
        s_mm, peak_done, e32_done, exp_done, total_done, inv_done, prob_done = (
            sem("c_" + n) for n in ("s_mm", "peak_done", "e32_done", "exp_done", "total_done", "inv_done", "prob_done"))
        pT_mm, pT_hi_done, pT_done = (sem("c_" + n) for n in ("pT_mm", "pT_hi_done", "pT_done"))
        o_mm, o32_done, o_hi_done, o_done = (sem("c_" + n) for n in ("o_mm", "o32_done", "o_hi_done", "o_done"))
        out_mm, xb_done, out_done = (sem("c_" + n) for n in ("out_mm", "xb_done", "out_done"))
        pool_passed, dve_passed = sem("c_pool_passed"), sem("c_dve_passed")
        block = st.enter_context(nc.Block())

        def at(b):
            return bass.ds(b.count(1), 1)

        def heads(ap):
            return ap.rearrange("q (m h) -> q h m", h=H)

        @block.sync
        def _(sp):
            for n, m in enumerate((WqT, WkT, WvT, WoT)):
                sp.dma_start(raw[:, n, :], m.rearrange("p c o -> p (c o)")).then_inc(w_in, 16)

            def step(s, t, f):
                if f is not None:
                    p = f.parity
                    if not f.first(2):
                        sp.wait_ge(cT_mm, f.count(1, -1))
                        sp.wait_ge(z_done, f.count(1, -1))
                    whole = KEYS // 128
                    sp.dma_start(rows[p][:, 0:whole, :], ctx[at(f), 0:whole * 128, :].rearrange("a (k p) d -> p (a k) d", p=128)
                                 ).then_inc(rows_in[p], 16)
                    sp.dma_start(rows[p][0:KEYS - whole * 128, whole, :], ctx[at(f), whole * 128:KEYS, :].rearrange("a p d -> p (a d)")
                                 ).then_inc(rows_in[p], 16)
                    sp.dma_start(x_in[p][:, :], x[at(f), :, :].rearrange("a q d -> q (a d)")).then_inc(x_in_in[p], 16)
                if s is not None:
                    if not s.first(2):
                        sp.wait_ge(stored[s.parity], s.uses())
                    sp.dma_start(x_res[s.parity][:, :], x[at(s), :, :].rearrange("a q d -> q (a d)")).then_inc(res_in[s.parity], 16)
                if t is not None:
                    sp.wait_ge(out_done, t.count(1, 1))
                    sp.dma_start(x_out[at(t), :, :].rearrange("a q d -> q (a d)"), x_res[t.parity][:, :]).then_inc(stored[t.parity], 16)

            pipeline(sp, NB, step)
            for p in range(2):
                sp.wait_ge(stored[p], 16 * (NB // 2))

        @block.gpsimd
        def _(pool):
            make_identity(nc, pool, ident, ident_ok)
            nc.gpsimd.memset(half[:, :], -0.5).then_inc(ident_ok, 1)
            pool.wait_ge(gate_ok, 1)
            nc.gpsimd.tensor_scalar(bo_row[:, :], bo_row[:, :], gate[:, 0:1], None, MUL).then_inc(bo_ok, 1)
            pool.wait_ge(bo_ok, 1)
            pool.wait_ge(ident_ok, 3)

            def low(dst, src, ready, b, done):
                pool.wait_ge(ready, b.count(1, 1))
                nc.gpsimd.tensor_tensor(dst[1], src, dst[0].bitcast(F32), SUB).then_inc(done, 1)

            def step(s, t, f):
                if f is not None:
                    wait_apart(pool, mv_done, f.count(1, 1), pool_passed)
                    nc.gpsimd.tensor_scalar(var_eps[:, :], mv[:, 1:2], LN_EPS, None, ADD).then_inc(eps_done, 1)
                    pool.wait_ge(eps_done, f.count(1, 1))
                    nc.gpsimd.tensor_tensor(rstd[:, :], var_eps[:, :], half[:, :], ALU.pow).then_inc(rstd_done, 1)
                    if not f.first(1):
                        pool.wait_ge(zT_mm, f.count(1))
                    wait_apart(pool, rstd_done, f.count(1, 1), pool_passed)
                    nc.gpsimd.tensor_scalar(z[:, :], x_in[f.parity][:, :], mv[:, 0:1], rstd[:, 0:1], SUB, MUL).then_inc(z_done, 1)
                if t is not None:
                    pool.wait_ge(res_in[t.parity], t.uses(1))
                    nc.gpsimd.tensor_tensor(x_res[t.parity][:, :], x_res[t.parity][:, :], bo_row[:, :], ADD).then_inc(xb_done, 1)
                if f is not None:
                    low([u[:, :, :] for u in kT], k32[:, :, :], k_hi_done, f, k_done)
                if t is not None:
                    low([u[:, :] for u in oT], o32[:, :], o_hi_done, t, o_done)
                if f is not None:
                    last = KC - 1
                    n = chunks[last][1]
                    hi, lo = v[f.parity]
                    pool.wait_ge(v_hi_done, f.count(1, 1))
                    nc.gpsimd.tensor_tensor(lo[:, 0:last, :], v32[:, 0:last, :], hi[:, 0:last, :].bitcast(F32), SUB)
                    nc.gpsimd.tensor_tensor(lo[0:n, last, :], v32[0:n, last, :], hi[0:n, last, :].bitcast(F32), SUB).then_inc(v_done, 1)
                    low([u[:, :] for u in qT], q32[:, :], q_hi_done, f, q_done)

            pipeline(pool, NB, step)

        @block.scalar
        def _(act):
            small = [(gate, gate_in.partition_broadcast(Q)), (bo_row, bo.partition_broadcast(Q)),
                     (bias, biasT), (rmask, row_mask), (cmask, col_mask)]
            for dst, src in small:
                act.dma_start(dst[:], src).then_inc(small_in, 16)
            act.wait_ge(small_in, 16 * len(small))
            nc.scalar.activation(gate[:, :], gate[:, :], ACT.Tanh).then_inc(gate_ok, 1)
            act.wait_ge(w_in, 64)
            nc.scalar.activation(w[0][:, :, :], raw[:, :, :], ACT.Copy).then_inc(w_hi_ok, 1)

            def high(dst, src, ready, b, done):
                act.wait_ge(ready, b.count(1, 1))
                nc.scalar.activation(dst[0], src, ACT.Copy).then_inc(done, 1)

            def step(s, t, f):
                if f is not None:
                    high([u[:, :, :] for u in cT], ps[:, C_T:C_T + CC, 0:KEYS], cT_mm, f, cT_hi_done)
                if t is not None:
                    high([u[:, :] for u in pT], ps[:, P_OUT, 0:KC * Q], pT_mm, t, pT_hi_done)
                if s is not None:
                    act.wait_ge(e32_done, s.count(1, 1))
                    nc.scalar.activation(e32[:, :], e32[:, :], ACT.Exp).then_inc(exp_done, 1)
                if f is not None:
                    if not f.first(1):
                        act.wait_ge(s_mm, f.count(1))
                    high([u[:, :, :] for u in kT], k32[:, :, :], k32_done, f, k_hi_done)
                    high([u[:, :] for u in zT], ps[:, Z_Q, 0:CC * Q], zT_mm, f, zT_hi_done)
                if t is not None:
                    if not t.first(1):
                        act.wait_ge(out_mm, t.count(1))
                    high([u[:, :] for u in oT], o32[:, :], o32_done, t, o_hi_done)
                if f is not None:
                    last = KC - 1
                    n = chunks[last][1]
                    hi = v[f.parity][0]
                    if not f.first(2):
                        act.wait_ge(o_mm, f.count(1, -1))
                    act.wait_ge(v32_done, f.count(1, 1))
                    nc.scalar.activation(hi[:, 0:last, :], v32[:, 0:last, :], ACT.Copy)
                    nc.scalar.activation(hi[0:n, last, :], v32[0:n, last, :], ACT.Copy).then_inc(v_hi_done, 1)
                    high([u[:, :] for u in qT], q32[:, :], q32_done, f, q_hi_done)

            pipeline(act, NB, step)

        @block.vector
        def _(dve):
            nc.vector.memset(prob[:, :], 0.0)
            dve.wait_ge(w_hi_ok, 1)
            nc.vector.tensor_tensor(w[1][:, :, :], raw[:, :, :], w[0][:, :, :].bitcast(F32), SUB).then_inc(w_lo_ok, 1)
            dve.wait_ge(small_in, 16 * 5)

            def low(dst, src, ready, b, done):
                dve.wait_ge(ready, b.count(1, 1))
                nc.vector.tensor_tensor(dst[1], src, dst[0].bitcast(F32), SUB).then_inc(done, 1)

            def step(s, t, f):
                if f is not None:
                    dve.wait_ge(x_in_in[f.parity], f.uses(1))
                    nc.vector.bn_stats(stats[:, :], x_in[f.parity][:, :]).then_inc(stats_done, 1)
                    if not f.first(1):
                        wait_apart(dve, z_done, f.count(1), dve_passed)
                    wait_apart(dve, stats_done, f.count(1, 1), dve_passed)
                    nc.vector.bn_aggr(mv[:, :], stats[:, :]).then_inc(mv_done, 1)
                    low([u[:, :, :] for u in cT], ps[:, C_T:C_T + CC, 0:KEYS], cT_hi_done, f, cT_done)
                if t is not None:
                    low([u[:, :] for u in pT], ps[:, P_OUT, 0:KC * Q], pT_hi_done, t, pT_done)
                if s is not None:
                    dve.wait_ge(s_mm, s.count(1, 1))
                    nc.vector.tensor_reduce(peak[:, :], heads(ps[0:Q, S_B, 0:KEYS]), AX.X, ALU.max).then_inc(peak_done, 1)
                    dve.wait_ge(peak_done, s.count(1, 1))
                    nc.vector.tensor_tensor(heads(e32[:, :]), heads(ps[0:Q, S_B, 0:KEYS]),
                                            peak[:, :].unsqueeze(2).broadcast_to([Q, H, PER]), SUB).then_inc(e32_done, 1)
                if f is not None:
                    dve.wait_ge(k_mm, f.count(1, 1))
                    if not f.first(1):
                        dve.wait_ge(k_done, f.count(1))
                    for c in range(CC):
                        last = nc.vector.scalar_tensor_tensor(out=k32[:, c, :], in0=ps[:, K_0 + c, 0:KEYS],
                                                              scalar=bias[:, CC + c:CC + c + 1], in1=cmask[:, c, :],
                                                              op0=ADD, op1=MUL)
                    last.then_inc(k32_done, 1)
                    low([u[:, :] for u in zT], ps[:, Z_Q, 0:CC * Q], zT_hi_done, f, zT_done)
                if t is not None:
                    dve.wait_ge(o_mm, t.count(1, 1))
                    if not t.first(1):
                        dve.wait_ge(o_done, t.count(1))
                    for c in range(CC):
                        last = nc.vector.tensor_scalar(o32[:, c * Q:(c + 1) * Q], ps[:, O_B, c * Q:(c + 1) * Q],
                                                       bias[:, 2 * CC + c:2 * CC + c + 1], None, ADD)
                    last.then_inc(o32_done, 1)
                if s is not None:
                    dve.wait_ge(exp_done, s.count(1, 1))
                    nc.vector.tensor_reduce(total[:, :], heads(e32[:, :]), AX.X, ADD).then_inc(total_done, 1)
                    dve.wait_ge(total_done, s.count(1, 1))
                    nc.vector.reciprocal(inv[:, :], total[:, :]).then_inc(inv_done, 1)
                    dve.wait_ge(inv_done, s.count(1, 1))
                    nc.vector.tensor_tensor(heads(prob[:, 0:KEYS]), heads(e32[:, :]),
                                            inv[:, :].unsqueeze(2).broadcast_to([Q, H, PER]), MUL).then_inc(prob_done, 1)
                if f is not None:
                    dve.wait_ge(v_mm, f.count(1, 1))
                    if not f.first(1):
                        dve.wait_ge(v_done, f.count(1))
                    for k, (_, n) in enumerate(chunks):
                        src = ps[0:n, C_T + k // 2, (k % 2) * D:(k % 2 + 1) * D]
                        last = nc.vector.tensor_tensor(v32[0:n, k, :], src, rmask[0:n, :], MUL)
                    last.then_inc(v32_done, 1)
                    dve.wait_ge(q_mm, f.count(1, 1))
                    if not f.first(1):
                        dve.wait_ge(q_done, f.count(1))
                    for c in range(CC):
                        last = nc.vector.tensor_scalar(q32[:, c * Q:(c + 1) * Q], ps[:, Z_Q, c * Q:(c + 1) * Q],
                                                       bias[:, c:c + 1], SCALE, ADD, MUL)
                    last.then_inc(q32_done, 1)
                if t is not None:
                    dve.wait_ge(out_mm, t.count(1, 1))
                    dve.wait_ge(xb_done, t.count(1, 1))
                    nc.vector.scalar_tensor_tensor(out=x_res[t.parity][:, :], in0=ps[0:Q, P_OUT, 0:D], scalar=gate[:, 0:1],
                                                   in1=x_res[t.parity][:, :], op0=MUL, op1=ADD).then_inc(out_done, 1)

            pipeline(dve, NB, step)

        @block.tensor
        def _(pe):
            pe.wait_ge(ident_ok, 2)
            pe.wait_ge(w_lo_ok, 1)

            def step(s, t, f):
                if f is not None:
                    pe.wait_ge(rows_in[f.parity], f.uses(1) + f.uses(1))
                    if not f.first(1):
                        pe.wait_ge(v32_done, f.count(1))
                    for c in range(CC):
                        for k, (k0, n) in enumerate(chunks):
                            last = nc.tensor.transpose(ps[:, C_T + c, k0:k0 + n], rows[f.parity][0:n, k, c * 128:(c + 1) * 128],
                                                       ident[0:n, 0:n])
                    last.then_inc(cT_mm, 1)
                if t is not None:
                    pe.wait_ge(prob_done, t.count(1, 1))
                    if not t.first(1):
                        pe.wait_ge(out_done, t.count(1))
                    for k in range(KC):
                        last = nc.tensor.transpose(ps[:, P_OUT, k * Q:(k + 1) * Q], prob[:, k * 128:(k + 1) * 128], ident[0:Q, 0:Q])
                    last.then_inc(pT_mm, 1)
                if s is not None:
                    pe.wait_ge(k_done, s.count(1, 1))
                    pe.wait_ge(q_done, s.count(1, 1))
                    if not s.first(1):
                        pe.wait_ge(e32_done, s.count(1))
                    for c in range(CC):
                        last = mm3(nc, ps[0:Q, S_B, 0:KEYS], [u[:, c * Q:(c + 1) * Q] for u in qT],
                                   [u[:, c, :] for u in kT], c == 0, c == CC - 1)
                    last.then_inc(s_mm, 1)
                if f is not None:
                    pe.wait_ge(cT_done, f.count(1, 1))
                    for o in range(CC):
                        for c in range(CC):
                            last = mm3(nc, ps[:, K_0 + o, 0:KEYS], [u[:, c, o * 128:(o + 1) * 128] for u in wk],
                                       [u[:, c, :] for u in cT], c == 0, c == CC - 1)
                    last.then_inc(k_mm, 1)
                    pe.wait_ge(z_done, f.count(1, 1))
                    for c in range(CC):
                        last = nc.tensor.transpose(ps[:, Z_Q, c * Q:(c + 1) * Q], z[:, c * 128:(c + 1) * 128], ident[0:Q, 0:Q])
                    last.then_inc(zT_mm, 1)
                if t is not None:
                    pe.wait_ge(pT_done, t.count(1, 1))
                    pe.wait_ge(v_done, t.count(1, 1))
                    for c in range(CC):
                        for k, (_, n) in enumerate(chunks):
                            last = mm3(nc, ps[:, O_B, c * Q:(c + 1) * Q], [u[0:n, k, c * 128:(c + 1) * 128] for u in v[t.parity]],
                                       [u[0:n, k * Q:(k + 1) * Q] for u in pT], k == 0, k == KC - 1)
                    last.then_inc(o_mm, 1)
                if f is not None:
                    for k, (k0, n) in enumerate(chunks):
                        for c in range(CC):
                            last = mm3(nc, ps[0:n, C_T + k // 2, (k % 2) * D:(k % 2 + 1) * D],
                                       [u[:, c, k0:k0 + n] for u in cT], [u[:, c, :] for u in wv], c == 0, c == CC - 1)
                    last.then_inc(v_mm, 1)
                    pe.wait_ge(zT_done, f.count(1, 1))
                    for o in range(CC):
                        for c in range(CC):
                            last = mm3(nc, ps[:, Z_Q, o * Q:(o + 1) * Q], [u[:, c, o * 128:(o + 1) * 128] for u in wq],
                                       [u[:, c * Q:(c + 1) * Q] for u in zT], c == 0, c == CC - 1)
                    last.then_inc(q_mm, 1)
                if t is not None:
                    pe.wait_ge(o_done, t.count(1, 1))
                    for c in range(CC):
                        last = mm3(nc, ps[0:Q, P_OUT, 0:D], [u[:, c * Q:(c + 1) * Q] for u in oT], [u[:, c, :] for u in wo],
                                   c == 0, c == CC - 1)
                    last.then_inc(out_mm, 1)

            pipeline(pe, NB, step)


def grouped_sigmoid_ffn(nc, x_in, gate_in, routerT, e_bias, packed, x_out):
    T = x_in.shape[0] // 128
    D = x_in.shape[1]
    CC = D // 128
    NR = routerT.shape[2]
    NE = packed.shape[0]
    NG, TOPG, TOP = 8, 4, 8
    PG = NR // NG
    FAR = 3.0e38
    PB = 512 // NR - 1
    while T % PB:
        PB -= 1
    BANKS = T // PB
    with ExitStack() as outer:
        def sb(name, shape, dt=F32, stack=outer):
            return stack.enter_context(nc.sbuf_tensor(name, shape, dt))
        X = sb("g_X", [128, T, D])
        gate = sb("g_gate", [128, 1])
        zT = (sb("g_zT_hi", [128, CC, T * 128], F32R), sb("g_zT_lo", [128, CC, T * 128], F32R))
        coef = sb("g_coef", [128, NE, T])
        ident = sb("g_ident", [128, 128])
        with ExitStack() as st:
            def sem(name):
                return nc.alloc_semaphore(name)
            router_raw = sb("g_router_raw", [128, CC, NR], stack=st)
            router = (sb("g_router_hi", [128, CC, NR], F32R, st), sb("g_router_lo", [128, CC, NR], F32R, st))
            ebias = sb("g_ebias", [128, NR], stack=st)
            score = sb("g_score", [128, T, NR], stack=st)
            biased = sb("g_biased", [128, T, NR], stack=st)
            work = sb("g_work", [128, T, NR], stack=st)
            top1 = sb("g_top1", [128, T, NG], stack=st)
            top2 = sb("g_top2", [128, T, NG], stack=st)
            count = sb("g_count", [128, T, NG], stack=st)
            best = sb("g_best", [128, T, 8], stack=st)
            best_at = sb("g_best_at", [128, T, 8], U32, st)
            at_f = sb("g_at_f", [128, T, 8], stack=st)
            numbers = sb("g_numbers", [128, 8], stack=st)
            total = sb("g_total", [128, T], stack=st)
            logits_ps = st.enter_context(nc.psum_tensor("g_logits_ps", [128, BANKS, 512], F32))
            router_in, bias_in, router_ok, numbers_ok, score_done, own = (
                sem("g_" + n) for n in ("router_in", "bias_in", "router_ok", "numbers_ok", "score_done", "own"))
            sync, gpsimd, scalar, vector, tensor, logits_done, gate_done, NBLK = norm_and_turn(
                nc, "L0_", st, x_in, gate_in, X, gate, zT, ident, router, logits_ps, NR, PB)
            block = st.enter_context(nc.Block())

            @block.sync
            def _(sp):
                sp.dma_start(router_raw[:, :, :], routerT).then_inc(router_in, 16)
                sp.dma_start(ebias[:, :], e_bias.partition_broadcast(128)).then_inc(bias_in, 16)
                sync(sp)

            @block.gpsimd
            def _(pool):
                nc.gpsimd.iota(numbers[:, :], pattern=[[1, 8]], base=0, channel_multiplier=0,
                               allow_small_or_imprecise_dtypes=True).then_inc(numbers_ok, 1)
                gpsimd(pool)

            @block.scalar
            def _(act):
                act.wait_ge(router_in, 16)
                nc.scalar.activation(router[0][:, :, :], router_raw[:, :, :], ACT.Copy).then_inc(router_ok, 1)
                scalar(act)
                act.wait_ge(logits_done, NBLK)
                for b in range(BANKS):
                    last = nc.scalar.activation(score[:, b * PB:(b + 1) * PB, :],
                                                logits_ps[:, b, 0:PB * NR].rearrange("p (t e) -> p t e", e=NR), ACT.Sigmoid)
                last.then_inc(score_done, 1)

            @block.vector
            def _(dve):
                chain = Chain(dve, own)
                ALL = [128, T, NR]
                GROUPS = [128, T * NG, PG]

                def groups(ap):
                    return ap[:, :, :].rearrange("p t (g e) -> p (t g) e", e=PG)

                def flat(ap):
                    return ap[:, :, :].rearrange("p t g -> p (t g)")

                dve.wait_ge(router_ok, 1)
                nc.vector.tensor_tensor(router[1][:, :, :], router_raw[:, :, :], router[0][:, :, :].bitcast(F32), SUB).then_inc(router_ok, 1)
                vector(dve)
                dve.wait_ge(score_done, 1)
                dve.wait_ge(bias_in, 16)
                chain.link(nc.vector.tensor_tensor(biased[:, :, :], score[:, :, :], ebias[:, :].unsqueeze(1).broadcast_to(ALL), ADD))
                chain.link(nc.vector.tensor_reduce(flat(top1), groups(biased), AX.X, ALU.max))
                chain.link(nc.vector.tensor_tensor(groups(work), groups(biased), flat(top1).unsqueeze(2).broadcast_to(GROUPS), ALU.is_equal))
                chain.link(nc.vector.tensor_reduce(flat(count), groups(work), AX.X, ADD))
                chain.link(nc.vector.scalar_tensor_tensor(out=work[:, :, :], in0=work[:, :, :], scalar=-FAR, in1=biased[:, :, :], op0=MUL, op1=ADD))
                chain.link(nc.vector.tensor_reduce(flat(top2), groups(work), AX.X, ALU.max))
                chain.link(nc.vector.tensor_scalar(count[:, :, :], count[:, :, :], 1.5, -FAR, ALU.is_lt, MUL))
                chain.link(nc.vector.tensor_tensor(count[:, :, :], count[:, :, :], top1[:, :, :], ADD))
                chain.link(nc.vector.tensor_tensor(top2[:, :, :], top2[:, :, :], count[:, :, :], ALU.max))
                chain.link(nc.vector.tensor_tensor(top1[:, :, :], top1[:, :, :], top2[:, :, :], ADD))
                for t in range(T):
                    last = nc.vector.max(best[:, t, :], top1[:, t, :])
                chain.link(last)
                for t in range(T):
                    last = nc.vector.max_index(best_at[:, t, :], best[:, t, :], top1[:, t, :])
                chain.link(last)
                chain.link(nc.vector.tensor_copy(at_f[:, :, :], best_at[:, :, :]))
                dve.wait_ge(numbers_ok, 1)
                for k in range(TOPG):
                    dst = count if k == 0 else top2
                    chain.link(nc.vector.tensor_tensor(dst[:, :, :], numbers[:, :].unsqueeze(1).broadcast_to([128, T, NG]),
                                                       at_f[:, :, k:k + 1].broadcast_to([128, T, NG]), ALU.is_equal))
                    if k:
                        chain.link(nc.vector.tensor_tensor(count[:, :, :], count[:, :, :], top2[:, :, :], ADD))
                chain.link(nc.vector.tensor_scalar(top2[:, :, :], count[:, :, :], 0.5, -FAR, ALU.is_lt, MUL))
                chain.link(nc.vector.tensor_tensor(groups(work), groups(biased), flat(count).unsqueeze(2).broadcast_to(GROUPS), MUL))
                chain.link(nc.vector.tensor_tensor(groups(work), groups(work), flat(top2).unsqueeze(2).broadcast_to(GROUPS), ADD))
                for t in range(T):
                    last = nc.vector.max(best[:, t, :], work[:, t, :])
                chain.link(last)
                for t in range(T):
                    last = nc.vector.match_replace(biased[:, t, :], best[:, t, :], work[:, t, :], -1.1 * FAR)
                chain.link(last)
                chain.link(nc.vector.tensor_tensor(work[:, :, :], work[:, :, :], biased[:, :, :], ALU.not_equal))
                chain.link(nc.vector.tensor_tensor(score[:, :, :], score[:, :, :], work[:, :, :], MUL))
                chain.link(nc.vector.tensor_reduce(total[:, :], score[:, :, :], AX.X, ADD))
                chain.link(nc.vector.tensor_scalar(total[:, :], total[:, :], 1e-20, None, ADD))
                chain.link(nc.vector.reciprocal(total[:, :], total[:, :]))
                dve.wait_ge(gate_done, 1)
                chain.link(nc.vector.tensor_scalar(total[:, :], total[:, :], gate[:, 0:1], None, MUL))
                nc.vector.tensor_tensor(coef[:, 0:NR, :], score[:, :, :].rearrange("p t e -> p e t"),
                                        total[:, :].unsqueeze(1).broadcast_to([128, NR, T]), MUL)
                chain.link(nc.vector.memset(coef[:, NR:NE, :], 1.0))
                nc.vector.tensor_scalar(coef[:, NR:NE, :], coef[:, NR:NE, :], gate[:, 0:1], None, MUL)

            @block.tensor
            def _(pe):
                pe.wait_ge(router_ok, 2)
                tensor(pe)

        dense_experts(nc, "L0_", X, zT, coef, packed, x_out)


def build(nc, a, out):
    shape = out.shape
    x1, x2, x3 = (nc.dram_tensor(n, shape, F32).ap() for n in ("x1", "x2", "x3"))

    def flat(ap):
        return ap.rearrange("b q d -> (b q) d")
    p = "L0_xattn_"
    with nc.cleanup_on_exit():
        perceiver_attention(nc, a["x"], a["ctx_1024"], a["g_xattn"][0:1], a[p + "gamma_media"], a[p + "beta_media"],
                            a[p + "gamma_lat"], a[p + "beta_lat"], a[p + "Wq"], a[p + "bq"], a[p + "Wkv"], a[p + "bkv"],
                            a[p + "Wo"], a[p + "bo"], x1)
    with nc.cleanup_on_exit():
        grouped_sigmoid_ffn(nc, flat(x1), a["g_ffn"][0:1], a["L0_ffn_routerT"], a["L0_ffn_e_bias"], a["L0_ffn_packed"],
                            flat(x2))
    p = "L1_xattn_"
    with nc.cleanup_on_exit():
        strided_attention(nc, x2, a["ctx_1024"], a["g_xattn"][1:2], a[p + "WqT"], a[p + "WkT"], a[p + "WvT"], a[p + "WoT"],
                          a[p + "biasT"], a[p + "bo"], a["L1_row_mask"], a["L1_col_mask"], x3)
    with nc.cleanup_on_exit():
        softmax_top2_ffn(nc, flat(x3), a["g_ffn"][1:2], a["L1_ffn_routerT"], a["L1_ffn_packed"], flat(out))


def pack_experts(gate, up, down):
    import numpy as np
    n, d, h = gate.shape

    def rows(w):
        return w.reshape(n, d // 128, 128, h).transpose(0, 2, 1, 3).reshape(n, 128, -1)
    return np.concatenate([rows(gate), rows(up), down], axis=2)


def shared_as_experts(gate, up, down):
    import numpy as np
    d, h = gate.shape
    n = h // 128
    return (gate.reshape(d, n, 128).transpose(1, 0, 2), up.reshape(d, n, 128).transpose(1, 0, 2), down.reshape(n, 128, d))


def by_partition(w):
    r, n = w.shape
    return w.reshape(r // 128, 128, n).transpose(1, 0, 2)


def kernel(**inputs):
    import numpy as np
    import concourse.bacc as bacc
    from concourse.bass_utils import run_bass_kernel_spmd

    given = {name: np.asarray(a) for name, a in inputs.items()}
    arrays = {name: given[name] for name in PLAIN if name in given}
    for layer, names in (("L0_ffn", ("gate_w", "up_w", "down_w", "sh_gate_w", "sh_up_w", "sh_down_w")),
                         ("L1_ffn", ("experts_gate", "experts_up", "experts_down", "shared_gate", "shared_up", "shared_down"))):
        w = [given[f"{layer}_{n}"] for n in names]
        arrays[f"{layer}_packed"] = np.concatenate([pack_experts(*w[:3]), pack_experts(*shared_as_experts(*w[3:]))], axis=0)
    arrays["L0_ffn_routerT"] = by_partition(given["L0_ffn_router_w"].T)
    arrays["L1_ffn_routerT"] = by_partition(given["L1_ffn_router"])
    for m in ("Wq", "Wk", "Wv", "Wo"):
        arrays[f"L1_xattn_{m}T"] = by_partition(given[f"L1_xattn_{m}"].T)
    arrays["L1_xattn_biasT"] = np.concatenate([given[f"L1_xattn_{b}"].reshape(2, 128).T for b in ("bq", "bk", "bv")], axis=1)
    heads, keys, dims = 16, given["ctx_1024"].shape[1] // 16 * 16, given["x"].shape[2]
    dim_head = np.arange(dims) // (dims // heads)
    arrays["L1_row_mask"] = (np.arange(128)[:, None] % heads == dim_head[None, :]).astype(np.float32)
    arrays["L1_col_mask"] = by_partition((dim_head[:, None] == np.arange(keys)[None, :] % heads).astype(np.float32))

    nc = bacc.Bacc("TRN2", target_bir_lowering=False, num_devices=1)
    feed, aps = {}, {}
    for name, a in arrays.items():
        a = np.ascontiguousarray(a)
        feed[f"in_{name}"] = a
        aps[name] = nc.dram_tensor(f"in_{name}", a.shape, mybir.dt.from_np(a.dtype), kind="ExternalInput").ap()
    out = nc.dram_tensor("out_x", given["x"].shape, F32, kind="ExternalOutput").ap()
    build(nc, aps, out)
    r = run_bass_kernel_spmd(nc, [feed], core_ids=[0])
    return r.results[0]["out_x"]


PLAIN = ["x", "ctx_1024", "g_xattn", "g_ffn", "L0_xattn_gamma_media", "L0_xattn_beta_media", "L0_xattn_gamma_lat",
         "L0_xattn_beta_lat", "L0_xattn_Wq", "L0_xattn_bq", "L0_xattn_Wkv", "L0_xattn_bkv", "L0_xattn_Wo", "L0_xattn_bo",
         "L0_ffn_e_bias", "L1_xattn_bq", "L1_xattn_bk", "L1_xattn_bv", "L1_xattn_bo"]
```

```python
import concourse.bass as bass
from concourse import mybir
from contextlib import ExitStack

F32 = mybir.dt.float32
F32R = mybir.dt.float32r
I32 = mybir.dt.int32
U32 = mybir.dt.uint32
ALU = mybir.AluOpType
ACT = mybir.ActivationFunctionType
AX = mybir.AxisListType
LN_EPS = 1e-5
SUB, MUL, ADD = ALU.subtract, ALU.mult, ALU.add


class Batch:

    def __init__(self, i, off):
        self.i, self.off = i, off

    def count(self, per, k=0):
        return self.i * (2 * per) + (self.off * per + k)

    @property
    def parity(self):
        return self.off % 2

    def uses(self, k=0):
        return self.i * 16 + (16 * (self.off // 2 + k))

    def __add__(self, d):
        return Batch(self.i, self.off + d)

    def first(self, n):
        return isinstance(self.i, int) and self.off < n

    def last(self, nb):
        return isinstance(self.i, int) and self.off >= nb


def pipeline(eng, nb, step):
    step(None, None, Batch(0, 0))
    step(Batch(0, 0), None, Batch(0, 1))
    step(Batch(0, 1), Batch(0, 0), Batch(0, 2))
    with eng.Fori(0, (nb - 4) // 2) as i:
        for off in (2, 3):
            step(Batch(i, off), Batch(i, off - 1), Batch(i, off + 1))
    step(Batch(0, nb - 2), Batch(0, nb - 3), Batch(0, nb - 1))
    step(Batch(0, nb - 1), Batch(0, nb - 2), None)
    step(None, Batch(0, nb - 1), None)


def wait_apart(eng, sem, value, passed):
    eng.wait_ge(sem, value)
    eng.sem_inc(passed, 1)


def mm3(nc, out, left, right, start, stop):
    (lh, ll), (rh, rl) = left, right
    nc.tensor.matmul(out, lh, rh, start=start, stop=False)
    nc.tensor.matmul(out, lh, rl, start=False, stop=False)
    return nc.tensor.matmul(out, ll, rh, start=False, stop=stop)


def make_identity(nc, pool, ident, sem):
    nc.gpsimd.memset(ident[:, :], 0.0).then_inc(sem, 1)
    pool.wait_ge(sem, 1)
    nc.gpsimd.affine_select(out=ident[:, :], in_=ident[:, :], compare_op=ALU.not_equal, fill=1.0,
                            base=0, pattern=[[-1, 128]], channel_multiplier=1).then_inc(sem, 1)


def row(ap, parts):
    return ap.partition_broadcast(parts)


def perceiver_attention(nc, x, ctx, g_xattn, gamma_media, beta_media, gamma_lat, beta_lat,
                        Wq, bq, Wkv, bkv, Wo, bo, x1, zeroed):
    NB, Q, D = x.shape
    M = ctx.shape[1]
    DH = 128
    H = Wq.shape[1] // DH
    CC = D // 128
    MC = 3
    MP = M // MC
    KC = MC + 1
    KEYS = Q + M
    KPAD = KEYS + KEYS % 2
    ROWS = H * Q
    R = ROWS // 128
    HG = 2
    GH = H // HG
    GC = GH * Q
    SCALE = float(DH) ** -0.5
    kc_rows = [Q] + [MP] * MC
    kc_col = [0] + [Q + MP * c for c in range(MC)]

    with ExitStack() as outer:
        def sb(name, shape, dt=F32, stack=outer):
            return stack.enter_context(nc.sbuf_tensor(name, shape, dt))

        def split_sb(name, shape, stack=outer):
            return (sb(name + "_hi", shape, F32R, stack), sb(name + "_lo", shape, F32R, stack))

        wq = split_sb("wq", [128, CC, H * DH])
        wkT = split_sb("wkT", [DH, H, D])
        wvo = split_sb("wvo", [128, CC, H, D])
        ident = sb("ident_a", [128, 128])
        gm = sb("gm", [MP, D])
        bm = sb("bm", [MP, D])
        gl = sb("gl", [Q, D])
        bl = sb("bl", [Q, D])
        biasT = sb("biasT", [DH, 2 * H])
        bqT, bvT = biasT[:, 0:H], biasT[:, H:2 * H]
        gate = sb("gate_a", [Q, 1])
        gbo = sb("gbo", [Q, D])
        half = sb("half_a", [128, 4])
        xT = [split_sb(f"xT{p}", [128, CC, KPAD]) for p in range(2)]

        with ExitStack() as st:
            def sem(name):
                return nc.alloc_semaphore(name)
            wq_raw = sb("wq_raw", [128, CC, H * DH], stack=st)
            wkv_raw = sb("wkv_raw", [128, CC, 2 * H * DH], stack=st)
            wo_raw = sb("wo_raw", [DH, H, D], stack=st)
            wvT = split_sb("wvT", [DH, H, D], st)
            wo = split_sb("wo", [DH, H, D], st)
            bv = split_sb("bv", [DH, H, Q], st)
            wkT_ps = st.enter_context(nc.psum_tensor("wkT_ps", [128, 4, 2 * D], F32))
            bvo_ps = st.enter_context(nc.psum_tensor("bvo_ps", [128, 512], F32))
            PAIRS = H // 2
            bias_rows = sb("bias_rows", [2 * H, DH], stack=st)
            biasT_ps = st.enter_context(nc.psum_tensor("biasT_ps", [128, 512], F32))
            wq_in, wkv_in, wo_in, small_in = sem("wq_in"), sem("wkv_in"), sem("wo_in"), sem("small_in")
            ident_ok, turned, hi_ok, lo_ok = sem("ident_ok"), sem("turned"), sem("hi_ok"), sem("lo_ok")
            gate_ok, consts_ok, bvo_mm, bias_ok = sem("gate_ok"), sem("consts_ok"), sem("bvo_mm"), sem("bias_ok")
            N_CONSTS = 2 * len(xT) + 1

            def turned_pair(g):
                dst = (wkT, wvT)[g // PAIRS]
                at = 2 * (g % PAIRS)
                return [w[:, at:at + 2, :].rearrange("p h c -> p (h c)") for w in dst], (SCALE, 1.0)[g // PAIRS]

            def wvo_head(h):
                return [w[:, :, h, :] for w in wvo]

            def head_ps(h):
                return wkT_ps[:, h % 4, :].rearrange("p (c d) -> p c d", c=CC)
            N_PAIRS, N_WO, N_WVO = 2 * PAIRS, 2 * PAIRS + 2, 2 * PAIRS + 3
            block = st.enter_context(nc.Block())

            @block.sync
            def _(sp):
                sp.dma_start(wkv_raw[:, :, :], Wkv.rearrange("(c p) n -> p c n", p=128)).then_inc(wkv_in, 16)
                sp.dma_start(wq_raw[:, :, :], Wq.rearrange("(c p) n -> p c n", p=128)).then_inc(wq_in, 16)
                sp.dma_start(wo_raw[:, :, :], Wo.rearrange("(h p) n -> p h n", p=128)).then_inc(wo_in, 16)

            @block.gpsimd
            def _(pool):
                make_identity(nc, pool, ident, ident_ok)
                nc.gpsimd.memset(half[:, :], -0.5)
                for pair in xT:
                    for part in pair:
                        nc.gpsimd.memset(part[:, :, KEYS:KPAD].bitcast(F32), 0.0).then_inc(consts_ok, 1)
                pool.wait_ge(gate_ok, 1)
                nc.gpsimd.tensor_scalar(gbo[:, :], gbo[:, :], gate[:, 0:1], None, MUL).then_inc(consts_ok, 1)

            @block.scalar
            def _(act):
                small = [(gbo, row(bo, Q)), (gate, row(g_xattn[0:1], Q)), (gm, row(gamma_media, MP)),
                         (bm, row(beta_media, MP)), (gl, row(gamma_lat, Q)), (bl, row(beta_lat, Q)),
                         (bias_rows[0:H, :], bq.rearrange("(h p) -> h p", p=DH)),
                         (bias_rows[H:2 * H, :], bkv[H * DH:].rearrange("(h p) -> h p", p=DH))]
                for dst, src in small:
                    act.dma_start(dst[:, :], src).then_inc(small_in, 16)
                act.wait_ge(small_in, 16 * len(small))
                nc.scalar.activation(gate[:, :], gate[:, :], ACT.Tanh).then_inc(gate_ok, 1)
                for g in range(2 * PAIRS):
                    (hi, _lo), scale = turned_pair(g)
                    act.wait_ge(turned, g + 1)
                    nc.scalar.activation(hi, wkT_ps[:, g % 4, :], ACT.Copy, scale=scale).then_inc(hi_ok, 1)
                act.wait_ge(bias_ok, 1)
                nc.scalar.activation(bv[0][:, :, :], bvT.unsqueeze(2).broadcast_to([DH, H, Q]), ACT.Copy).then_inc(hi_ok, 1)
                for ready, dst, src in ((wo_in, wo, wo_raw), (wq_in, wq, wq_raw)):
                    act.wait_ge(ready, 16)
                    nc.scalar.activation(dst[0][:, :, :], src[:, :, :], ACT.Copy).then_inc(hi_ok, 1)
                for h in range(H):
                    act.wait_ge(turned, N_PAIRS + h + 1)
                    nc.scalar.activation(wvo_head(h)[0], head_ps(h), ACT.Copy).then_inc(hi_ok, 1)

            @block.vector
            def _(dve):
                dve.wait_ge(turned, 1)
                nc.vector.tensor_copy(biasT[:, :], biasT_ps[:, 0:2 * H]).then_inc(bias_ok, 1)
                for g in range(2 * PAIRS):
                    (hi, lo), scale = turned_pair(g)
                    dve.wait_ge(hi_ok, g + 1)
                    nc.vector.scalar_tensor_tensor(out=lo, in0=wkT_ps[:, g % 4, :], scalar=scale, in1=hi.bitcast(F32),
                                                   op0=MUL, op1=SUB).then_inc(lo_ok, 1)
                dve.wait_ge(bias_ok, 1)
                for n, (dst, src) in enumerate(((bv, bvT.unsqueeze(2).broadcast_to([DH, H, Q])), (wo, wo_raw[:, :, :]), (wq, wq_raw[:, :, :]))):
                    dve.wait_ge(hi_ok, N_PAIRS + n + 1)
                    nc.vector.tensor_tensor(dst[1][:, :, :], src, dst[0][:, :, :].bitcast(F32), SUB).then_inc(lo_ok, 1)
                for h in range(H):
                    dve.wait_ge(hi_ok, N_WVO + h + 1)
                    hi, lo = wvo_head(h)
                    nc.vector.tensor_tensor(lo, head_ps(h), hi.bitcast(F32), SUB).then_inc(lo_ok, 1)
                dve.wait_ge(bvo_mm, 1)
                dve.wait_ge(consts_ok, N_CONSTS)
                nc.vector.scalar_tensor_tensor(out=gbo[:, :], in0=bvo_ps[0:Q, 0:D], scalar=gate[:, 0:1], in1=gbo[:, :],
                                               op0=MUL, op1=ADD)

            @block.tensor
            def _(pe):
                pe.wait_ge(ident_ok, 2)
                pe.wait_ge(small_in, 16 * 8)
                nc.tensor.transpose(biasT_ps[:, 0:2 * H], bias_rows[:, :], ident[0:2 * H, 0:2 * H])
                pe.wait_ge(wkv_in, 16)
                for g in range(2 * PAIRS):
                    if g >= 4:
                        pe.wait_ge(lo_ok, g - 3)
                    for k in range(2 * CC):
                        h, c = 2 * g + k // CC, k % CC
                        last = nc.tensor.transpose(wkT_ps[:, g % 4, k * 128:(k + 1) * 128],
                                                   wkv_raw[:, c, h * DH:(h + 1) * DH], ident[:, :])
                    last.then_inc(turned, 1)
                pe.wait_ge(lo_ok, N_WO)
                for h in range(H):
                    last = mm3(nc, bvo_ps[0:Q, 0:D], [w[:, h, :] for w in bv], [w[:, h, :] for w in wo], h == 0, h == H - 1)
                last.then_inc(bvo_mm, 1)
                for h in range(H):
                    if h >= 4:
                        pe.wait_ge(lo_ok, N_WVO + h - 3)
                    for c in range(CC):
                        last = mm3(nc, wkT_ps[:, h % 4, c * D:(c + 1) * D], [w[:, h, c * 128:(c + 1) * 128] for w in wvT],
                                   [w[:, h, :] for w in wo], True, True)
                    last.then_inc(turned, 1)

        with ExitStack() as st:
            def sem(name):
                return nc.alloc_semaphore(name)
            ctx_raw = [sb(f"ctx_raw{p}", [MP, MC, D], stack=st) for p in range(2)]
            x_lat = [sb(f"x_lat{p}", [Q, D], stack=st) for p in range(2)]
            x_res = [sb(f"x_res{p}", [Q, D], stack=st) for p in range(2)]
            zeros = sb("zeros", [128, D], stack=st)
            raw_stats = sb("raw_stats", [128, KC + 1, 6], stack=st)
            mean_var = sb("mean_var", [128, KC + 1, 2], stack=st)
            var_eps = sb("var_eps", [128, KC + 1], stack=st)
            rstd = sb("rstd", [128, KC + 1], stack=st)
            xn32 = sb("xn32", [128, KC, D], stack=st)
            xn = [split_sb(f"xn{p}", [128, KC, D], st) for p in range(2)]
            head32 = sb("head32", [DH, ROWS], stack=st)
            q = split_sb("q", [DH, ROWS], st)
            qk = [split_sb(f"qk{p}", [128, CC, ROWS], st) for p in range(2)]
            probs = [sb(f"probs{n}", [128, KEYS], stack=st) for n in range(2)]
            nmax = sb("nmax", [128, 2], stack=st)
            rowsum = sb("rowsum", [128, 2], stack=st)
            rinv = sb("rinv", [128, 2], stack=st)
            pT = split_sb("pT", [MP, KC, ROWS], st)
            px = split_sb("px", [128, CC, ROWS], st)
            score_ps = st.enter_context(nc.psum_tensor("score_ps", [128, 2, 512], F32))
            turn_ps = st.enter_context(nc.psum_tensor("turn_ps", [128, 2, 512], F32))
            fill_ps = st.enter_context(nc.psum_tensor("fill_ps", [128, 4, 512], F32))

            ctx_in = [sem(f"ctx_in{p}") for p in range(2)]
            lat_in = [sem(f"lat_in{p}") for p in range(2)]
            res_in = [sem(f"res_in{p}") for p in range(2)]
            stored = [sem(f"stored{p}") for p in range(2)]
            bn_raw = sem("bn_raw")
            bn_done = sem("bn_done")
            ln_self = sem("ln_self")
            lat_z, med_z, lat_z2 = sem("lat_z"), sem("med_z"), sem("lat_z2")
            xn_ready = sem("xn_ready")
            xn_hi_done = sem("xn_hi_done")
            xn_lo_done = sem("xn_lo_done")
            xT_mm, xT_hi_done, xT_done = sem("xT_mm"), sem("xT_hi_done"), sem("xT_done")
            q_mm, q32_done, q_hi_done, q_done = (sem(n) for n in ("q_mm", "q32_done", "q_hi_done", "q_done"))
            qk_mm, qk_hi_done, qk_done = sem("qk_mm"), sem("qk_hi_done"), sem("qk_done")
            score_mm, nmax_done, exp_done, rinv_done, probs_done = (
                sem(n) for n in ("score_mm", "nmax_done", "exp_done", "rinv_done", "probs_done"))
            turn_mm, pT_hi_done, pT_done = sem("turn_mm"), sem("pT_hi_done"), sem("pT_done")
            px_mm, px_hi_done, px_done = sem("px_mm"), sem("px_hi_done"), sem("px_done")
            out_mm, xb_done, out_done = sem("out_mm"), sem("xb_done"), sem("out_done")
            zeros_ready, zeros_out = sem("zeros_ready"), sem("zeros_out")
            pool_passed, dve_passed = sem("pool_passed"), sem("dve_passed")
            block = st.enter_context(nc.Block())

            G4 = HG * CC
            PX_BANK, Q_BANK, QK_BANK = (0, 2, 3, 1), (1, 3), (0, 2, 1, 3)

            def f_index(b):
                return bass.ds(b.count(1), 1)

            def tile_no(b, r):
                return (b.off * R + r) % 2

            @block.sync
            def _(sp):
                def load_rows(f):
                    p = f.parity
                    if not f.first(2):
                        sp.wait_ge(xn_ready, f.count(1, -1))
                    sp.dma_start(ctx_raw[p][:, :, :], ctx[f_index(f), :, :].rearrange("a (p c) d -> p (a c) d", c=MC)
                                 ).then_inc(ctx_in[p], 16)
                    sp.dma_start(x_lat[p][:, :], x[f_index(f), :, :].rearrange("a q d -> q (a d)")).then_inc(lat_in[p], 16)

                def step(s, t, f):
                    if f is not None:
                        load_rows(f)
                    if s is not None:
                        share = zeroed.shape[0] // NB
                        sp.dma_start(zeroed.rearrange("(b k p) d -> b p k d", b=NB, p=128)[f_index(s), :, :, :].rearrange("a p k d -> p (a k) d"),
                                     zeros[:, :].unsqueeze(1).broadcast_to([128, share // 128, D])).then_inc(zeros_out, 16)
                        if not s.first(2):
                            sp.wait_ge(stored[s.parity], s.uses())
                        sp.dma_start(x_res[s.parity][:, :], x[f_index(s), :, :].rearrange("a q d -> q (a d)")
                                     ).then_inc(res_in[s.parity], 16)

                sp.wait_ge(zeros_ready, 1)
                pipeline(sp, NB, step)
                sp.wait_ge(zeros_out, 16 * NB)

            @block.gpsimd
            def _(pool):
                def norm(f):
                    p = f.parity
                    zlat, zmed = x_lat[p], ctx_raw[p]
                    wait_apart(pool, bn_done, f.count(2, 1), pool_passed)
                    nc.gpsimd.tensor_scalar(var_eps[:, 0:KC], mean_var[:, 0:KC, 1], LN_EPS, None, ADD).then_inc(ln_self, 1)
                    pool.wait_ge(ln_self, f.count(6, 1))
                    nc.gpsimd.tensor_tensor(rstd[:, 0:KC], var_eps[:, 0:KC], half[:, 0:KC], ALU.pow).then_inc(ln_self, 1)
                    wait_apart(pool, bn_done, f.count(2, 2), pool_passed)
                    nc.gpsimd.tensor_scalar(var_eps[0:Q, KC:KC + 1], mean_var[0:Q, KC, 1:2], LN_EPS, None, ADD).then_inc(ln_self, 1)
                    pool.wait_ge(ln_self, f.count(6, 3))
                    nc.gpsimd.tensor_tensor(rstd[0:Q, KC:KC + 1], var_eps[0:Q, KC:KC + 1], half[0:Q, 0:1], ALU.pow).then_inc(ln_self, 1)
                    pool.wait_ge(med_z, f.count(1, 1))
                    nc.gpsimd.tensor_tensor(zmed[:, :, :], zmed[:, :, :], gm[:, :].unsqueeze(1).broadcast_to([MP, MC, D]),
                                            MUL).then_inc(ln_self, 1)
                    pool.wait_ge(ln_self, f.count(6, 5))
                    if not f.first(1):
                        pool.wait_ge(xT_mm, f.count(CC))
                        pool.wait_ge(xn_hi_done, f.count(1))
                    nc.gpsimd.tensor_tensor(xn32[0:MP, 1:KC, :], zmed[:, :, :], bm[:, :].unsqueeze(1).broadcast_to([MP, MC, D]),
                                            ADD)
                    pool.wait_ge(lat_z2, f.count(1, 1))
                    nc.gpsimd.tensor_tensor(zlat[:, :], zlat[:, :], gl[:, :], MUL).then_inc(ln_self, 1)
                    pool.wait_ge(ln_self, f.count(6, 6))
                    nc.gpsimd.tensor_tensor(xn32[0:Q, 0, :], zlat[:, :], bl[:, :], ADD).then_inc(xn_ready, 1)

                def step(s, t, f):
                    if t is not None:
                        pool.wait_ge(res_in[t.parity], t.uses(1))
                        nc.gpsimd.tensor_tensor(x_res[t.parity][:, :], x_res[t.parity][:, :], gbo[:, :], ADD).then_inc(xb_done, 1)
                    if f is not None:
                        norm(f)
                    if f is not None:
                        for g in range(HG):
                            cols = slice(g * GC, (g + 1) * GC)
                            pool.wait_ge(q_hi_done, f.count(HG, g + 1))
                            nc.gpsimd.tensor_tensor(q[1][:, cols], head32[:, cols], q[0][:, cols].bitcast(F32), SUB
                                                    ).then_inc(q_done, 1)
                        p = f.parity
                        pool.wait_ge(xn_hi_done, f.count(1, 1))
                        pool.wait_ge(xn_ready, f.count(1, 1))
                        nc.gpsimd.tensor_tensor(xn[p][1][0:Q, 0, :], xn32[0:Q, 0, :], xn[p][0][0:Q, 0, :].bitcast(F32), SUB)
                        nc.gpsimd.tensor_tensor(xn[p][1][0:MP, 1:KC, :], xn32[0:MP, 1:KC, :],
                                                xn[p][0][0:MP, 1:KC, :].bitcast(F32), SUB).then_inc(xn_lo_done, 1)

                pipeline(pool, NB, step)

            @block.scalar
            def _(act):
                def copy(dst, src, done):
                    nc.scalar.activation(dst, src, ACT.Copy).then_inc(done, 1)

                def exps(s, r):
                    n = tile_no(s, r)
                    act.wait_ge(nmax_done, s.count(R, r + 1))
                    if not (s.first(1) and r < 2):
                        act.wait_ge(turn_mm, s.count(R, r - 1))
                    nc.scalar.activation(probs[n][:, :], score_ps[:, n, 0:KEYS], ACT.Exp, bias=nmax[:, n:n + 1],
                                         accum_out=rowsum[:, n:n + 1]).then_inc(exp_done, 1)

                def pT_hi(b, r):
                    n = tile_no(b, r)
                    act.wait_ge(turn_mm, b.count(R, r + 1))
                    if not b.first(1):
                        act.wait_ge(px_mm, b.count(G4, -2 if r < 3 else 0))
                    copy(pT[0][:, :, r * 128:(r + 1) * 128], turn_ps[0:MP, n, :].rearrange("p (k r) -> p k r", k=KC), pT_hi_done)

                def px_hi(t, k):
                    g, c = divmod(k, CC)
                    act.wait_ge(px_mm, t.count(G4, k + 1))
                    if not t.first(1) and k == 0:
                        act.wait_ge(out_mm, t.count(1))
                    copy(px[0][:, c, g * GC:(g + 1) * GC], fill_ps[:, PX_BANK[k], 0:GC], px_hi_done)

                def step(s, t, f):
                    for r in range(R):
                        if s is not None:
                            exps(s, r)
                        if r < 2 and t is not None:
                            for k in (2 * r, 2 * r + 1):
                                px_hi(t, k)
                        if r == 2 and f is not None:
                            p = f.parity
                            act.wait_ge(xn_ready, f.count(1, 1))
                            if not f.first(2):
                                act.wait_ge(px_mm, f.count(G4, -G4))
                            nc.scalar.activation(xn[p][0][0:Q, 0, :], xn32[0:Q, 0, :], ACT.Copy)
                            copy(xn[p][0][0:MP, 1:KC, :], xn32[0:MP, 1:KC, :], xn_hi_done)
                        if r == 2 and f is not None:
                            for c in range(CC):
                                act.wait_ge(xT_mm, f.count(CC, c + 1))
                                if not f.first(2) and c == 0:
                                    act.wait_ge(score_mm, f.count(R, -R))
                                copy(xT[f.parity][0][:, c, 0:KEYS], fill_ps[:, 2 + c, 0:KEYS], xT_hi_done)
                        if r in (3, 4) and f is not None:
                            g = r - 3
                            cols = slice(g * GC, (g + 1) * GC)
                            act.wait_ge(q32_done, f.count(HG, g + 1))
                            if not f.first(1) and g == 0:
                                act.wait_ge(qk_mm, f.count(G4))
                            copy(q[0][:, cols], head32[:, cols], q_hi_done)
                        if r in (5, 6) and f is not None:
                            for k in range(CC * (r - 5), CC * (r - 4)):
                                g, c = divmod(k, CC)
                                act.wait_ge(qk_mm, f.count(G4, k + 1))
                                copy(qk[f.parity][0][:, c, g * GC:(g + 1) * GC], fill_ps[:, QK_BANK[k], 0:GC], qk_hi_done)
                        if r == 4 and t is not None:
                            act.wait_ge(out_done, t.count(1, 1))
                            act.dma_start(x1[f_index(t), :, :].rearrange("a q d -> q (a d)"), x_res[t.parity][:, :]).then_inc(stored[t.parity], 16)
                        if r == 0 and t is not None:
                            pT_hi(t, R - 1)
                        if r >= 1 and s is not None:
                            pT_hi(s, r - 1)

                pipeline(act, NB, step)
                for p in range(2):
                    act.wait_ge(stored[p], 16 * (NB // 2))

            @block.vector
            def _(dve):
                def norm_stats(f, again):
                    p = f.parity
                    if not again:
                        dve.wait_ge(lat_in[p], f.uses(1))
                        nc.vector.bn_stats(raw_stats[0:Q, 0, :], x_lat[p][:, :])
                        dve.wait_ge(ctx_in[p], f.uses(1))
                        for c in range(MC):
                            last = nc.vector.bn_stats(raw_stats[0:MP, c + 1, :], ctx_raw[p][:, c, :])
                    else:
                        dve.wait_ge(ln_self, f.count(6, 2))
                        nc.vector.tensor_scalar(x_lat[p][:, :], x_lat[p][:, :], mean_var[0:Q, 0, 0:1], rstd[0:Q, 0:1],
                                                SUB, MUL).then_inc(lat_z, 1)
                        for c in range(MC):
                            last = nc.vector.tensor_scalar(ctx_raw[p][:, c, :], ctx_raw[p][:, c, :], mean_var[0:MP, c + 1, 0:1],
                                                           rstd[0:MP, c + 1:c + 2], SUB, MUL)
                        last.then_inc(med_z, 1)
                        wait_apart(dve, lat_z, f.count(1, 1), dve_passed)
                        last = nc.vector.bn_stats(raw_stats[0:Q, KC, :], x_lat[p][:, :])
                    last.then_inc(bn_raw, 1)
                    wait_apart(dve, bn_raw, f.count(2, 1 + again), dve_passed)
                    if again:
                        nc.vector.bn_aggr(mean_var[0:Q, KC, :], raw_stats[0:Q, KC, :]).then_inc(bn_done, 1)
                        return
                    if not f.first(1):
                        wait_apart(dve, xn_ready, f.count(1), dve_passed)
                    nc.vector.bn_aggr(mean_var[0:Q, 0, :], raw_stats[0:Q, 0, :])
                    for c in range(MC):
                        last = nc.vector.bn_aggr(mean_var[0:MP, c + 1, :], raw_stats[0:MP, c + 1, :])
                    last.then_inc(bn_done, 1)

                def row_max(s, r):
                    n = tile_no(s, r)
                    dve.wait_ge(score_mm, s.count(R, r + 1))
                    nc.vector.tensor_reduce(nmax[:, n:n + 1], score_ps[:, n, 0:KEYS], AX.X, ALU.max, negate=True
                                            ).then_inc(nmax_done, 1)

                def norm_probs(b, r):
                    n = tile_no(b, r)
                    dve.wait_ge(exp_done, b.count(R, r + 1))
                    nc.vector.reciprocal(rinv[:, n:n + 1], rowsum[:, n:n + 1]).then_inc(rinv_done, 1)
                    dve.wait_ge(rinv_done, b.count(R, r + 1))
                    nc.vector.tensor_scalar(probs[n][:, :], probs[n][:, :], rinv[:, n:n + 1], None, MUL).then_inc(probs_done, 1)

                def low(dst, src, ready, value, done):
                    dve.wait_ge(ready, value)
                    nc.vector.tensor_tensor(dst[1], src, dst[0].bitcast(F32), SUB).then_inc(done, 1)

                def pT_lo(b, r):
                    n = tile_no(b, r)
                    low([w[:, :, r * 128:(r + 1) * 128] for w in pT], turn_ps[0:MP, n, :].rearrange("p (k r) -> p k r", k=KC),
                        pT_hi_done, b.count(R, r + 1), pT_done)

                def bias_add(dst, g, src, bias, ready, value, done):
                    dve.wait_ge(ready, value)
                    nc.vector.tensor_tensor(dst[:, g * GC:(g + 1) * GC].rearrange("p (h q) -> p h q", h=GH),
                                            src.rearrange("p (h q) -> p h q", h=GH),
                                            bias[:, g * GH:(g + 1) * GH].unsqueeze(2).broadcast_to([DH, GH, Q]),
                                            ADD).then_inc(done, 1)

                def step(s, t, f):
                    for r in range(R):
                        if r == 0 and t is not None:
                            norm_probs(t, R - 1)
                        if r >= 1 and s is not None:
                            norm_probs(s, r - 1)
                        if s is not None:
                            row_max(s, r)
                        if r < 2 and f is not None:
                            norm_stats(f, r)
                        if r < 2 and t is not None:
                            for k in (2 * r, 2 * r + 1):
                                g, c = divmod(k, CC)
                                low([w[:, c, g * GC:(g + 1) * GC] for w in px], fill_ps[:, PX_BANK[k], 0:GC],
                                    px_hi_done, t.count(G4, k + 1), px_done)
                        if r == 2 and f is not None:
                            p = f.parity
                            dve.wait_ge(ln_self, f.count(6, 4))
                            nc.vector.tensor_scalar(x_lat[p][:, :], x_lat[p][:, :], mean_var[0:Q, KC, 0:1], rstd[0:Q, KC:KC + 1],
                                                    SUB, MUL).then_inc(lat_z2, 1)
                        if r == 2 and f is not None:
                            for c in range(CC):
                                low([w[:, c, 0:KEYS] for w in xT[f.parity]], fill_ps[:, 2 + c, 0:KEYS],
                                    xT_hi_done, f.count(CC, c + 1), xT_done)
                        if r == 3 and t is not None:
                            p = t.parity
                            dve.wait_ge(out_mm, t.count(1, 1))
                            dve.wait_ge(xb_done, t.count(1, 1))
                            nc.vector.scalar_tensor_tensor(out=x_res[p][:, :], in0=fill_ps[0:Q, 0, 0:D], scalar=gate[:, 0:1],
                                                           in1=x_res[p][:, :], op0=MUL, op1=ADD).then_inc(out_done, 1)
                        if r in (3, 4) and f is not None:
                            g = r - 3
                            if not f.first(1) and g == 0:
                                dve.wait_ge(q_done, f.count(HG))
                            bias_add(head32, g, fill_ps[:, Q_BANK[g], 0:GC], bqT, q_mm, f.count(HG, g + 1), q32_done)
                        if r in (5, 6) and f is not None:
                            for k in range(CC * (r - 5), CC * (r - 4)):
                                g, c = divmod(k, CC)
                                low([w[:, c, g * GC:(g + 1) * GC] for w in qk[f.parity]], fill_ps[:, QK_BANK[k], 0:GC],
                                    qk_hi_done, f.count(G4, k + 1), qk_done)
                        if r == 0 and t is not None:
                            pT_lo(t, R - 1)
                        if r >= 1 and s is not None:
                            pT_lo(s, r - 1)

                nc.vector.memset(zeros[:, :], 0.0).then_inc(zeros_ready, 1)
                nc.vector.memset(mean_var[:, :, :], 1.0)
                pipeline(dve, NB, step)

            @block.tensor
            def _(pe):
                def scores(s, r):
                    n, p = tile_no(s, r), s.parity
                    if r == 0:
                        pe.wait_ge(qk_done, s.count(G4, G4))
                    if not (s.first(1) and r < 2):
                        pe.wait_ge(exp_done, s.count(R, r - 1))
                    for c in range(CC):
                        last = mm3(nc, score_ps[:, n, 0:KPAD], [w[:, c, r * 128:(r + 1) * 128] for w in qk[p]],
                                   [w[:, c, :] for w in xT[p]], c == 0, c == CC - 1)
                    last.then_inc(score_mm, 1)

                def turn(b, r):
                    n = tile_no(b, r)
                    pe.wait_ge(probs_done, b.count(R, r + 1))
                    if not (b.first(1) and r < 2):
                        pe.wait_ge(pT_done, b.count(R, r - 1))
                    for k in range(KC):
                        last = nc.tensor.transpose(turn_ps[0:MP, n, k * 128:(k + 1) * 128],
                                                   probs[n][:, kc_col[k]:kc_col[k] + MP], ident[:, :])
                    last.then_inc(turn_mm, 1)

                def weighted_rows(t, k):
                    g, c = divmod(k, CC)
                    pe.wait_ge(pT_done, t.count(R, 4 if g == 0 else R))
                    pe.wait_ge(xn_lo_done, t.count(1, 1))
                    for kc, n in enumerate(kc_rows):
                        last = mm3(nc, fill_ps[:, PX_BANK[k], 0:GC], [w[0:n, kc, c * 128:(c + 1) * 128] for w in xn[t.parity]],
                                   [w[0:n, kc, g * GC:(g + 1) * GC] for w in pT], kc == 0, kc == KC - 1)
                    last.then_inc(px_mm, 1)

                def head_mm(dst, w, rhs, g, done):
                    for h in range(g * GH, (g + 1) * GH):
                        for c in range(CC):
                            last = mm3(nc, dst[:, (h - g * GH) * Q:(h - g * GH + 1) * Q],
                                       [u[:, c, h * DH:(h + 1) * DH] for u in w], rhs(h, c), c == 0, c == CC - 1)
                    last.then_inc(done, 1)

                def step(s, t, f):
                    for r in range(R):
                        if r == 0 and t is not None:
                            if s is not None:
                                pe.wait_ge(qk_done, s.count(G4, CC))
                            weighted_rows(t, 0)
                        if s is not None:
                            scores(s, r)
                        if r < 2 and t is not None:
                            for k in ((1,), (2, 3))[r]:
                                weighted_rows(t, k)
                        if r == 2 and t is not None:
                            for h in range(H):
                                if h % GH == 0:
                                    pe.wait_ge(px_done, t.count(G4, CC * (h // GH + 1)))
                                for c in range(CC):
                                    last = mm3(nc, fill_ps[0:Q, 0, 0:D], [w[:, c, h * Q:(h + 1) * Q] for w in px],
                                               [w[:, c, h, :] for w in wvo], (h, c) == (0, 0), (h, c) == (H - 1, CC - 1))
                            last.then_inc(out_mm, 1)
                        if r == 2 and f is not None:
                            pe.wait_ge(xn_ready, f.count(1, 1))
                            for c in range(CC):
                                for kc, n in enumerate(kc_rows):
                                    last = nc.tensor.transpose(fill_ps[:, 2 + c, kc_col[kc]:kc_col[kc] + n],
                                                               xn32[0:n, kc, c * 128:(c + 1) * 128], ident[0:n, 0:n])
                                last.then_inc(xT_mm, 1)
                        if r == 3 and f is not None:
                            pe.wait_ge(xT_done, f.count(CC, CC))
                            head_mm(fill_ps[:, Q_BANK[0], :], wq, lambda h, c: [w[:, c, 0:Q] for w in xT[f.parity]], 0, q_mm)
                        if r == 4 and f is not None:
                            head_mm(fill_ps[:, Q_BANK[1], :], wq, lambda h, c: [w[:, c, 0:Q] for w in xT[f.parity]], 1, q_mm)
                        if r in (5, 6) and f is not None:
                            for k in range(CC * (r - 5), CC * (r - 4)):
                                g, c = divmod(k, CC)
                                if k == 0 and t is not None:
                                    pe.wait_ge(out_done, t.count(1, 1))
                                pe.wait_ge(q_done, f.count(HG, g + 1))
                                for h in range(g * GH, (g + 1) * GH):
                                    last = mm3(nc, fill_ps[:, QK_BANK[k], (h - g * GH) * Q:(h - g * GH + 1) * Q],
                                               [w[:, h, c * 128:(c + 1) * 128] for w in wkT],
                                               [w[:, h * Q:(h + 1) * Q] for w in q], True, True)
                                last.then_inc(qk_mm, 1)
                        if r == 0 and t is not None:
                            turn(t, R - 1)
                        if r >= 1 and s is not None:
                            turn(s, r - 1)

                pipeline(pe, NB, step)


class Chain:

    def __init__(self, eng, sem):
        self.eng, self.sem, self.n = eng, sem, 0

    def link(self, instruction):
        self.n += 1
        instruction.then_inc(self.sem, 1)
        self.eng.wait_ge(self.sem, self.n)


def norm_and_turn(nc, tag, st, x_in, gate_in, X, gate, zT, ident, router, logits_ps, n_logits, per_bank,
                  z_all=None):
    P, T, D = X.shape
    CC = D // 128
    B = 4
    NBLK = T // B

    def sem(name):
        return nc.alloc_semaphore(tag + name)

    def sb(name, shape, dt=F32):
        return st.enter_context(nc.sbuf_tensor(tag + name, shape, dt))
    raw_stats = sb("f_raw_stats", [P, B, 6])
    mean_var = sb("f_mean_var", [P, T, 2])
    var_eps = sb("f_var_eps", [P, T])
    rstd = sb("f_rstd", [P, T])
    half = sb("f_half", [P, B])
    z = [sb(f"f_z{i}", [P, B, D]) for i in range(2)] if z_all is None else None

    def z_of(b, k):
        return z[b % 2][:, k, :] if z else z_all[:, B * b + k, :]

    turn_ps = st.enter_context(nc.psum_tensor(tag + "f_turn_ps", [P, CC, B * P], F32))
    across_ps = st.enter_context(nc.psum_tensor(tag + "f_across_ps", [P, B * P], F32))
    across = [sb(f"f_across{i}", [n_logits, B * P]) for i in range(2)]
    across_mm, across_done = sem("across_mm"), sem("across_done")
    x_loaded = [sem(f"x_loaded{i}") for i in range(NBLK)]
    gate_loaded, ident_ok, gate_done = sem("gate_loaded"), sem("ident_ok_f"), sem("gate_done")
    stats_done, mv_done, eps_done, rstd_done = (sem(n) for n in ("stats_done", "mv_done", "eps_done", "rstd_done"))
    z_done, turned, hi_done, lo_done, logits_done = (sem(n) for n in ("z_done", "turned", "z_hi_done", "z_lo_done", "logits_done"))
    x_v = x_in.rearrange("(t p) d -> p t d", p=P)

    def sync(sp):
        for b in range(NBLK):
            sp.dma_start(X[:, B * b:B * (b + 1), :], x_v[:, B * b:B * (b + 1), :]).then_inc(x_loaded[b], 16)

    def gpsimd(pool):
        make_identity(nc, pool, ident, ident_ok)
        nc.gpsimd.memset(half[:, :], -0.5).then_inc(ident_ok, 1)
        pool.wait_ge(ident_ok, 3)
        for b in range(NBLK):
            tiles = slice(B * b, B * (b + 1))
            pool.wait_ge(mv_done, b + 1)
            nc.gpsimd.tensor_scalar(var_eps[:, tiles], mean_var[:, tiles, 1], LN_EPS, None, ADD).then_inc(eps_done, 1)
            pool.wait_ge(eps_done, b + 1)
            nc.gpsimd.tensor_tensor(rstd[:, tiles], var_eps[:, tiles], half[:, :], ALU.pow).then_inc(rstd_done, 1)

    def scalar(act):
        act.dma_start(gate[:, :], gate_in.partition_broadcast(P)).then_inc(gate_loaded, 16)
        act.wait_ge(gate_loaded, 16)
        nc.scalar.activation(gate[:, :], gate[:, :], ACT.Tanh).then_inc(gate_done, 1)

        def logits_out(b):
            act.wait_ge(across_mm, b + 1)
            if b >= 2:
                act.wait_ge(logits_done, b - 1)
            nc.scalar.activation(across[b % 2][:, :], across_ps[0:n_logits, :], ACT.Copy).then_inc(across_done, 1)

        for b in range(NBLK):
            for c in range(CC):
                act.wait_ge(turned, CC * b + c + 1)
                nc.scalar.activation(zT[0][:, c, b * B * P:(b + 1) * B * P], turn_ps[:, c, :], ACT.Copy).then_inc(hi_done, 1)
            if b >= 1:
                logits_out(b - 1)
        logits_out(NBLK - 1)

    def vector(dve):
        def stats(b):
            dve.wait_ge(x_loaded[b], 16)
            for k in range(B):
                last = nc.vector.bn_stats(raw_stats[:, k, :], X[:, B * b + k, :])
            last.then_inc(stats_done, 1)
            dve.wait_ge(stats_done, b + 1)
            for k in range(B):
                last = nc.vector.bn_aggr(mean_var[:, B * b + k, :], raw_stats[:, k, :])
            last.then_inc(mv_done, 1)

        def scaled(b):
            dve.wait_ge(rstd_done, b + 1)
            if b >= 2:
                dve.wait_ge(turned, CC * (b - 1))
            for k in range(B):
                t = B * b + k
                last = nc.vector.tensor_scalar(z_of(b, k), X[:, t, :], mean_var[:, t, 0:1], rstd[:, t:t + 1], SUB, MUL)
            last.then_inc(z_done, 1)

        def low(b):
            for c in range(CC):
                dve.wait_ge(hi_done, CC * b + c + 1)
                cols = slice(b * B * P, (b + 1) * B * P)
                nc.vector.tensor_tensor(zT[1][:, c, cols], turn_ps[:, c, :], zT[0][:, c, cols].bitcast(F32), SUB).then_inc(lo_done, 1)

        stats(0)
        for b in range(NBLK):
            if b + 1 < NBLK:
                dve.wait_ge(mv_done, b + 1)
                stats(b + 1)
            scaled(b)
            if b >= 1:
                low(b - 1)
        low(NBLK - 1)

    def tensor(pe):
        pe.wait_ge(ident_ok, 2)

        def turn(b):
            pe.wait_ge(z_done, b + 1)
            for c in range(CC):
                if b >= 1:
                    pe.wait_ge(lo_done, CC * (b - 1) + c + 1)
                for k in range(B):
                    last = nc.tensor.transpose(turn_ps[:, c, k * P:(k + 1) * P], z_of(b, k)[:, c * 128:(c + 1) * 128], ident[:, :])
                last.then_inc(turned, 1)

        def logits(b):
            pe.wait_ge(lo_done, CC * (b + 1))
            for c in range(CC):
                last = mm3(nc, across_ps[0:n_logits, :], [w[:, c, :] for w in router],
                           [w[:, c, b * B * P:(b + 1) * B * P] for w in zT], c == 0, c == CC - 1)
            last.then_inc(across_mm, 1)

        def logits_turned(b):
            pe.wait_ge(across_done, b + 1)
            for k in range(B):
                bank, at = divmod(B * b + k, per_bank)
                last = nc.tensor.transpose(logits_ps[:, bank, at * n_logits:(at + 1) * n_logits],
                                           across[b % 2][:, k * P:(k + 1) * P], ident[0:n_logits, 0:n_logits])
            last.then_inc(logits_done, 1)

        turn(0)
        for b in range(1, NBLK + 1):
            if b < NBLK:
                turn(b)
            if b >= 2:
                logits_turned(b - 2)
            logits(b - 1)
        logits_turned(NBLK - 1)

    return sync, gpsimd, scalar, vector, tensor, logits_done, gate_done, NBLK


def dense_experts(nc, tag, X, zT, coef, packed, x_out, pool_work=None, dve_work=None, sp_early=None, sp_work=None,
                  sp_late=None):
    P, T, D = X.shape
    CC = D // 128
    NE = packed.shape[0]
    B = 4
    NBLK = T // B
    WIDTH = packed.shape[2]
    UP, DOWN = CC * 128, 2 * CC * 128
    assert NE % 2 == 0 and NE >= 4

    with ExitStack() as st:
        def sem(name):
            return nc.alloc_semaphore(tag + name)

        def sb(name, shape, dt=F32):
            return st.enter_context(nc.sbuf_tensor(tag + name, shape, dt))
        w_raw = [sb(f"w_raw{p}", [P, WIDTH]) for p in range(2)]
        w = [(sb(f"w_hi{p}", [P, WIDTH], F32R), sb(f"w_lo{p}", [P, WIDTH], F32R)) for p in range(2)]
        weight = [sb(f"weight{p}", [P, T]) for p in range(2)]
        gated = [sb(f"gated{n}", [P, B * P]) for n in range(2)]
        h32 = [sb(f"h32_{n}", [P, B * P]) for n in range(2)]
        h = [(sb(f"h_hi{n}", [P, B * P], F32R), sb(f"h_lo{n}", [P, B * P], F32R)) for n in range(2)]
        gate_ps = st.enter_context(nc.psum_tensor(tag + "gate_ps", [P, 2, 512], F32))
        up_ps = st.enter_context(nc.psum_tensor(tag + "up_ps", [P, 2, 512], F32))
        down_ps = st.enter_context(nc.psum_tensor(tag + "down_ps", [P, 2, B * D], F32))
        w_in = [sem(f"w_in{p}") for p in range(2)]
        w_hi_done, w_lo_done, weight_done = sem("w_hi_done"), sem("w_lo_done"), sem("weight_done")
        gate_mm, up_mm, down_mm = sem("gate_mm"), sem("up_mm"), sem("down_mm")
        gated_done, h32_done, h_hi_done, h_done, added = (sem(n) for n in ("gated_done", "h32_done", "h_hi_done", "h_done", "added"))
        x_stored = sem("x_stored")
        block = st.enter_context(nc.Block())

        def experts(eng, one, after=None):
            for e in range(2):
                one(Batch(0, e))
            if NE > 4:
                with eng.Fori(0, (NE - 4) // 2) as i:
                    for off in (2, 3):
                        one(Batch(i, off))
            for e in range(NE - 2, NE):
                one(Batch(0, e))
            if after:
                after()

        def odd(e, j):
            return (e.off * NBLK + j) % 2

        def early(e, j, n):
            return isinstance(e.i, int) and e.off * NBLK + j < n

        @block.sync
        def _(sp):
            def one(e):
                p = e.parity
                if not e.first(2):
                    sp.wait_ge(w_lo_done, e.count(1, -1))
                sp.dma_start(w_raw[p][:, :], packed[bass.ds(e.count(1), 1), :, :].rearrange("a p n -> p (a n)")).then_inc(w_in[p], 16)
                if sp_early and e.first(2) and e.off == 1:
                    sp_early(sp)
            experts(sp, one)
            if sp_work:
                sp_work(sp)
            out_v = x_out.rearrange("(t p) d -> p t d", p=P)
            for j in range(NBLK):
                sp.wait_ge(added, (NE - 1) * NBLK + j + 1)
                sp.dma_start(out_v[:, B * j:B * (j + 1), :], X[:, B * j:B * (j + 1), :]).then_inc(x_stored, 16)
            sp.wait_ge(x_stored, 16 * NBLK)
            if sp_late:
                sp_late(sp)

        def splits_next(e, j):
            return j == 2 and not e.last(NE - 1)

        def split_weights(eng, e):
            p = e.parity
            eng.wait_ge(w_hi_done, e.count(1, 1))
            eng.tensor_tensor(w[p][1][:, :], w_raw[p][:, :], w[p][0][:, :].bitcast(F32), SUB).then_inc(w_lo_done, 1)

        def split_h(eng, e, j):
            n = odd(e, j)
            eng.wait_ge(h_hi_done, e.count(NBLK, j + 1))
            eng.tensor_tensor(h[n][1][:, :], h32[n][:, :], h[n][0][:, :].bitcast(F32), SUB).then_inc(h_done, 1)

        @block.gpsimd
        def _(pool):
            if pool_work:
                pool_work(pool)
                return

            def one(e):
                if e.first(1):
                    split_weights(nc.gpsimd, e)
                for j in range(NBLK):
                    split_h(nc.gpsimd, e, j)
                    if splits_next(e, j):
                        split_weights(nc.gpsimd, e + 1)
            experts(pool, one)

        @block.scalar
        def _(act):
            def high_weights(e):
                p = e.parity
                act.wait_ge(w_in[p], e.uses(1))
                if not e.first(2):
                    act.wait_ge(down_mm, e.count(NBLK, -NBLK))
                nc.scalar.activation(w[p][0][:, :], w_raw[p][:, :], ACT.Copy).then_inc(w_hi_done, 1)

            def one(e):
                if e.first(1):
                    high_weights(e)
                for j in range(NBLK):
                    n = odd(e, j)
                    act.wait_ge(gate_mm, e.count(NBLK, j + 1))
                    if not early(e, j, 2):
                        act.wait_ge(h32_done, e.count(NBLK, j - 1))
                    nc.scalar.activation(gated[n][:, :], gate_ps[:, n, :], ACT.Silu).then_inc(gated_done, 1)
                    act.wait_ge(h32_done, e.count(NBLK, j + 1))
                    if not early(e, j, 2):
                        act.wait_ge(down_mm, e.count(NBLK, j - 1))
                    nc.scalar.activation(h[n][0][:, :], h32[n][:, :], ACT.Copy).then_inc(h_hi_done, 1)
                    if splits_next(e, j):
                        high_weights(e + 1)
            experts(act, one)

        @block.vector
        def _(dve):
            def add(e, j):
                n = odd(e, j)
                dve.wait_ge(down_mm, e.count(NBLK, j + 1))
                if j == 0:
                    dve.wait_ge(weight_done, e.count(1, 1))
                if not early(e, j, NBLK):
                    dve.wait_ge(added, e.count(NBLK, j + 1 - NBLK))
                for k in range(B):
                    t = B * j + k
                    last = nc.vector.scalar_tensor_tensor(out=X[:, t, :], in0=down_ps[:, n, k * D:(k + 1) * D],
                                                          scalar=weight[e.parity][:, t:t + 1], in1=X[:, t, :],
                                                          op0=MUL, op1=ADD)
                last.then_inc(added, 1)

            def one(e):
                nc.vector.tensor_copy(weight[e.parity][:, :], coef[:, bass.ds(e.count(1), 1), :].rearrange("p a t -> p (a t)")).then_inc(weight_done, 1)
                if pool_work and e.first(1):
                    split_weights(nc.vector, e)
                for j in range(NBLK):
                    n = odd(e, j)
                    dve.wait_ge(gated_done, e.count(NBLK, j + 1))
                    dve.wait_ge(up_mm, e.count(NBLK, j + 1))
                    if not early(e, j, 2):
                        dve.wait_ge(h_done, e.count(NBLK, j - 1))
                    nc.vector.tensor_tensor(h32[n][:, :], gated[n][:, :], up_ps[:, n, :], MUL).then_inc(h32_done, 1)
                    if pool_work:
                        split_h(nc.vector, e, j)
                    if j:
                        add(e, j - 1)
                    elif not early(e, j, 1):
                        add(e + -1, NBLK - 1)
                    if pool_work and splits_next(e, j):
                        split_weights(nc.vector, e + 1)
            experts(dve, one, lambda: add(Batch(0, NE - 1), NBLK - 1))
            if dve_work:
                dve_work(dve)

        @block.tensor
        def _(pe):
            def down(e, j):
                n, p = odd(e, j), e.parity
                pe.wait_ge(h_done, e.count(NBLK, j + 1))
                if not early(e, j, 2):
                    pe.wait_ge(added, e.count(NBLK, j - 1))
                for k in range(B):
                    last = mm3(nc, down_ps[:, n, k * D:(k + 1) * D], [u[:, k * P:(k + 1) * P] for u in h[n]],
                               [u[:, DOWN:DOWN + D] for u in w[p]], True, True)
                last.then_inc(down_mm, 1)

            def one(e):
                p = e.parity
                for j in range(NBLK):
                    n = odd(e, j)
                    if j == 0:
                        pe.wait_ge(w_lo_done, e.count(1, 1))
                    if not early(e, j, 2):
                        pe.wait_ge(h32_done, e.count(NBLK, j - 1))
                    for ps, at, done in ((gate_ps, 0, gate_mm), (up_ps, UP, up_mm)):
                        for c in range(CC):
                            last = mm3(nc, ps[:, n, :], [u[:, at + c * 128:at + (c + 1) * 128] for u in w[p]],
                                       [u[:, c, j * B * P:(j + 1) * B * P] for u in zT], c == 0, c == CC - 1)
                        last.then_inc(done, 1)
                    if j:
                        down(e, j - 1)
                    elif not early(e, j, 1):
                        down(e + -1, NBLK - 1)
            experts(pe, one, lambda: down(Batch(0, NE - 1), NBLK - 1))


def softmax_top2_ffn(nc, x_in, gate_in, routerT, packed, x_out):
    T = x_in.shape[0] // 128
    D = x_in.shape[1]
    CC = D // 128
    NR = routerT.shape[2]
    NE = packed.shape[0]
    TOP = 2
    with ExitStack() as outer:
        def sb(name, shape, dt=F32, stack=outer):
            return stack.enter_context(nc.sbuf_tensor(name, shape, dt))
        X = sb("X", [128, T, D])
        gate = sb("gate", [128, 1])
        zT = (sb("zT_hi", [128, CC, T * 128], F32R), sb("zT_lo", [128, CC, T * 128], F32R))
        coef = sb("coef", [128, NE, T])
        ident = sb("ident_f", [128, 128])
        with ExitStack() as st:
            def sem(name):
                return nc.alloc_semaphore(name)
            router_raw = sb("router_raw", [128, CC, NR], stack=st)
            router = (sb("router_hi", [128, CC, NR], F32R, st), sb("router_lo", [128, CC, NR], F32R, st))
            prob = sb("prob", [128, T, NR], stack=st)
            best = sb("best", [128, T, 8], stack=st)
            best_at = sb("best_at", [128, T, 8], U32, st)
            at_f = sb("at_f", [128, T, 8], stack=st)
            numbers = sb("numbers", [128, NR], stack=st)
            hit = sb("hit", [128, T, NR], stack=st)
            total = sb("total", [128, T], stack=st)
            peak = sb("peak", [128, T], stack=st)
            logits_ps = st.enter_context(nc.psum_tensor("logits_ps", [128, 1, 512], F32))
            router_in, router_ok, numbers_ok, shifted, exp_done, own = (
                sem(n) for n in ("router_in", "router_ok", "numbers_ok", "shifted", "exp_done_r", "own"))
            sync, gpsimd, scalar, vector, tensor, logits_done, gate_done, NBLK = norm_and_turn(
                nc, "L1_", st, x_in, gate_in, X, gate, zT, ident, router, logits_ps, NR, T)
            block = st.enter_context(nc.Block())

            @block.sync
            def _(sp):
                sp.dma_start(router_raw[:, :, :], routerT).then_inc(router_in, 16)
                sync(sp)

            @block.gpsimd
            def _(pool):
                nc.gpsimd.iota(numbers[:, :], pattern=[[1, NR]], base=0, channel_multiplier=0,
                               allow_small_or_imprecise_dtypes=True).then_inc(numbers_ok, 1)
                gpsimd(pool)

            @block.scalar
            def _(act):
                act.wait_ge(router_in, 16)
                nc.scalar.activation(router[0][:, :, :], router_raw[:, :, :], ACT.Copy).then_inc(router_ok, 1)
                scalar(act)
                act.wait_ge(shifted, 1)
                nc.scalar.activation(prob[:, :, :], prob[:, :, :], ACT.Exp).then_inc(exp_done, 1)

            @block.vector
            def _(dve):
                chain = Chain(dve, own)
                dve.wait_ge(router_ok, 1)
                nc.vector.tensor_tensor(router[1][:, :, :], router_raw[:, :, :], router[0][:, :, :].bitcast(F32), SUB).then_inc(router_ok, 1)
                vector(dve)
                dve.wait_ge(logits_done, NBLK)
                logits = logits_ps[:, 0, 0:T * NR].rearrange("p (t e) -> p t e", e=NR)
                chain.link(nc.vector.tensor_reduce(peak[:, :], logits, AX.X, ALU.max))
                nc.vector.tensor_tensor(prob[:, :, :], logits, peak[:, :].unsqueeze(2).broadcast_to([128, T, NR]), SUB).then_inc(shifted, 1)
                dve.wait_ge(exp_done, 1)
                chain.link(nc.vector.tensor_reduce(total[:, :], prob[:, :, :], AX.X, ADD))
                chain.link(nc.vector.reciprocal(total[:, :], total[:, :]))
                chain.link(nc.vector.tensor_tensor(prob[:, :, :], prob[:, :, :], total[:, :].unsqueeze(2).broadcast_to([128, T, NR]), MUL))
                for t in range(T):
                    last = nc.vector.max(best[:, t, :], prob[:, t, :])
                chain.link(last)
                for t in range(T):
                    last = nc.vector.max_index(best_at[:, t, :], best[:, t, :], prob[:, t, :])
                chain.link(last)
                chain.link(nc.vector.tensor_copy(at_f[:, :, :], best_at[:, :, :]))
                dve.wait_ge(numbers_ok, 1)
                dve.wait_ge(gate_done, 1)
                for k in range(TOP):
                    chain.link(nc.vector.tensor_tensor(hit[:, :, :], numbers[:, :].unsqueeze(1).broadcast_to([128, T, NR]),
                                                       at_f[:, :, k:k + 1].broadcast_to([128, T, NR]), ALU.is_equal))
                    dst = prob if k == 0 else hit
                    chain.link(nc.vector.tensor_tensor(dst[:, :, :], hit[:, :, :], best[:, :, k:k + 1].broadcast_to([128, T, NR]), MUL))
                chain.link(nc.vector.tensor_tensor(prob[:, :, :], prob[:, :, :], hit[:, :, :], ADD))
                nc.vector.tensor_scalar(coef[:, 0:NR, :], prob[:, :, :].rearrange("p t e -> p e t"), gate[:, 0:1], None, MUL)
                chain.link(nc.vector.memset(coef[:, NR:NE, :], 1.0))
                nc.vector.tensor_scalar(coef[:, NR:NE, :], coef[:, NR:NE, :], gate[:, 0:1], None, MUL)

            @block.tensor
            def _(pe):
                pe.wait_ge(router_ok, 2)
                tensor(pe)

        dense_experts(nc, "L1_", X, zT, coef, packed, x_out)


def pipeline_ahead(eng, nb, step):
    step(None, None, None, Batch(0, 0))
    for s in range(-1, 2):
        step(*(Batch(0, s + k) if s + k >= 0 else None for k in (0, -1, 1, 2)))
    with eng.Fori(0, (nb - 4) // 2) as i:
        for off in (2, 3):
            step(Batch(i, off), Batch(i, off - 1), Batch(i, off + 1), Batch(i, off + 2))
    for s in range(nb - 2, nb + 1):
        step(*(Batch(0, s + k) if s + k < nb else None for k in (0, -1, 1, 2)))


def strided_attention(nc, x, ys, slots, weights, ctx, gate_in, WqT, WkT, WvT, WoT, biasT, bo, row_mask, col_mask, x_out):
    NB, Q, D = x.shape
    H = 16
    DH = D // H
    TOP = slots.shape[2]
    PER = ctx.shape[1] // H
    KEYS = PER * H
    CC = D // 128
    chunks = [(k, min(128, KEYS - k)) for k in range(0, KEYS, 128)]
    KC = len(chunks)
    SCALE = float(DH) ** -0.5
    C_T, Z_Q, K_0, S_B, P_OUT, O_B = 0, 2, 3, 5, 6, 7

    with ExitStack() as st:
        def sb(name, shape, dt=F32):
            return st.enter_context(nc.sbuf_tensor(name, shape, dt))

        def split_sb(name, shape):
            return (sb(name + "_hi", shape, F32R), sb(name + "_lo", shape, F32R))

        def sem(name):
            return nc.alloc_semaphore(name)

        raw = sb("c_w_raw", [128, 4, CC * D])
        w = split_sb("c_w", [128, 4, CC * D])
        wq, wk, wv, wo = ([part[:, n, :].rearrange("p (c o) -> p c o", c=CC) for part in w] for n in range(4))
        bias = sb("c_bias", [128, 3 * CC])
        bo_row = sb("c_bo", [Q, D])
        gate = sb("c_gate", [Q, 1])
        rmask = sb("c_row_mask", [128, D])
        cmask = sb("c_col_mask", [128, CC, KEYS])
        ident = sb("c_ident", [128, 128])
        half = sb("c_half", [Q, 1])
        rows = [sb(f"c_rows{p}", [128, KC, D]) for p in range(2)]
        x_in = [sb(f"c_x_in{p}", [Q, D]) for p in range(2)]
        x_res = [sb(f"c_x_res{p}", [Q, D]) for p in range(2)]
        slot_now = [sb(f"c_slot{p}", [Q, TOP], U32) for p in range(2)]
        weight_now = [sb(f"c_weight{p}", [Q, TOP]) for p in range(2)]
        got = [[sb(f"c_got{p}_{k}", [Q, D]) for k in range(TOP)] for p in range(2)]
        stats = sb("c_stats", [Q, 6])
        mv = sb("c_mv", [Q, 2])
        var_eps = sb("c_var_eps", [Q, 1])
        rstd = sb("c_rstd", [Q, 1])
        z = sb("c_z", [Q, D])
        cT = split_sb("c_cT", [128, CC, KEYS])
        zT = split_sb("c_zT", [128, CC * Q])
        k32 = sb("c_k32", [128, CC, KEYS])
        kT = split_sb("c_kT", [128, CC, KEYS])
        qT = split_sb("c_qT", [128, CC * Q])
        v32 = sb("c_v32", [128, KC, D])
        v = [split_sb(f"c_v{p}", [128, KC, D]) for p in range(2)]
        peak = sb("c_peak", [Q, H])
        e32 = sb("c_e32", [Q, KEYS])
        total = sb("c_total", [Q, H])
        inv = sb("c_inv", [Q, H])
        prob = sb("c_prob", [Q, KC * 128])
        pT = split_sb("c_pT", [128, KC * Q])
        oT = split_sb("c_oT", [128, CC * Q])
        ps = st.enter_context(nc.psum_tensor("c_ps", [128, 8, 512], F32))

        w_in, small_in, ident_ok, gate_ok, w_hi_ok, w_lo_ok, bo_ok = (
            sem(n) for n in ("c_w_in", "c_small_in", "c_ident_ok", "c_gate_ok", "c_w_hi_ok", "c_w_lo_ok", "c_bo_ok"))
        rows_in, x_in_in, slot_in, weight_in, stored = (
            [sem(f"c_{n}{p}") for p in range(2)] for n in ("rows_in", "x_in_in", "slot_in", "weight_in", "stored"))
        arrived = [[sem(f"c_arrived{p}_{k}") for k in range(TOP)] for p in range(2)]
        added = sem("c_added")
        stats_done, mv_done, eps_done, rstd_done, z_done = (sem("c_" + n) for n in ("stats_done", "mv_done", "eps_done", "rstd_done", "z_done"))
        cT_mm, cT_hi_done, cT_done = (sem("c_" + n) for n in ("cT_mm", "cT_hi_done", "cT_done"))
        zT_mm, zT_hi_done, zT_done = (sem("c_" + n) for n in ("zT_mm", "zT_hi_done", "zT_done"))
        k_mm, k32_done, k_hi_done, k_done = (sem("c_" + n) for n in ("k_mm", "k32_done", "k_hi_done", "k_done"))
        q_mm, q_hi_done, q_done = (sem("c_" + n) for n in ("q_mm", "q_hi_done", "q_done"))
        v_mm, v32_done, v_hi_done, v_done = (sem("c_" + n) for n in ("v_mm", "v32_done", "v_hi_done", "v_done"))
        s_mm, peak_done, e32_done, exp_done, total_done, inv_done, prob_done = (
            sem("c_" + n) for n in ("s_mm", "peak_done", "e32_done", "exp_done", "total_done", "inv_done", "prob_done"))
        pT_mm, pT_hi_done, pT_done = (sem("c_" + n) for n in ("pT_mm", "pT_hi_done", "pT_done"))
        o_mm, o_hi_done, o_done = (sem("c_" + n) for n in ("o_mm", "o_hi_done", "o_done"))
        out_mm, xb_done, out_done = (sem("c_" + n) for n in ("out_mm", "xb_done", "out_done"))
        pool_passed, dve_passed = sem("c_pool_passed"), sem("c_dve_passed")
        block = st.enter_context(nc.Block())

        def at(b):
            return bass.ds(b.count(1), 1)

        def heads(ap):
            return ap.rearrange("q (m h) -> q h m", h=H)

        @block.sync
        def _(sp):
            for n, m in enumerate((WqT, WkT, WvT, WoT)):
                sp.dma_start(raw[:, n, :], m.rearrange("p c o -> p (c o)")).then_inc(w_in, 16)

            def step(s, t, f, g):
                if g is not None:
                    p = g.parity
                    if not g.first(2):
                        sp.wait_ge(cT_mm, g.count(1, -1))
                    whole = KEYS // 128
                    sp.dma_start(rows[p][:, 0:whole, :], ctx[at(g), 0:whole * 128, :].rearrange("a (k p) d -> p (a k) d", p=128)
                                 ).then_inc(rows_in[p], 16)
                    sp.dma_start(rows[p][0:KEYS - whole * 128, whole, :], ctx[at(g), whole * 128:KEYS, :].rearrange("a p d -> p (a d)")
                                 ).then_inc(rows_in[p], 16)
                    for dst, src, done in ((slot_now, slots, slot_in), (weight_now, weights, weight_in), (x_in, x, x_in_in)):
                        if dst is slot_now and not g.first(2):
                            sp.wait_ge(added, g.count(TOP, -TOP))
                        if dst is x_in and not g.first(2):
                            sp.wait_ge(xb_done, g.count(1, -1))
                        sp.dma_start(dst[p][:, :], src[at(g), :, :].rearrange("a q d -> q (a d)")).then_inc(done[p], 16)

            pipeline_ahead(sp, NB, step)

        @block.gpsimd
        def _(pool):
            make_identity(nc, pool, ident, ident_ok)
            nc.gpsimd.memset(half[:, :], -0.5).then_inc(ident_ok, 1)
            pool.wait_ge(gate_ok, 1)
            nc.gpsimd.tensor_scalar(bo_row[:, :], bo_row[:, :], gate[:, 0:1], None, MUL).then_inc(bo_ok, 1)
            pool.wait_ge(bo_ok, 1)
            pool.wait_ge(ident_ok, 3)

            def low(dst, src, ready, b, done):
                pool.wait_ge(ready, b.count(1, 1))
                nc.gpsimd.tensor_tensor(dst[1], src, dst[0].bitcast(F32), SUB).then_inc(done, 1)

            def gather(g, start, stop):
                if g is not None:
                    p = g.parity
                    for k in range(start, stop):
                        nc.gpsimd.indirect_dma_start(out=got[p][k][:, :], out_offset=None, in_=ys,
                                                     in_offset=bass.IndirectOffsetOnAxis(ap=slot_now[p][:, k:k + 1], axis=0)
                                                     ).then_inc(arrived[p][k], 16)

            def step(s, t, f, g):
                if g is not None:
                    wait_apart(pool, slot_in[g.parity], g.uses(1), pool_passed)
                gather(g, 0, 2)
                if f is not None:
                    wait_apart(pool, mv_done, f.count(1, 1), pool_passed)
                    nc.gpsimd.tensor_scalar(var_eps[:, :], mv[:, 1:2], LN_EPS, None, ADD).then_inc(eps_done, 1)
                    pool.wait_ge(eps_done, f.count(1, 1))
                    nc.gpsimd.tensor_tensor(rstd[:, :], var_eps[:, :], half[:, :], ALU.pow).then_inc(rstd_done, 1)
                if s is not None:
                    if not s.first(2):
                        pool.wait_ge(stored[s.parity], s.uses())
                    pool.wait_ge(added, s.count(TOP, TOP))
                    nc.gpsimd.tensor_tensor(x_res[s.parity][:, :], x_in[s.parity][:, :], bo_row[:, :], ADD).then_inc(xb_done, 1)
                gather(g, 2, 4)
                if f is not None:
                    low([u[:, :, :] for u in kT], k32[:, :, :], k_hi_done, f, k_done)
                gather(g, 4, TOP)
                if f is not None:
                    last = KC - 1
                    n = chunks[last][1]
                    hi, lo = v[f.parity]
                    pool.wait_ge(v_hi_done, f.count(1, 1))
                    nc.gpsimd.tensor_tensor(lo[:, 0:last, :], v32[:, 0:last, :], hi[:, 0:last, :].bitcast(F32), SUB)
                    nc.gpsimd.tensor_tensor(lo[0:n, last, :], v32[0:n, last, :], hi[0:n, last, :].bitcast(F32), SUB).then_inc(v_done, 1)

            pipeline_ahead(pool, NB, step)

        @block.scalar
        def _(act):
            small = [(gate, gate_in.partition_broadcast(Q)), (bo_row, bo.partition_broadcast(Q)),
                     (bias, biasT), (rmask, row_mask), (cmask, col_mask)]
            for dst, src in small:
                act.dma_start(dst[:], src).then_inc(small_in, 16)
            act.wait_ge(small_in, 16 * len(small))
            nc.scalar.activation(gate[:, :], gate[:, :], ACT.Tanh).then_inc(gate_ok, 1)
            act.wait_ge(w_in, 64)
            nc.scalar.activation(w[0][:, :, :], raw[:, :, :], ACT.Copy).then_inc(w_hi_ok, 1)

            def high(dst, src, ready, b, done):
                act.wait_ge(ready, b.count(1, 1))
                nc.scalar.activation(dst[0], src, ACT.Copy).then_inc(done, 1)

            def high_biased(pair, bank, c, b):
                cols = slice(c * Q, (c + 1) * Q)
                return nc.scalar.activation(pair[0][:, cols], ps[:, bank, cols], ACT.Identity, bias=bias[:, b:b + 1])

            def step(s, t, f, g):
                if f is not None:
                    high([u[:, :, :] for u in cT], ps[:, C_T:C_T + CC, 0:KEYS], cT_mm, f, cT_hi_done)
                if t is not None:
                    high([u[:, :] for u in pT], ps[:, P_OUT, 0:KC * Q], pT_mm, t, pT_hi_done)
                if s is not None:
                    act.wait_ge(e32_done, s.count(1, 1))
                    nc.scalar.activation(e32[:, :], e32[:, :], ACT.Exp, scale=SCALE).then_inc(exp_done, 1)
                if t is not None:
                    if not t.first(1):
                        act.wait_ge(out_mm, t.count(1))
                    act.wait_ge(o_mm, t.count(1, 1))
                    for c in range(CC):
                        last = high_biased(oT, O_B, c, 2 * CC + c)
                    last.then_inc(o_hi_done, 1)
                if f is not None:
                    if not f.first(1):
                        act.wait_ge(s_mm, f.count(1))
                    high([u[:, :] for u in zT], ps[:, Z_Q, 0:CC * Q], zT_mm, f, zT_hi_done)
                    high([u[:, :, :] for u in kT], k32[:, :, :], k32_done, f, k_hi_done)
                if f is not None:
                    last = KC - 1
                    n = chunks[last][1]
                    hi = v[f.parity][0]
                    act.wait_ge(q_mm, f.count(1, 1))
                    for c in range(CC):
                        last_q = high_biased(qT, Z_Q, c, c)
                    last_q.then_inc(q_hi_done, 1)
                    if not f.first(2):
                        act.wait_ge(o_mm, f.count(1, -1))
                    act.wait_ge(v32_done, f.count(1, 1))
                    nc.scalar.activation(hi[:, 0:last, :], v32[:, 0:last, :], ACT.Copy)
                    nc.scalar.activation(hi[0:n, last, :], v32[0:n, last, :], ACT.Copy).then_inc(v_hi_done, 1)
                if t is not None:
                    act.wait_ge(out_done, t.count(1, 1))
                    act.dma_start(x_out[at(t), :, :].rearrange("a q d -> q (a d)"), x_res[t.parity][:, :]).then_inc(stored[t.parity], 16)

            pipeline_ahead(act, NB, step)
            for p in range(2):
                act.wait_ge(stored[p], 16 * (NB // 2))

        @block.vector
        def _(dve):
            nc.vector.memset(prob[:, :], 0.0)
            dve.wait_ge(w_hi_ok, 1)
            nc.vector.tensor_tensor(w[1][:, :, :], raw[:, :, :], w[0][:, :, :].bitcast(F32), SUB).then_inc(w_lo_ok, 1)
            dve.wait_ge(small_in, 16 * 5)

            def low(dst, src, ready, b, done):
                dve.wait_ge(ready, b.count(1, 1))
                nc.vector.tensor_tensor(dst[1], src, dst[0].bitcast(F32), SUB).then_inc(done, 1)

            def add(g, start, stop):
                if g is None:
                    return
                p = g.parity
                for k in range(start, stop):
                    if k == 0:
                        dve.wait_ge(x_in_in[p], g.uses(1))
                        dve.wait_ge(weight_in[p], g.uses(1))
                    else:
                        dve.wait_ge(added, g.count(TOP, k))
                    dve.wait_ge(arrived[p][k], g.uses(1))
                    nc.vector.scalar_tensor_tensor(out=x_in[p][:, :], in0=got[p][k][:, :], scalar=weight_now[p][:, k:k + 1],
                                                   in1=x_in[p][:, :], op0=MUL, op1=ADD).then_inc(added, 1)

            def low_biased(pair, bank, first_bias, ready, b, done):
                dve.wait_ge(ready, b.count(1, 1))
                for c in range(CC):
                    cols = slice(c * Q, (c + 1) * Q)
                    last = nc.vector.scalar_tensor_tensor(out=pair[1][:, cols], in0=ps[:, bank, cols],
                                                          scalar=bias[:, first_bias + c:first_bias + c + 1],
                                                          in1=pair[0][:, cols].bitcast(F32), op0=ADD, op1=SUB)
                last.then_inc(done, 1)

            def step(s, t, f, g):
                if f is not None:
                    low([u[:, :, :] for u in cT], ps[:, C_T:C_T + CC, 0:KEYS], cT_hi_done, f, cT_done)
                if t is not None:
                    low([u[:, :] for u in pT], ps[:, P_OUT, 0:KC * Q], pT_hi_done, t, pT_done)
                add(f, 3, TOP)
                if f is not None:
                    dve.wait_ge(added, f.count(TOP, TOP))
                    nc.vector.bn_stats(stats[:, :], x_in[f.parity][:, :]).then_inc(stats_done, 1)
                    if not f.first(1):
                        wait_apart(dve, z_done, f.count(1), dve_passed)
                    wait_apart(dve, stats_done, f.count(1, 1), dve_passed)
                    nc.vector.bn_aggr(mv[:, :], stats[:, :]).then_inc(mv_done, 1)
                if f is not None:
                    dve.wait_ge(k_mm, f.count(1, 1))
                    if not f.first(1):
                        dve.wait_ge(k_done, f.count(1))
                    for c in range(CC):
                        last = nc.vector.scalar_tensor_tensor(out=k32[:, c, :], in0=ps[:, K_0 + c, 0:KEYS],
                                                              scalar=bias[:, CC + c:CC + c + 1], in1=cmask[:, c, :],
                                                              op0=ADD, op1=MUL)
                    last.then_inc(k32_done, 1)
                if f is not None:
                    if not f.first(1):
                        dve.wait_ge(zT_mm, f.count(1))
                    dve.wait_ge(rstd_done, f.count(1, 1))
                    nc.vector.tensor_scalar(z[:, :], x_in[f.parity][:, :], mv[:, 0:1], rstd[:, 0:1], SUB, MUL).then_inc(z_done, 1)
                if s is not None:
                    dve.wait_ge(s_mm, s.count(1, 1))
                    nc.vector.tensor_reduce(peak[:, :], heads(ps[0:Q, S_B, 0:KEYS]), AX.X, ALU.max).then_inc(peak_done, 1)
                    dve.wait_ge(peak_done, s.count(1, 1))
                    nc.vector.tensor_tensor(heads(e32[:, :]), heads(ps[0:Q, S_B, 0:KEYS]),
                                            peak[:, :].unsqueeze(2).broadcast_to([Q, H, PER]), SUB).then_inc(e32_done, 1)
                if t is not None:
                    low_biased(oT, O_B, 2 * CC, o_hi_done, t, o_done)
                if f is not None:
                    low([u[:, :] for u in zT], ps[:, Z_Q, 0:CC * Q], zT_hi_done, f, zT_done)
                add(g, 0, 1)
                if s is not None:
                    dve.wait_ge(exp_done, s.count(1, 1))
                    nc.vector.tensor_reduce(total[:, :], heads(e32[:, :]), AX.X, ADD).then_inc(total_done, 1)
                    dve.wait_ge(total_done, s.count(1, 1))
                    nc.vector.reciprocal(inv[:, :], total[:, :]).then_inc(inv_done, 1)
                    dve.wait_ge(inv_done, s.count(1, 1))
                    nc.vector.tensor_tensor(heads(prob[:, 0:KEYS]), heads(e32[:, :]),
                                            inv[:, :].unsqueeze(2).broadcast_to([Q, H, PER]), MUL).then_inc(prob_done, 1)
                if f is not None:
                    dve.wait_ge(v_mm, f.count(1, 1))
                    if not f.first(1):
                        dve.wait_ge(v_done, f.count(1))
                    for k, (_, n) in enumerate(chunks):
                        src = ps[0:n, C_T + k // 2, (k % 2) * D:(k % 2 + 1) * D]
                        last = nc.vector.tensor_tensor(v32[0:n, k, :], src, rmask[0:n, :], MUL)
                    last.then_inc(v32_done, 1)
                if t is not None:
                    dve.wait_ge(out_mm, t.count(1, 1))
                    dve.wait_ge(xb_done, t.count(1, 1))
                    nc.vector.scalar_tensor_tensor(out=x_res[t.parity][:, :], in0=ps[0:Q, P_OUT, 0:D], scalar=gate[:, 0:1],
                                                   in1=x_res[t.parity][:, :], op0=MUL, op1=ADD).then_inc(out_done, 1)
                if f is not None:
                    low_biased(qT, Z_Q, 0, q_hi_done, f, q_done)
                add(g, 1, 3)

            pipeline_ahead(dve, NB, step)

        @block.tensor
        def _(pe):
            pe.wait_ge(ident_ok, 2)
            pe.wait_ge(w_lo_ok, 1)

            def step(s, t, f, g):
                if f is not None:
                    pe.wait_ge(rows_in[f.parity], f.uses(1) + f.uses(1))
                    if not f.first(1):
                        pe.wait_ge(v32_done, f.count(1))
                    for c in range(CC):
                        for k, (k0, n) in enumerate(chunks):
                            last = nc.tensor.transpose(ps[:, C_T + c, k0:k0 + n], rows[f.parity][0:n, k, c * 128:(c + 1) * 128],
                                                       ident[0:n, 0:n])
                    last.then_inc(cT_mm, 1)
                if t is not None:
                    pe.wait_ge(prob_done, t.count(1, 1))
                    if not t.first(1):
                        pe.wait_ge(out_done, t.count(1))
                    for k in range(KC):
                        last = nc.tensor.transpose(ps[:, P_OUT, k * Q:(k + 1) * Q], prob[:, k * 128:(k + 1) * 128], ident[0:Q, 0:Q])
                    last.then_inc(pT_mm, 1)
                if s is not None:
                    pe.wait_ge(k_done, s.count(1, 1))
                    pe.wait_ge(q_done, s.count(1, 1))
                    if not s.first(1):
                        pe.wait_ge(e32_done, s.count(1))
                    for c in range(CC):
                        last = mm3(nc, ps[0:Q, S_B, 0:KEYS], [u[:, c * Q:(c + 1) * Q] for u in qT],
                                   [u[:, c, :] for u in kT], c == 0, c == CC - 1)
                    last.then_inc(s_mm, 1)
                if f is not None:
                    pe.wait_ge(cT_done, f.count(1, 1))
                    for o in range(CC):
                        for c in range(CC):
                            last = mm3(nc, ps[:, K_0 + o, 0:KEYS], [u[:, c, o * 128:(o + 1) * 128] for u in wk],
                                       [u[:, c, :] for u in cT], c == 0, c == CC - 1)
                    last.then_inc(k_mm, 1)
                if t is not None:
                    pe.wait_ge(pT_done, t.count(1, 1))
                    pe.wait_ge(v_done, t.count(1, 1))
                    for c in range(CC):
                        for k, (_, n) in enumerate(chunks):
                            last = mm3(nc, ps[:, O_B, c * Q:(c + 1) * Q], [u[0:n, k, c * 128:(c + 1) * 128] for u in v[t.parity]],
                                       [u[0:n, k * Q:(k + 1) * Q] for u in pT], k == 0, k == KC - 1)
                    last.then_inc(o_mm, 1)
                if f is not None:
                    pe.wait_ge(z_done, f.count(1, 1))
                    for c in range(CC):
                        last = nc.tensor.transpose(ps[:, Z_Q, c * Q:(c + 1) * Q], z[:, c * 128:(c + 1) * 128], ident[0:Q, 0:Q])
                    last.then_inc(zT_mm, 1)
                if f is not None:
                    for k, (k0, n) in enumerate(chunks):
                        for c in range(CC):
                            last = mm3(nc, ps[0:n, C_T + k // 2, (k % 2) * D:(k % 2 + 1) * D],
                                       [u[:, c, k0:k0 + n] for u in cT], [u[:, c, :] for u in wv], c == 0, c == CC - 1)
                    last.then_inc(v_mm, 1)
                    pe.wait_ge(zT_done, f.count(1, 1))
                    for o in range(CC):
                        for c in range(CC):
                            last = mm3(nc, ps[:, Z_Q, o * Q:(o + 1) * Q], [u[:, c, o * 128:(o + 1) * 128] for u in wq],
                                       [u[:, c * Q:(c + 1) * Q] for u in zT], c == 0, c == CC - 1)
                    last.then_inc(q_mm, 1)
                if t is not None:
                    pe.wait_ge(o_done, t.count(1, 1))
                    for c in range(CC):
                        last = mm3(nc, ps[0:Q, P_OUT, 0:D], [u[:, c * Q:(c + 1) * Q] for u in oT], [u[:, c, :] for u in wo],
                                   c == 0, c == CC - 1)
                    last.then_inc(out_mm, 1)

            pipeline_ahead(pe, NB, step)


SLOTS = 256


def slot_tiles(rows, top, experts):
    return (rows * top + experts * (SLOTS - 1)) // SLOTS


class Step(Batch):

    def count(self, per, k=0):
        return self.i * (4 * per) + (self.off * per + k)

    def uses(self, buffers, k=0):
        return self.i * (16 * 4 // buffers) + 16 * (self.off // buffers + k)

    def __add__(self, d):
        return Step(self.i, self.off + d)


def routed_experts(nc, xs, ys, tile_expert, packed, NT, ident):
    D = xs.shape[1]
    CC = D // 128
    S = SLOTS // 128
    WIDTH = packed.shape[2]
    UP, DOWN = CC * 128, 2 * CC * 128
    xs_v = xs.rearrange("(n s p) d -> n p s d", s=S, p=128)
    ys_v = ys.rearrange("(n s p) d -> n p s d", s=S, p=128)
    with ExitStack() as st:
        def sb(name, shape, dt=F32):
            return st.enter_context(nc.sbuf_tensor("r_" + name, shape, dt))

        def sem(name):
            return nc.alloc_semaphore("r_" + name)
        rows = [sb(f"rows{n}", [128, S, D]) for n in range(4)]
        w_raw = [sb(f"w_raw{n}", [128, WIDTH]) for n in range(4)]
        w = [(sb(f"w_hi{n}", [128, WIDTH], F32R), sb(f"w_lo{n}", [128, WIDTH], F32R)) for n in range(4)]
        xT = [(sb(f"xT_hi{n}", [128, CC * SLOTS], F32R), sb(f"xT_lo{n}", [128, CC * SLOTS], F32R)) for n in range(2)]
        gated = [sb(f"gated{n}", [128, SLOTS]) for n in range(2)]
        h32 = [sb(f"h32_{n}", [128, SLOTS]) for n in range(2)]
        h = [(sb(f"h_hi{n}", [128, SLOTS], F32R), sb(f"h_lo{n}", [128, SLOTS], F32R)) for n in range(2)]
        y = [sb(f"y{n}", [128, S, D]) for n in range(4)]
        turn_ps = st.enter_context(nc.psum_tensor("r_turn_ps", [128, 2, 512], F32))
        up_ps = st.enter_context(nc.psum_tensor("r_up_ps", [128, 2, 512], F32))
        down_ps = st.enter_context(nc.psum_tensor("r_down_ps", [128, 2, 512], F32))
        rows_in = [sem(f"rows_in{n}") for n in range(4)]
        w_in = [sem(f"w_in{n}") for n in range(4)]
        y_out = [sem(f"y_out{n}") for n in range(4)]
        turned, x_hi_done, x_done = sem("turned"), sem("x_hi_done"), sem("x_done")
        w_hi_done, w_done = sem("w_hi_done"), sem("w_done")
        up_mm, gated_done, h32_done, h_hi_done, h_done = (sem(n) for n in ("up_mm", "gated_done", "h32_done", "h_hi_done", "h_done"))
        down_mm, y_done = sem("down_mm"), sem("y_done")
        block = st.enter_context(nc.Block())

        def buf(tiles, t):
            return tiles[t.off % len(tiles)]

        def steps(eng, step):
            def at(i, off):
                def tile(k):
                    known = isinstance(i, int)
                    return None if known and not 0 <= off + k < NT else Step(i, off + k)
                step(tile(2), tile(1), tile(0), tile(-2))
            for off in range(-2, 6):
                at(0, off)
            with eng.Fori(0, (NT - 8) // 4) as i:
                for off in range(6, 10):
                    at(i, off)
            for off in range(NT - 2, NT + 2):
                at(0, off)

        assert NT % 4 == 0

        @block.sync
        def _(sp):
            def load(t):
                if not t.first(4):
                    sp.wait_ge(turned, t.count(1, -3))
                sp.dma_start(buf(rows, t)[:, :, :], xs_v[bass.ds(t.count(1), 1), :, :, :].rearrange("a p s d -> p (a s) d")
                             ).then_inc(buf(rows_in, t), 16)
                if not t.first(4):
                    sp.wait_ge(w_done, t.count(1, -3))
                expert = sp.value_load(tile_expert[0:1, bass.ds(t.count(1), 1)], min_val=0, max_val=packed.shape[0] - 1)
                sp.dma_start(buf(w_raw, t)[:, :], packed[bass.ds(expert, 1), :, :].rearrange("a p n -> p (a n)")).then_inc(buf(w_in, t), 16)

            def store(t):
                sp.wait_ge(y_done, t.count(1, 1))
                sp.dma_start(ys_v[bass.ds(t.count(1), 1), :, :, :].rearrange("a p s d -> p (a s) d"), buf(y, t)[:, :, :]
                             ).then_inc(buf(y_out, t), 16)
            for n in range(6):
                load(Step(0, n))
            with sp.Fori(0, (NT - 8) // 4) as i:
                for off in range(6, 10):
                    load(Step(i, off))
                    store(Step(i, off - 6))
            for n in range(NT - 8, NT):
                if n + 6 < NT:
                    load(Step(0, n + 6))
                store(Step(0, n))
            for n in range(4):
                sp.wait_ge(y_out[n], 16 * (NT // 4))

        @block.gpsimd
        def _(pool):
            def step(d, a, b, c):
                if d is not None:
                    pool.wait_ge(w_hi_done, d.count(1, 1))
                    hi, lo = buf(w, d)
                    nc.gpsimd.tensor_tensor(lo[:, :], buf(w_raw, d)[:, :], hi[:, :].bitcast(F32), SUB).then_inc(w_done, 1)
                if b is not None:
                    pool.wait_ge(h_hi_done, b.count(1, 1))
                    hi, lo = buf(h, b)
                    nc.gpsimd.tensor_tensor(lo[:, :], buf(h32, b)[:, :], hi[:, :].bitcast(F32), SUB).then_inc(h_done, 1)
            steps(pool, step)

        @block.scalar
        def _(act):
            def step(d, a, b, c):
                if a is not None:
                    act.wait_ge(turned, a.count(1, 1))
                    if not a.first(2):
                        act.wait_ge(up_mm, a.count(1, -1))
                    nc.scalar.activation(buf(xT, a)[0][:, :], turn_ps[:, a.off % 2, :], ACT.Copy).then_inc(x_hi_done, 1)
                if d is not None:
                    act.wait_ge(buf(w_in, d), d.uses(4, 1))
                    if not d.first(4):
                        act.wait_ge(down_mm, d.count(1, -3))
                    nc.scalar.activation(buf(w, d)[0][:, :], buf(w_raw, d)[:, :], ACT.Copy).then_inc(w_hi_done, 1)
                if b is not None:
                    act.wait_ge(up_mm, b.count(1, 1))
                    if not b.first(2):
                        act.wait_ge(h32_done, b.count(1, -1))
                    nc.scalar.activation(buf(gated, b)[:, :], up_ps[:, b.off % 2, 0:SLOTS], ACT.Silu).then_inc(gated_done, 1)
                    act.wait_ge(h32_done, b.count(1, 1))
                    if not b.first(2):
                        act.wait_ge(down_mm, b.count(1, -1))
                    nc.scalar.activation(buf(h, b)[0][:, :], buf(h32, b)[:, :], ACT.Copy).then_inc(h_hi_done, 1)
            steps(act, step)

        @block.vector
        def _(dve):
            def step(d, a, b, c):
                if a is not None:
                    hi, lo = buf(xT, a)
                    dve.wait_ge(x_hi_done, a.count(1, 1))
                    nc.vector.tensor_tensor(lo[:, :], turn_ps[:, a.off % 2, :], hi[:, :].bitcast(F32), SUB).then_inc(x_done, 1)
                if c is not None:
                    dve.wait_ge(down_mm, c.count(1, 1))
                    if not c.first(4):
                        dve.wait_ge(buf(y_out, c), c.uses(4))
                    nc.vector.tensor_copy(buf(y, c)[:, :, :], down_ps[:, c.off % 2, :].rearrange("p (s d) -> p s d", s=S)).then_inc(y_done, 1)
                if b is not None:
                    dve.wait_ge(gated_done, b.count(1, 1))
                    if not b.first(2):
                        dve.wait_ge(h_done, b.count(1, -1))
                    nc.vector.tensor_tensor(buf(h32, b)[:, :], buf(gated, b)[:, :], up_ps[:, b.off % 2, SLOTS:2 * SLOTS], MUL).then_inc(h32_done, 1)
            steps(dve, step)

        @block.tensor
        def _(pe):
            def step(d, a, b, c):
                if a is not None:
                    pe.wait_ge(buf(rows_in, a), a.uses(4, 1))
                    if not a.first(2):
                        pe.wait_ge(x_done, a.count(1, -1))
                    for n in range(CC):
                        for s in range(S):
                            last = nc.tensor.transpose(turn_ps[:, a.off % 2, n * SLOTS + s * 128:n * SLOTS + (s + 1) * 128],
                                                       buf(rows, a)[:, s, n * 128:(n + 1) * 128], ident[:, :])
                    last.then_inc(turned, 1)
                if c is not None:
                    pe.wait_ge(h_done, c.count(1, 1))
                    if not c.first(2):
                        pe.wait_ge(y_done, c.count(1, -1))
                    for s in range(S):
                        last = mm3(nc, down_ps[:, c.off % 2, s * D:(s + 1) * D], [u[:, s * 128:(s + 1) * 128] for u in buf(h, c)],
                                   [u[:, DOWN:DOWN + D] for u in buf(w, c)], True, True)
                    last.then_inc(down_mm, 1)
                if b is not None:
                    pe.wait_ge(x_done, b.count(1, 1))
                    pe.wait_ge(w_done, b.count(1, 1))
                    if not b.first(2):
                        pe.wait_ge(h32_done, b.count(1, -1))
                    for k, start in enumerate((0, UP)):
                        for n in range(CC):
                            last = mm3(nc, up_ps[:, b.off % 2, k * SLOTS:(k + 1) * SLOTS],
                                       [u[:, start + n * 128:start + (n + 1) * 128] for u in buf(w, b)],
                                       [u[:, n * SLOTS:(n + 1) * SLOTS] for u in buf(xT, b)], n == 0, n == CC - 1)
                    last.then_inc(up_mm, 1)
            steps(pe, step)


def grouped_sigmoid_ffn(nc, x_in, gate_in, routerT, e_bias, packed, shared, xs, ys, x_out, slots_out, weights_out):
    T = x_in.shape[0] // 128
    D = x_in.shape[1]
    CC = D // 128
    NR = routerT.shape[2]
    NG, TOPG, TOP = 8, 4, 8
    PG = NR // NG
    FAR = 3.0e38
    PB = 512 // NR - 1
    while T % PB:
        PB -= 1
    BANKS = T // PB
    NT = xs.shape[0] // SLOTS
    NSH = shared.shape[0]
    LEVELS = T * 128 // SLOTS
    assert T <= 256
    NTC = 256 // 128
    BF = mybir.dt.bfloat16
    places = nc.dram_tensor("tile_experts", (NTC, 128), I32).ap()
    with ExitStack() as outer:
        def sb(name, shape, dt=F32, stack=outer):
            return stack.enter_context(nc.sbuf_tensor(name, shape, dt))
        X = sb("g_X", [128, T, D])
        gate = sb("g_gate", [128, 1])
        ident = sb("g_ident", [128, 128])
        slot = sb("g_slot", [128, T, TOP], U32)
        slot_weight = sb("g_slot_weight", [128, T, TOP])
        tile_expert = sb("g_tile_expert", [1, NTC * 128], I32)
        with ExitStack() as mid:
            z = sb("g_z", [128, T, D], stack=mid)
            zT = (sb("g_zT_hi", [128, CC, T * 128], F32R, mid), sb("g_zT_lo", [128, CC, T * 128], F32R, mid))
            coef = sb("g_coef", [128, NSH, T], stack=mid)
            score = sb("g_score", [128, T, NR], stack=mid)
            work = sb("g_work", [128, T, NR], stack=mid)
            best = sb("g_best", [128, T, 8], stack=mid)
            with ExitStack() as st:
                def sem(name):
                    return nc.alloc_semaphore("g_" + name)
                router_raw = sb("g_router_raw", [128, CC, NR], stack=st)
                router = (sb("g_router_hi", [128, CC, NR], F32R, st), sb("g_router_lo", [128, CC, NR], F32R, st))
                ebias = sb("g_ebias", [128, NR], stack=st)
                biased = sb("g_biased", [128, T, NR], stack=st)
                top1 = sb("g_top1", [128, T, NG], stack=st)
                top2 = sb("g_top2", [128, T, NG], stack=st)
                count = sb("g_count", [128, T, NG], stack=st)
                best_at = sb("g_best_at", [128, T, 8], U32, st)
                at_f = sb("g_at_f", [128, T, 8], stack=st)
                numbers = sb("g_numbers", [128, 16], stack=st)
                tile_no = sb("g_tile_no", [128, NTC], stack=st)
                total = sb("g_total", [128, T], stack=st)
                chosen = sb("g_chosen", [128, T, NR], BF, st)
                seen = [sb(f"g_seen{n}", [128, T + 1, NR], BF, st) for n in range(2)]
                before = sb("g_before", [128, 128], BF, st)
                ones = sb("g_ones", [128, 128], BF, st)
                full = sb("g_full", [128, NR, LEVELS], stack=st)
                tiles = sb("g_tiles", [128, NR], stack=st)
                upto = [sb(f"g_upto{n}", [128, NR], stack=st) for n in range(2)]
                passed = sb("g_passed", [128, NTC, NR], stack=st)
                expert_f = sb("g_expert_f", [128, NTC], stack=st)
                expert_i = sb("g_expert_i", [128, NTC], I32, st)
                logits_ps = st.enter_context(nc.psum_tensor("g_logits_ps", [128, BANKS, 512], F32))
                total_ps = st.enter_context(nc.psum_tensor("g_total_ps", [128, 512], F32))
                router_in, bias_in, router_ok, numbers_ok, score_done, own, seen_done, rank_mm, experts_ok, places_out, places_in = (
                    sem(n) for n in ("router_in", "bias_in", "router_ok", "numbers_ok", "score_done", "own", "seen_done",
                                     "rank_mm", "experts_ok", "places_out", "places_in"))
                sync, gpsimd, scalar, vector, tensor, logits_done, gate_done, NBLK = norm_and_turn(
                    nc, "L0_", st, x_in, gate_in, X, gate, zT, ident, router, logits_ps, NR, PB, z)
                block = st.enter_context(nc.Block())

                @block.sync
                def _(sp):
                    sp.dma_start(router_raw[:, :, :], routerT).then_inc(router_in, 16)
                    sp.dma_start(ebias[:, :], e_bias.partition_broadcast(128)).then_inc(bias_in, 16)
                    sync(sp)
                    sp.wait_ge(experts_ok, 1)
                    with nc.allow_non_contiguous_dma(reason="one number from each partition"):
                        sp.dma_start(places.rearrange("j p -> p j"), expert_i[:, :]).then_inc(places_out, 16)
                    sp.wait_ge(places_out, 16)
                    sp.dma_start(tile_expert[0:1, :], places.rearrange("(a j) p -> a (j p)", a=1)).then_inc(places_in, 16)
                    sp.wait_ge(places_in, 16)

                @block.gpsimd
                def _(pool):
                    for dst, pattern, step in ((numbers[:, :], [[1, 16]], 0), (tile_no[:, :], [[128, NTC]], 1)):
                        nc.gpsimd.iota(dst, pattern=pattern, base=0, channel_multiplier=step,
                                       allow_small_or_imprecise_dtypes=True).then_inc(numbers_ok, 1)
                    nc.gpsimd.memset(ones[:, :], 1.0).then_inc(numbers_ok, 1)
                    pool.wait_ge(numbers_ok, 3)
                    nc.gpsimd.affine_select(out=before[:, :], in_=ones[:, :], compare_op=ALU.is_gt, fill=0.0, base=0,
                                            pattern=[[1, 128]], channel_multiplier=-1).then_inc(numbers_ok, 1)
                    gpsimd(pool)

                @block.scalar
                def _(act):
                    act.wait_ge(router_in, 16)
                    nc.scalar.activation(router[0][:, :, :], router_raw[:, :, :], ACT.Copy).then_inc(router_ok, 1)
                    scalar(act)
                    act.wait_ge(logits_done, NBLK)
                    for b in range(BANKS):
                        last = nc.scalar.activation(score[:, b * PB:(b + 1) * PB, :],
                                                    logits_ps[:, b, 0:PB * NR].rearrange("p (t e) -> p t e", e=NR), ACT.Sigmoid)
                    last.then_inc(score_done, 1)

                @block.vector
                def _(dve):
                    chain = Chain(dve, own)
                    ALL = [128, T, NR]
                    GROUPS = [128, T * NG, PG]
                    V = nc.vector

                    def groups(ap):
                        return ap[:, :, :].rearrange("p t (g e) -> p (t g) e", e=PG)

                    def flat(ap):
                        return ap[:, :, :].rearrange("p t g -> p (t g)")

                    dve.wait_ge(router_ok, 1)
                    V.tensor_tensor(router[1][:, :, :], router_raw[:, :, :], router[0][:, :, :].bitcast(F32), SUB).then_inc(router_ok, 1)
                    vector(dve)
                    dve.wait_ge(score_done, 1)
                    dve.wait_ge(bias_in, 16)
                    chain.link(V.tensor_tensor(biased[:, :, :], score[:, :, :], ebias[:, :].unsqueeze(1).broadcast_to(ALL), ADD))
                    chain.link(V.tensor_reduce(flat(top1), groups(biased), AX.X, ALU.max))
                    chain.link(V.tensor_tensor(groups(work), groups(biased), flat(top1).unsqueeze(2).broadcast_to(GROUPS), ALU.is_equal))
                    chain.link(V.tensor_reduce(flat(count), groups(work), AX.X, ADD))
                    chain.link(V.scalar_tensor_tensor(out=work[:, :, :], in0=work[:, :, :], scalar=-FAR, in1=biased[:, :, :], op0=MUL, op1=ADD))
                    chain.link(V.tensor_reduce(flat(top2), groups(work), AX.X, ALU.max))
                    chain.link(V.tensor_scalar(count[:, :, :], count[:, :, :], 1.5, -FAR, ALU.is_lt, MUL))
                    chain.link(V.tensor_tensor(count[:, :, :], count[:, :, :], top1[:, :, :], ADD))
                    chain.link(V.tensor_tensor(top2[:, :, :], top2[:, :, :], count[:, :, :], ALU.max))
                    chain.link(V.tensor_tensor(top1[:, :, :], top1[:, :, :], top2[:, :, :], ADD))
                    for t in range(T):
                        last = V.max(best[:, t, :], top1[:, t, :])
                    chain.link(last)
                    for t in range(T):
                        last = V.max_index(best_at[:, t, :], best[:, t, :], top1[:, t, :])
                    chain.link(last)
                    chain.link(V.tensor_copy(at_f[:, :, :], best_at[:, :, :]))
                    dve.wait_ge(numbers_ok, 3)
                    for k in range(TOPG):
                        dst = count if k == 0 else top2
                        chain.link(V.tensor_tensor(dst[:, :, :], numbers[:, 0:NG].unsqueeze(1).broadcast_to([128, T, NG]),
                                                   at_f[:, :, k:k + 1].broadcast_to([128, T, NG]), ALU.is_equal))
                        if k:
                            chain.link(V.tensor_tensor(count[:, :, :], count[:, :, :], top2[:, :, :], ADD))
                    chain.link(V.tensor_scalar(top2[:, :, :], count[:, :, :], 0.5, -FAR, ALU.is_lt, MUL))
                    chain.link(V.tensor_tensor(groups(work), groups(biased), flat(count).unsqueeze(2).broadcast_to(GROUPS), MUL))
                    chain.link(V.tensor_tensor(groups(work), groups(work), flat(top2).unsqueeze(2).broadcast_to(GROUPS), ADD))
                    for t in range(T):
                        last = V.max(best[:, t, :], work[:, t, :])
                    chain.link(last)
                    for t in range(T):
                        last = V.match_replace(biased[:, t, :], best[:, t, :], work[:, t, :], -1.1 * FAR)
                    chain.link(last)
                    chain.link(V.tensor_tensor(chosen[:, :, :], work[:, :, :], biased[:, :, :], ALU.not_equal))
                    for n in range(2):
                        last = V.memset(seen[n][:, 0:1, :], 0.0)
                    chain.link(V.tensor_copy(seen[0][:, 1:T + 1, :], chosen[:, :, :]))
                    step, now = 1, 0
                    while step < T:
                        old, new = seen[now], seen[1 - now]
                        V.tensor_copy(new[:, 1:step + 1, :], old[:, 1:step + 1, :])
                        last = V.tensor_tensor(new[:, step + 1:T + 1, :], old[:, step + 1:T + 1, :], old[:, 1:T + 1 - step, :], ADD)
                        step, now = 2 * step, 1 - now
                        chain.link(last)
                    V.tensor_copy(seen[now][:, 0:1, :], seen[now][:, 0:1, :]).then_inc(seen_done, 1)
                    chain.link(V.tensor_tensor(score[:, :, :], score[:, :, :], chosen[:, :, :], MUL))
                    chain.link(V.tensor_reduce(total[:, :], score[:, :, :], AX.X, ADD))
                    chain.link(V.tensor_scalar(total[:, :], total[:, :], 1e-20, None, ADD))
                    chain.link(V.reciprocal(total[:, :], total[:, :]))
                    dve.wait_ge(gate_done, 1)
                    chain.link(V.tensor_scalar(total[:, :], total[:, :], gate[:, 0:1], None, MUL))
                    V.tensor_tensor(score[:, :, :], score[:, :, :], total[:, :].unsqueeze(2).broadcast_to(ALL), MUL)
                    chain.link(V.memset(coef[:, :, :], 1.0))
                    V.tensor_scalar(coef[:, :, :], coef[:, :, :], gate[:, 0:1], None, MUL)
                    dve.wait_ge(rank_mm, 1)
                    chain.link(V.tensor_scalar(tiles[:, :], total_ps[:, 0:NR], 1.0 / SLOTS, None, MUL))
                    chain.link(V.tensor_tensor(full[:, :, :], tiles[:, :].unsqueeze(2).broadcast_to([128, NR, LEVELS]),
                                               numbers[:, 0:LEVELS].unsqueeze(1).broadcast_to([128, NR, LEVELS]), ALU.is_gt))
                    chain.link(V.tensor_reduce(tiles[:, :], full[:, :, :], AX.X, ADD))
                    chain.link(V.tensor_copy(upto[0][:, :], tiles[:, :]))
                    step, at = 1, 0
                    while step < NR:
                        old, new = upto[at], upto[1 - at]
                        V.tensor_copy(new[:, 0:step], old[:, 0:step])
                        chain.link(V.tensor_tensor(new[:, step:NR], old[:, step:NR], old[:, 0:NR - step], ADD))
                        step, at = 2 * step, 1 - at
                    upto_e, first = upto[at], upto[1 - at]
                    chain.link(V.tensor_tensor(passed[:, :, :], upto_e[:, :].unsqueeze(1).broadcast_to([128, NTC, NR]),
                                               tile_no[:, :].unsqueeze(2).broadcast_to([128, NTC, NR]), ALU.is_le))
                    chain.link(V.tensor_reduce(expert_f[:, :], passed[:, :, :], AX.X, ADD))
                    V.tensor_scalar(expert_i[:, :], expert_f[:, :], float(NR - 1), None, ALU.min).then_inc(experts_ok, 1)
                    chain.link(V.tensor_tensor(first[:, :], upto_e[:, :], tiles[:, :], SUB))
                    chain.link(V.tensor_scalar(first[:, :], first[:, :], float(SLOTS), 1.0, MUL, ADD))
                    for b in range(BANKS):
                        last = V.tensor_tensor(work[:, b * PB:(b + 1) * PB, :], logits_ps[:, b, 0:PB * NR].rearrange("p (t e) -> p t e", e=NR),
                                               first[:, :].unsqueeze(1).broadcast_to([128, PB, NR]), ADD)
                    chain.link(last)
                    chain.link(V.tensor_tensor(work[:, :, :], work[:, :, :], chosen[:, :, :], MUL))
                    for t in range(T):
                        last = V.max(best[:, t, :], work[:, t, :])
                    chain.link(last)
                    V.tensor_scalar(slot[:, :, :], best[:, :, :], -1.0, None, ADD)

                @block.tensor
                def _(pe):
                    pe.wait_ge(router_ok, 2)
                    tensor(pe)
                    pe.wait_ge(numbers_ok, 4)
                    pe.wait_ge(seen_done, 1)
                    pe.wait_ge(score_done, 1)
                    final = seen[steps_parity(T)]
                    nc.tensor.matmul(total_ps[:, 0:NR], ones[:, :], final[:, T, :], start=True, stop=True)
                    for b in range(BANKS):
                        dst = logits_ps[:, b, 0:PB * NR]
                        nc.tensor.matmul(dst, before[:, :], chosen[:, b * PB:(b + 1) * PB, :], start=True, stop=False)
                        last = nc.tensor.matmul(dst, ones[:, :], final[:, b * PB:(b + 1) * PB, :], start=False, stop=True)
                    last.then_inc(rank_mm, 1)

            DEEP = 4
            z_now = [sb(f"g_z_now{n}", [128, D], stack=mid) for n in range(DEEP)]
            slot_now = [sb(f"g_slot_now{n}", [128, TOP], U32, mid) for n in range(DEEP)]
            hit = sb("g_hit", [128, T, NR], stack=mid)
            copied, sent = ([nc.alloc_semaphore(f"g_{name}{n}") for n in range(DEEP)] for name in ("copied", "sent"))
            hit_done, waited, slots_stored = (nc.alloc_semaphore("g_" + n) for n in ("hit_done", "waited", "slots_stored"))
            assert T % DEEP == 0

            def tiles(eng, tile):
                with eng.Fori(0, (T - DEEP) // DEEP) as i:
                    for off in range(DEEP, 2 * DEEP):
                        tile(Step(i, off))

            def copy_tile(sp, t):
                n = t.off % DEEP
                if not t.first(DEEP):
                    sp.wait_ge(sent[n], t.i * (16 * TOP) + 16 * TOP * (t.off // DEEP))
                for dst, src in ((z_now, z), (slot_now, slot)):
                    sp.dma_start(dst[n][:, :], src[:, bass.ds(t.count(1), 1), :].rearrange("p a d -> p (a d)")).then_inc(copied[n], 16)

            def copy_first(sp):
                for n in range(DEEP):
                    copy_tile(sp, Step(0, n))

            def copy_rest(sp):
                tiles(sp, lambda t: copy_tile(sp, t))

            def write_slots(pool):
                def tile(t):
                    n = t.off % DEEP
                    wait_apart(pool, copied[n], t.i * 32 + 32 * (t.off // DEEP + 1), waited)
                    for k in range(TOP):
                        nc.gpsimd.indirect_dma_start(out=xs, out_offset=bass.IndirectOffsetOnAxis(ap=slot_now[n][:, k:k + 1], axis=0),
                                                     in_=z_now[n][:, :], in_offset=None).then_inc(sent[n], 16)
                for n in range(DEEP):
                    tile(Step(0, n))
                tiles(pool, tile)
                for n in range(DEEP):
                    pool.wait_ge(sent[n], 16 * TOP * (T // DEEP))

            def slot_weights(dve):
                chain = Chain(dve, hit_done)
                for k in range(TOP):
                    chain.link(nc.vector.tensor_tensor(hit[:, :, :], work[:, :, :], best[:, :, k:k + 1].broadcast_to([128, T, NR]), ALU.is_equal))
                    chain.link(nc.vector.tensor_tensor(hit[:, :, :], hit[:, :, :], score[:, :, :], MUL))
                    chain.link(nc.vector.tensor_reduce(slot_weight[:, :, k:k + 1].rearrange("p t a -> p (t a)"), hit[:, :, :], AX.X, ADD))

            def store_slots(sp):
                with nc.allow_non_contiguous_dma(reason="eight numbers to a row"):
                    sp.dma_start(slots_out.rearrange("(t p) k -> p t k", p=128), slot[:, :, :]).then_inc(slots_stored, 16)
                    sp.wait_ge(hit_done, 3 * TOP)
                    sp.dma_start(weights_out.rearrange("(t p) k -> p t k", p=128), slot_weight[:, :, :]).then_inc(slots_stored, 16)
                sp.wait_ge(slots_stored, 32)

            dense_experts(nc, "L0_", X, zT, coef, shared, x_out, write_slots, slot_weights, copy_first, copy_rest,
                          store_slots)

        routed_experts(nc, xs, ys, tile_expert, packed, NT, ident)


def steps_parity(count):
    n, step = 0, 1
    while step < count:
        n, step = 1 - n, 2 * step
    return n


def build(nc, a, out):
    shape = out.shape
    x1, x2, x3 = (nc.dram_tensor(n, shape, F32).ap() for n in ("x1", "x2", "x3"))

    NB, Q, D = shape
    tiles = slot_tiles(NB * Q, 8, a["L0_ffn_packed"].shape[0])
    tiles += -tiles % 16
    xs, ys = (nc.dram_tensor(n, (tiles * SLOTS, D), F32).ap() for n in ("slots_in", "slots_out"))
    slots, weights = (nc.dram_tensor(n, (NB, Q, 8), dt).ap() for n, dt in (("row_slots", U32), ("row_weights", F32)))

    def flat(ap):
        return ap.rearrange("b q d -> (b q) d")
    p = "L0_xattn_"
    with nc.cleanup_on_exit():
        perceiver_attention(nc, a["x"], a["ctx_1024"], a["g_xattn"][0:1], a[p + "gamma_media"], a[p + "beta_media"],
                            a[p + "gamma_lat"], a[p + "beta_lat"], a[p + "Wq"], a[p + "bq"], a[p + "Wkv"], a[p + "bkv"],
                            a[p + "Wo"], a[p + "bo"], x1, xs)
    with nc.cleanup_on_exit():
        grouped_sigmoid_ffn(nc, flat(x1), a["g_ffn"][0:1], a["L0_ffn_routerT"], a["L0_ffn_e_bias"], a["L0_ffn_packed"],
                            a["L0_ffn_shared"], xs, ys, flat(x2), flat(slots), flat(weights))
    p = "L1_xattn_"
    with nc.cleanup_on_exit():
        strided_attention(nc, x2, ys, slots, weights, a["ctx_1024"], a["g_xattn"][1:2], a[p + "WqT"], a[p + "WkT"], a[p + "WvT"], a[p + "WoT"],
                          a[p + "biasT"], a[p + "bo"], a["L1_row_mask"], a["L1_col_mask"], x3)
    with nc.cleanup_on_exit():
        softmax_top2_ffn(nc, flat(x3), a["g_ffn"][1:2], a["L1_ffn_routerT"], a["L1_ffn_packed"], flat(out))


def pack_experts(gate, up, down):
    import numpy as np
    n, d, h = gate.shape

    def rows(w):
        return w.reshape(n, d // 128, 128, h).transpose(0, 2, 1, 3).reshape(n, 128, -1)
    return np.concatenate([rows(gate), rows(up), down], axis=2)


def shared_as_experts(gate, up, down):
    import numpy as np
    d, h = gate.shape
    n = h // 128
    return (gate.reshape(d, n, 128).transpose(1, 0, 2), up.reshape(d, n, 128).transpose(1, 0, 2), down.reshape(n, 128, d))


def by_partition(w):
    r, n = w.shape
    return w.reshape(r // 128, 128, n).transpose(1, 0, 2)


def kernel(**inputs):
    import numpy as np
    import concourse.bacc as bacc
    from concourse.bass_utils import run_bass_kernel_spmd

    given = {name: np.asarray(a) for name, a in inputs.items()}
    arrays = {name: given[name] for name in PLAIN if name in given}
    for layer, names in (("L0_ffn", ("gate_w", "up_w", "down_w", "sh_gate_w", "sh_up_w", "sh_down_w")),
                         ("L1_ffn", ("experts_gate", "experts_up", "experts_down", "shared_gate", "shared_up", "shared_down"))):
        w = [given[f"{layer}_{n}"] for n in names]
        arrays[f"{layer}_packed"] = pack_experts(*w[:3])
        arrays[f"{layer}_shared"] = pack_experts(*shared_as_experts(*w[3:]))
    arrays["L1_ffn_packed"] = np.concatenate([arrays.pop("L1_ffn_packed"), arrays.pop("L1_ffn_shared")], axis=0)
    arrays["L0_ffn_routerT"] = by_partition(given["L0_ffn_router_w"].T)
    arrays["L1_ffn_routerT"] = by_partition(given["L1_ffn_router"])
    for m in ("Wq", "Wk", "Wv", "Wo"):
        arrays[f"L1_xattn_{m}T"] = by_partition(given[f"L1_xattn_{m}"].T)
    arrays["L1_xattn_biasT"] = np.concatenate([given[f"L1_xattn_{b}"].reshape(2, 128).T for b in ("bq", "bk", "bv")], axis=1)
    heads, keys, dims = 16, given["ctx_1024"].shape[1] // 16 * 16, given["x"].shape[2]
    dim_head = np.arange(dims) // (dims // heads)
    arrays["L1_row_mask"] = (np.arange(128)[:, None] % heads == dim_head[None, :]).astype(np.float32)
    arrays["L1_col_mask"] = by_partition((dim_head[:, None] == np.arange(keys)[None, :] % heads).astype(np.float32))

    nc = bacc.Bacc("TRN2", target_bir_lowering=False, num_devices=1)
    feed, aps = {}, {}
    for name, a in arrays.items():
        a = np.ascontiguousarray(a)
        feed[f"in_{name}"] = a
        aps[name] = nc.dram_tensor(f"in_{name}", a.shape, mybir.dt.from_np(a.dtype), kind="ExternalInput").ap()
    out = nc.dram_tensor("out_x", given["x"].shape, F32, kind="ExternalOutput").ap()
    build(nc, aps, out)
    r = run_bass_kernel_spmd(nc, [feed], core_ids=[0])
    return r.results[0]["out_x"]


PLAIN = ["x", "ctx_1024", "g_xattn", "g_ffn", "L0_xattn_gamma_media", "L0_xattn_beta_media", "L0_xattn_gamma_lat",
         "L0_xattn_beta_lat", "L0_xattn_Wq", "L0_xattn_bq", "L0_xattn_Wkv", "L0_xattn_bkv", "L0_xattn_Wo", "L0_xattn_bo",
         "L0_ffn_e_bias", "L1_xattn_bq", "L1_xattn_bk", "L1_xattn_bv", "L1_xattn_bo"]
```
